# Optimizing a Trainium2 kernel written in Bass

```python
import numpy as np
import jax
import jax.numpy as jnp

def _softmax(x, axis=-1):
    return jax.nn.softmax(x, axis=axis)

def _gelu(x):
    return jax.nn.gelu(x, approximate=True)

def _silu(x):
    return jax.nn.silu(x)

def _sigmoid(x):
    return jax.nn.sigmoid(x)

def _layernorm(x, axis=-1, eps=1e-05):
    m = jnp.mean(x, axis=axis, keepdims=True)
    v = jnp.var(x, axis=axis, keepdims=True)
    return (x - m) / jnp.sqrt(v + eps)

def _scatter_add(tgt, idx, src, axis=0):
    return tgt.at[idx].add(src)

def _segment_sum(src, seg, n):
    return jax.ops.segment_sum(src, seg, n)
kernel_name = 'mk_sandwich_d2_jaxref_r8_529ce3'

def setup_inputs(seed: int=0):
    np.random.seed(seed)
    _w = jnp.asarray

    def _L0_attn_setup():
        import jax, jax.numpy as jnp
        import numpy as np
        B, S, D, F = (8, 512, 128, 384)
        EPS = 1e-06

        def rmsnorm(x, w):
            rms = jax.lax.rsqrt(jnp.mean(x * x, axis=-1, keepdims=True) + EPS)
            return x * rms * w

        def linear_scan(x, a):

            def combine(c1, c2):
                a1, h1 = c1
                a2, h2 = c2
                return (a1 * a2, a2 * h1 + h2)
            return jax.lax.associative_scan(combine, (a, x), axis=1)[1]
        key = jax.random.key(seed)
        ks = jax.random.split(key, 10)
        s_d = 1.0 / np.sqrt(D)
        s_f = 1.0 / np.sqrt(F)
        return {'x': jax.random.normal(ks[0], (B, S, D), jnp.float32), 'w_rms_mix': jnp.ones((D,), jnp.float32), 'w_rms_ffn': jnp.ones((D,), jnp.float32), 'Wg': jax.random.normal(ks[1], (D, D), jnp.float32) * s_d, 'bg': jnp.zeros((D,), jnp.float32), 'Wv': jax.random.normal(ks[2], (D, D), jnp.float32) * s_d, 'bv': jnp.zeros((D,), jnp.float32), 'Wd': jax.random.normal(ks[3], (D, D), jnp.float32) * s_d, 'bd': jnp.ones((D,), jnp.float32), 'W_gate': jax.random.normal(ks[4], (D, F), jnp.float32) * s_d, 'W_up': jax.random.normal(ks[5], (D, F), jnp.float32) * s_d, 'W_out': jax.random.normal(ks[6], (F, D), jnp.float32) * s_f}
    _L0_attn_in = _L0_attn_setup()

    def _L0_ffn_setup():
        import jax, jax.numpy as jnp
        import numpy as np
        DIM = 128
        DEPTH = 6
        HEADS = 16
        DIM_HEAD = 64
        WINDOW = 32
        INNER = HEADS * DIM_HEAD
        DIM_INNER = int(DIM * 4 * 2 / 3)
        QK_SCALE = 8.0

        def shift_tokens(t):
            a, s = jnp.split(t, 2, -1)
            s = jnp.pad(s, ((0, 0), (1, 0), (0, 0)))[:, :-1]
            return jnp.concatenate([a, s], -1)

        def l2norm(t):
            return t / jnp.maximum(jnp.linalg.norm(t, axis=-1, keepdims=True), 1e-12)

        def rotate_half(x):
            x1, x2 = jnp.split(x, 2, -1)
            return jnp.concatenate([-x2, x1], -1)

        def rotary_tables(n):
            half = jnp.arange(0, DIM_HEAD, 2, dtype=jnp.float32)
            inv_freq = 1.0 / 10000.0 ** (half / DIM_HEAD)
            t = jnp.arange(n, dtype=jnp.float32)
            freqs = t[:, None] * inv_freq[None, :]
            freqs = jnp.concatenate([freqs, freqs], -1)
            base_scale = (half + 0.4 * DIM_HEAD) / (1.4 * DIM_HEAD)
            power = (t - n // 2) / (WINDOW // 2)
            scale = base_scale[None, :] ** power[:, None]
            scale = jnp.concatenate([scale, scale], -1)
            return (freqs, scale)

        def local_attention(q, k, v):
            b, h, n, d = q.shape
            w = WINDOW
            nw = n // w
            bq = q.reshape(b, h, nw, w, d)
            bk = k.reshape(b, h, nw, w, d)
            bv = v.reshape(b, h, nw, w, d)

            def look(t):
                p = jnp.pad(t, ((0, 0), (0, 0), (1, 0), (0, 0), (0, 0)))
                return jnp.concatenate([p[:, :, :nw], p[:, :, 1:]], axis=3)
            bk2, bv2 = (look(bk), look(bv))
            seq = jnp.arange(n).reshape(nw, w)
            seq_p = jnp.pad(seq, ((1, 0), (0, 0)), constant_values=-1)
            jt = jnp.concatenate([seq_p[:nw], seq_p[1:]], axis=1)
            it = seq[:, :, None]
            jb = jt[:, None, :]
            mask = (it < jb) | (it > jb + w) | (jb == -1)
            sim = jnp.einsum('bhwie,bhwje->bhwij', bq, bk2) * QK_SCALE
            sim = jnp.where(mask, -jnp.finfo(sim.dtype).max, sim)
            attn = jax.nn.softmax(sim, -1)
            out = jnp.einsum('bhwij,bhwje->bhwie', attn, bv2)
            return out.reshape(b, h, n, d)

        def attn_layer(x, Wqkv, qs, ksc, Wo):
            b, n, _ = x.shape
            qkv = x @ Wqkv
            q, k, v = jnp.split(qkv, 3, -1)
            sh = lambda t: t.reshape(b, n, HEADS, DIM_HEAD).transpose(0, 2, 1, 3)
            q, k, v = (sh(q), sh(k), sh(v))
            q = l2norm(q) * qs
            k = l2norm(k) * ksc
            freqs, scale = rotary_tables(n)
            cos, sin = (jnp.cos(freqs), jnp.sin(freqs))
            q = q * cos * scale + rotate_half(q) * sin * scale
            inv = 1.0 / scale
            k = k * cos * inv + rotate_half(k) * sin * inv
            out = local_attention(q, k, v)
            out = out.transpose(0, 2, 1, 3).reshape(b, n, INNER)
            return out @ Wo

        def ffn_layer(x, g, bln, W1, b1, W2, b2):
            mu = x.mean(-1, keepdims=True)
            var = ((x - mu) ** 2).mean(-1, keepdims=True)
            xn = (x - mu) / jnp.sqrt(var + 1e-05) * g + bln
            hg = xn @ W1 + b1
            a, gate = jnp.split(hg, 2, -1)
            return a * jax.nn.gelu(gate, approximate=False) @ W2 + b2
        key = jax.random.key(seed)
        ks = jax.random.split(key, 8)
        B, N = (2, 256)
        init = lambda k, shape: jax.random.normal(k, shape, jnp.float32) * 0.02
        return {'x': jax.random.normal(ks[0], (B, N, DIM), jnp.float32), 'Wqkv': init(ks[1], (DEPTH, DIM, 3 * INNER)), 'q_scale': jnp.ones((DEPTH, DIM_HEAD), jnp.float32), 'k_scale': jnp.ones((DEPTH, DIM_HEAD), jnp.float32), 'Wo': init(ks[2], (DEPTH, INNER, DIM)), 'ln_g': jnp.ones((DEPTH, DIM), jnp.float32), 'ln_b': jnp.zeros((DEPTH, DIM), jnp.float32), 'W1': init(ks[3], (DEPTH, DIM, 2 * DIM_INNER)), 'b1': jnp.zeros((DEPTH, 2 * DIM_INNER), jnp.float32), 'W2': init(ks[4], (DEPTH, DIM_INNER, DIM)), 'b2': jnp.zeros((DEPTH, DIM), jnp.float32)}
    _L0_ffn_in = _L0_ffn_setup()

    def _L1_attn_setup():
        import jax, jax.numpy as jnp
        import numpy as np
        B, T, D_MODEL, N_HEADS = (2, 256, 128, 16)
        HS = D_MODEL // N_HEADS
        key = jax.random.key(seed)
        k1, k2, k3 = jax.random.split(key, 3)
        x = jax.random.normal(k1, (B, T, D_MODEL), dtype=jnp.float32)
        W_qkv = jax.random.normal(k2, (3 * D_MODEL, D_MODEL), dtype=jnp.float32) * D_MODEL ** (-0.5)
        W_out = jax.random.normal(k3, (D_MODEL, D_MODEL), dtype=jnp.float32) * D_MODEL ** (-0.5)
        return {'x': x, 'W_qkv': W_qkv, 'W_out': W_out}
    _L1_attn_in = _L1_attn_setup()

    def _L1_ffn_setup():
        import jax, jax.numpy as jnp
        import numpy as np
        B, S, D = (4, 512, 128)
        E, I = (8, 256)
        CAPACITY = 2
        K = max(1, int(S / E * CAPACITY))
        key = jax.random.key(seed)
        k1, k2, k3, k4, k5 = jax.random.split(key, 5)
        x = jax.random.normal(k1, (B, S, D), dtype=jnp.float32)
        gate_w = jax.random.normal(k2, (D, E), dtype=jnp.float32) * 0.006
        Wg = jax.random.normal(k3, (E, D, I), dtype=jnp.float32) * 0.02
        Wu = jax.random.normal(k4, (E, D, I), dtype=jnp.float32) * 0.02
        Wd = jax.random.normal(k5, (E, I, D), dtype=jnp.float32) * 0.02
        return {'x': x, 'gate_w': gate_w, 'Wg': Wg, 'Wu': Wu, 'Wd': Wd}
    _L1_ffn_in = _L1_ffn_setup()
    _d = {'L0_attn_x': _L0_attn_in['x'], 'L0_attn_w_rms_mix': _L0_attn_in['w_rms_mix'], 'L0_attn_w_rms_ffn': _L0_attn_in['w_rms_ffn'], 'L0_attn_Wg': _L0_attn_in['Wg'], 'L0_attn_bg': _L0_attn_in['bg'], 'L0_attn_Wv': _L0_attn_in['Wv'], 'L0_attn_bv': _L0_attn_in['bv'], 'L0_attn_Wd': _L0_attn_in['Wd'], 'L0_attn_bd': _L0_attn_in['bd'], 'L0_attn_W_gate': _L0_attn_in['W_gate'], 'L0_attn_W_up': _L0_attn_in['W_up'], 'L0_attn_W_out': _L0_attn_in['W_out'], 'L0_ffn_Wqkv': _L0_ffn_in['Wqkv'], 'L0_ffn_q_scale': _L0_ffn_in['q_scale'], 'L0_ffn_k_scale': _L0_ffn_in['k_scale'], 'L0_ffn_Wo': _L0_ffn_in['Wo'], 'L0_ffn_ln_g': _L0_ffn_in['ln_g'], 'L0_ffn_ln_b': _L0_ffn_in['ln_b'], 'L0_ffn_W1': _L0_ffn_in['W1'], 'L0_ffn_b1': _L0_ffn_in['b1'], 'L0_ffn_W2': _L0_ffn_in['W2'], 'L0_ffn_b2': _L0_ffn_in['b2'], 'L1_attn_W_qkv': _L1_attn_in['W_qkv'], 'L1_attn_W_out': _L1_attn_in['W_out'], 'L1_ffn_gate_w': _L1_ffn_in['gate_w'], 'L1_ffn_Wg': _L1_ffn_in['Wg'], 'L1_ffn_Wu': _L1_ffn_in['Wu'], 'L1_ffn_Wd': _L1_ffn_in['Wd']}
    _x0 = _d['L0_attn_x']
    _d['L0_attn_x'] = jax.random.normal(jax.random.fold_in(jax.random.key(seed), 1), (2, 1024, 128), dtype=_x0.dtype)
    del _x0
    return _d

def reference(L0_attn_x, L0_attn_w_rms_mix, L0_attn_w_rms_ffn, L0_attn_Wg, L0_attn_bg, L0_attn_Wv, L0_attn_bv, L0_attn_Wd, L0_attn_bd, L0_attn_W_gate, L0_attn_W_up, L0_attn_W_out, L0_ffn_Wqkv, L0_ffn_q_scale, L0_ffn_k_scale, L0_ffn_Wo, L0_ffn_ln_g, L0_ffn_ln_b, L0_ffn_W1, L0_ffn_b1, L0_ffn_W2, L0_ffn_b2, L1_attn_W_qkv, L1_attn_W_out, L1_ffn_gate_w, L1_ffn_Wg, L1_ffn_Wu, L1_ffn_Wd):

    def _L0_attn_ref(x, w_rms_mix, w_rms_ffn, Wg, bg, Wv, bv, Wd, bd, W_gate, W_up, W_out):
        import jax, jax.numpy as jnp
        import numpy as np
        B, S, D, F = (8, 512, 128, 384)
        EPS = 1e-06

        def rmsnorm(x, w):
            rms = jax.lax.rsqrt(jnp.mean(x * x, axis=-1, keepdims=True) + EPS)
            return x * rms * w

        def linear_scan(x, a):

            def combine(c1, c2):
                a1, h1 = c1
                a2, h2 = c2
                return (a1 * a2, a2 * h1 + h2)
            return jax.lax.associative_scan(combine, (a, x), axis=1)[1]
        xn = rmsnorm(x, w_rms_mix)
        g = xn @ Wg + bg
        v = xn @ Wv + bv
        d = xn @ Wd + bd
        x_scan = jax.nn.sigmoid(g) * jnp.tanh(v)
        a = 0.001 + 0.998 * jax.nn.sigmoid(d)
        x = x + linear_scan(x_scan, a)
        yn = rmsnorm(x, w_rms_ffn)
        ffn = jax.nn.silu(yn @ W_gate) * (yn @ W_up) @ W_out
        return x + ffn

    def _L0_ffn_ref(x, Wqkv, q_scale, k_scale, Wo, ln_g, ln_b, W1, b1, W2, b2):
        import jax, jax.numpy as jnp
        import numpy as np
        DIM = 128
        DEPTH = 6
        HEADS = 16
        DIM_HEAD = 64
        WINDOW = 32
        INNER = HEADS * DIM_HEAD
        DIM_INNER = int(DIM * 4 * 2 / 3)
        QK_SCALE = 8.0

        def shift_tokens(t):
            a, s = jnp.split(t, 2, -1)
            s = jnp.pad(s, ((0, 0), (1, 0), (0, 0)))[:, :-1]
            return jnp.concatenate([a, s], -1)

        def l2norm(t):
            return t / jnp.maximum(jnp.linalg.norm(t, axis=-1, keepdims=True), 1e-12)

        def rotate_half(x):
            x1, x2 = jnp.split(x, 2, -1)
            return jnp.concatenate([-x2, x1], -1)

        def rotary_tables(n):
            half = jnp.arange(0, DIM_HEAD, 2, dtype=jnp.float32)
            inv_freq = 1.0 / 10000.0 ** (half / DIM_HEAD)
            t = jnp.arange(n, dtype=jnp.float32)
            freqs = t[:, None] * inv_freq[None, :]
            freqs = jnp.concatenate([freqs, freqs], -1)
            base_scale = (half + 0.4 * DIM_HEAD) / (1.4 * DIM_HEAD)
            power = (t - n // 2) / (WINDOW // 2)
            scale = base_scale[None, :] ** power[:, None]
            scale = jnp.concatenate([scale, scale], -1)
            return (freqs, scale)

        def local_attention(q, k, v):
            b, h, n, d = q.shape
            w = WINDOW
            nw = n // w
            bq = q.reshape(b, h, nw, w, d)
            bk = k.reshape(b, h, nw, w, d)
            bv = v.reshape(b, h, nw, w, d)

            def look(t):
                p = jnp.pad(t, ((0, 0), (0, 0), (1, 0), (0, 0), (0, 0)))
                return jnp.concatenate([p[:, :, :nw], p[:, :, 1:]], axis=3)
            bk2, bv2 = (look(bk), look(bv))
            seq = jnp.arange(n).reshape(nw, w)
            seq_p = jnp.pad(seq, ((1, 0), (0, 0)), constant_values=-1)
            jt = jnp.concatenate([seq_p[:nw], seq_p[1:]], axis=1)
            it = seq[:, :, None]
            jb = jt[:, None, :]
            mask = (it < jb) | (it > jb + w) | (jb == -1)
            sim = jnp.einsum('bhwie,bhwje->bhwij', bq, bk2) * QK_SCALE
            sim = jnp.where(mask, -jnp.finfo(sim.dtype).max, sim)
            attn = jax.nn.softmax(sim, -1)
            out = jnp.einsum('bhwij,bhwje->bhwie', attn, bv2)
            return out.reshape(b, h, n, d)

        def attn_layer(x, Wqkv, qs, ksc, Wo):
            b, n, _ = x.shape
            qkv = x @ Wqkv
            q, k, v = jnp.split(qkv, 3, -1)
            sh = lambda t: t.reshape(b, n, HEADS, DIM_HEAD).transpose(0, 2, 1, 3)
            q, k, v = (sh(q), sh(k), sh(v))
            q = l2norm(q) * qs
            k = l2norm(k) * ksc
            freqs, scale = rotary_tables(n)
            cos, sin = (jnp.cos(freqs), jnp.sin(freqs))
            q = q * cos * scale + rotate_half(q) * sin * scale
            inv = 1.0 / scale
            k = k * cos * inv + rotate_half(k) * sin * inv
            out = local_attention(q, k, v)
            out = out.transpose(0, 2, 1, 3).reshape(b, n, INNER)
            return out @ Wo

        def ffn_layer(x, g, bln, W1, b1, W2, b2):
            mu = x.mean(-1, keepdims=True)
            var = ((x - mu) ** 2).mean(-1, keepdims=True)
            xn = (x - mu) / jnp.sqrt(var + 1e-05) * g + bln
            hg = xn @ W1 + b1
            a, gate = jnp.split(hg, 2, -1)
            return a * jax.nn.gelu(gate, approximate=False) @ W2 + b2
        for i in range(DEPTH):
            x = attn_layer(shift_tokens(x), Wqkv[i], q_scale[i], k_scale[i], Wo[i]) + x
            x = ffn_layer(shift_tokens(x), ln_g[i], ln_b[i], W1[i], b1[i], W2[i], b2[i]) + x
        return x

    def _L1_attn_ref(x, W_qkv, W_out):
        import jax, jax.numpy as jnp
        import numpy as np
        B, T, D_MODEL, N_HEADS = (2, 256, 128, 16)
        HS = D_MODEL // N_HEADS
        Bx, Tx, Dm = x.shape
        nH, Hs = (N_HEADS, HS)
        qkv = x @ W_qkv.T
        qkv = qkv.reshape(Bx, Tx, 3 * nH, Hs).transpose(0, 2, 1, 3)
        q, k, v = (qkv[:, :nH], qkv[:, nH:2 * nH], qkv[:, 2 * nH:])
        q = jax.nn.softmax(q, axis=-1) * Hs ** (-0.5)
        k_exp = jnp.exp(k - jnp.max(k, axis=2, keepdims=True))
        k_exp_cumsum = jnp.cumsum(k_exp, axis=2)
        kv_outer = jnp.einsum('bhtc,bhtd->bhtcd', k_exp, v)
        kv_cumsum = jnp.cumsum(kv_outer, axis=2)
        kv = kv_cumsum / (k_exp_cumsum[..., None] + 1e-09)
        xo = jnp.einsum('bhtc,bhtcd->bhtd', q, kv)
        xo = xo.transpose(0, 2, 1, 3).reshape(Bx, Tx, Dm)
        return xo @ W_out.T

    def _L1_ffn_ref(x, gate_w, Wg, Wu, Wd):
        import jax, jax.numpy as jnp
        import numpy as np
        B, S, D = (4, 512, 128)
        E, I = (8, 256)
        CAPACITY = 2
        K = max(1, int(S / E * CAPACITY))
        logits = jnp.einsum('bsd,de->bse', x, gate_w)
        affinity = jax.nn.softmax(logits, axis=-1)
        affinity_T = jnp.transpose(affinity, (0, 2, 1))
        gating, index = jax.lax.top_k(affinity_T, K)
        b_idx = jnp.arange(x.shape[0])[:, None, None]
        x_sel = x[b_idx, index]
        g = jnp.einsum('bekd,edi->beki', x_sel, Wg)
        u = jnp.einsum('bekd,edi->beki', x_sel, Wu)
        h = jax.nn.silu(g) * u
        out = jnp.einsum('beki,eid->bekd', h, Wd)
        contrib = out * gating[..., None]
        x_out = jnp.zeros_like(x).at[b_idx, index].add(contrib)
        return x_out
    x = L0_attn_x
    x = x + _layernorm(_L0_attn_ref(_layernorm(x, axis=-1), L0_attn_w_rms_mix, L0_attn_w_rms_ffn, L0_attn_Wg, L0_attn_bg, L0_attn_Wv, L0_attn_bv, L0_attn_Wd, L0_attn_bd, L0_attn_W_gate, L0_attn_W_up, L0_attn_W_out), axis=-1)
    x = x + _layernorm(_L0_ffn_ref(_layernorm(x, axis=-1), L0_ffn_Wqkv, L0_ffn_q_scale, L0_ffn_k_scale, L0_ffn_Wo, L0_ffn_ln_g, L0_ffn_ln_b, L0_ffn_W1, L0_ffn_b1, L0_ffn_W2, L0_ffn_b2), axis=-1)
    x = x + _layernorm(_L1_attn_ref(_layernorm(x, axis=-1), L1_attn_W_qkv, L1_attn_W_out), axis=-1)
    x = x + _layernorm(_L1_ffn_ref(_layernorm(x, axis=-1), L1_ffn_gate_w, L1_ffn_Wg, L1_ffn_Wu, L1_ffn_Wd), axis=-1)
    return x

_drawn_inputs = setup_inputs


def setup_inputs(seed=0):
    import zlib

    import numpy as np

    out = dict(_drawn_inputs(seed))
    spreads = {'L0_attn_w_rms_mix': (1.0, 0.2),
     'L0_attn_w_rms_ffn': (1.0, 0.2),
     'L0_attn_bg': (0.0, 0.493),
     'L0_attn_bv': (0.0, 0.1),
     'L0_attn_bd': (1.0, 0.2),
     'L0_ffn_q_scale': (1.0, 0.6),
     'L0_ffn_k_scale': (1.0, 0.6),
     'L0_ffn_ln_g': (1.0, 0.6),
     'L0_ffn_ln_b': (0.0, 0.8),
     'L0_ffn_b1': (0.0, 0.687),
     'L0_ffn_b2': (0.0, 0.1)}
    factors = {'L0_ffn_W1': 3.715, 'L0_ffn_W2': 3.521}
    for name, (base, spread) in spreads.items():
        noise = np.random.default_rng([zlib.crc32(name.encode()), seed]).standard_normal(out[name].shape)
        drawn = base * np.exp(spread * noise) if base else spread * noise
        out[name] = jnp.asarray(drawn.astype(out[name].dtype))
    for name, factor in factors.items():
        out[name] = (out[name] * factor).astype(out[name].dtype)
    return out
```

```python
import concourse.bass as bass
import numpy as np
from concourse import mybir
from contextlib import ExitStack

F32 = mybir.dt.float32
BF16 = mybir.dt.bfloat16
ALU = mybir.AluOpType
ACT = mybir.ActivationFunctionType
AX = mybir.AxisListType

P = 128
B, S, D = 2, 1024, 128
NT = S // P
HALF = 512
NH = S // HALF
DEPTH, HEADS, DH, WIN = 6, 16, 64, 32
PAIRS = HEADS // 2
CH = 4
CB = NT // CH
KW = WIN + P
FA = 384
FI = 341
FJ = [128, 128, FI - 256]
NE, EI, TOPK = 8, 256, 128
LH, LC = 16, 8
NEG = -2.0 ** 100
STAGES = "ABCD"
LAYERS = 6


class Flow:

    def __init__(self, ctx, nc, name):
        self.sem = ctx.enter_context(nc.semaphore(name))
        self.used = 0

    def take(self, n=1):
        self.used += n
        return self.used

    def peek(self, n):
        return self.used + n

    def settle(self, eng):
        if self.used:
            eng.sem_inc(self.sem, -self.used)
        self.used = 0


def mixed_layers_kernel(nc, a, out, stages):
    ctx = ExitStack()
    with ctx:
        def sb(name, shape, dt=F32):
            return ctx.enter_context(nc.sbuf_tensor(name, shape, dt))

        def flow(name):
            return Flow(ctx, nc, name)

        X = sb("X", [P, B * NT, D])
        XT = sb("XT", [P, B, S])
        XN = sb("XN", [P, S])
        YT = sb("YT", [P, S])
        NTOK = sb("NTOK", [P, NT, D])
        XS = sb("XS", [P, S])
        ident = sb("ident", [P, P])
        identb = sb("identb", [P, P], BF16)
        bandmask = sb("bandmask", [P, 3, KW], BF16)
        minus_half = sb("minus_half", [P, 8])
        eps_tile = sb("eps_tile", [P, 4])
        bn = sb("bn", [P, NT, 6])
        mv = sb("mv", [P, NT, 2])
        ms = sb("ms", [P, NT])
        ve = sb("ve", [P, NT])
        rstd = sb("rstd", [P, NT])
        WQ = sb("WQ", [P, 2, PAIRS * 384])
        WO = sb("WO", [P, PAIRS, D])
        W1 = sb("W1", [P, 2 * FI])
        W2 = sb("W2", [P, 3, D])
        PL = sb("PL", [P, 9])
        QKS = sb("QKS", [P, 2, 256])
        COS0 = sb("COS0", [P, NT, 256])
        SIN0 = sb("SIN0", [P, NT, 256])
        COSL = sb("COSL", [P, NT, 256])
        SINL = sb("SINL", [P, NT, 256])
        QKT = sb("QKT", [P, 2, WIN + S])
        V = sb("V", [P, CH, CB, 2, DH + 1])
        VP = sb("VP", [WIN, CH, CB, 2, DH + 1])
        SQ = sb("SQ", [P, 2, 8, DH])
        N2 = sb("N2", [P, 8])
        N2G = sb("N2G", [P, 8])
        RN = sb("RN", [P, 8])
        R1 = sb("R1", [P, CB, 256])
        R2 = sb("R2", [P, CB, 256])
        RR = sb("RR", [P, CB, 256])
        QK = sb("QK", [P, 2, CB, 2, P])
        NMX = sb("NMX", [P, 4])
        PR = sb("PR", [P, 2, 4, KW])
        PTS = sb("PTS", [P, 4, P])
        PPS = sb("PPS", [WIN, 4, WIN])
        RO = sb("RO", [P, 4])
        ON = sb("ON", [P, CB, P])
        BIG = sb("BIG", [P, PAIRS * S])
        OTS = BIG[:, :].rearrange("p (h s) -> p h s", h=PAIRS)

        PS = ctx.enter_context(nc.psum_tensor("PS", [P, 8, HALF], F32))

        s_in, s_w, s_wq, s_out = (ctx.enter_context(nc.semaphore(n)) for n in
                                  ("inputs_in", "layer_in", "first_wqkv_in", "out_written"))

        def bank_tiles(bank, t):
            return PS[:, bank + t // 4, (t % 4) * P:(t % 4 + 1) * P]

        made = flow("constants_made")
        bandmask_f32 = BIG[:, 0:3 * KW].rearrange("p (m k) -> p m k", m=3)
        with nc.Block() as block:
            @block.sync
            def _(sp):
                sp.dma_start(X[:, :, :], a["x"].rearrange("(t p) d -> p t d", p=P)).then_inc(s_in, 16)
                sp.dma_start(COS0[:, :, :], a["cos"]).then_inc(s_in, 16)
                sp.dma_start(SIN0[:, :, :], a["sin"]).then_inc(s_in, 16)
                sp.dma_start(bandmask_f32, a["bandmask"]).then_inc(s_in, 16)
                sp.dma_start(WQ[:, 0, :], a["wqkv"][0, :, :]).then_inc(s_wq, 16)
                sp.wait_ge(s_in, 64)
                sp.wait_ge(s_wq, 16)

            @block.scalar
            def _(act):
                act.wait_ge(s_in, 64)
                nc.scalar.activation(bandmask[:, :, :], bandmask_f32, ACT.Copy)

            @block.gpsimd
            def _(pool):
                pool.memset(ident[:, :], 0.0).then_inc(made.sem, 1)
                pool.memset(identb[:, :], 0.0).then_inc(made.sem, 1)
                pool.memset(minus_half[:, :], -0.5)
                pool.memset(V[:, :, :, :, DH:DH + 1], 1.0)
                pool.memset(VP[:, :, :, :, DH:DH + 1], 1.0)
                pool.memset(QKT[:, 1, 0:WIN], 0.0)
                pool.wait_ge(made.sem, made.take(2))
                for m in (ident, identb):
                    pool.affine_select(out=m[:, :], in_=m[:, :], compare_op=ALU.not_equal, fill=1.0,
                                       base=0, pattern=[[-1, P]], channel_multiplier=1)
                made.settle(pool)

        to_tokens = flow("tile_transposed_to_tokens")
        stats_in = flow("bn_stats_done")
        aggr_in = flow("mean_var_done")
        var_in = flow("variance_ready")
        rstd_in = flow("rstd_ready")
        ntok_in = flow("normalised_tile_ready")
        nfeat_in = flow("normalised_half_in_psum")
        res_in = flow("normalised_tile_for_residual")

        def norm(tokens=None, features=None, rms=False, eps=1e-5, dst=None, scale=None, bias=None,
                 residual=None):
            src = tokens if tokens is not None else (lambda t: bank_tiles(0, t))
            with nc.Block() as block:
                @block.tensor
                def _(pe):
                    if features is not None:
                        for t in range(NT):
                            tr = nc.tensor.transpose(bank_tiles(0, t), features[:, t * P:(t + 1) * P],
                                                     ident[:, :])
                            if t % 4 == 3:
                                tr.then_inc(to_tokens.sem, 1)
                    if dst is not None:
                        for t in range(NT):
                            pe.wait_ge(ntok_in.sem, ntok_in.take())
                            tr = nc.tensor.transpose(bank_tiles(2, t), NTOK[:, t, :], ident[:, :])
                            if t % 4 == 3:
                                tr.then_inc(nfeat_in.sem, 1)
                    ntok_in.settle(pe)

                @block.vector
                def _(dve):
                    for t in range(NT):
                        if features is not None and t % 4 == 0:
                            dve.wait_ge(to_tokens.sem, to_tokens.take())
                        nc.vector.bn_stats(bn[:, t, :], src(t)).then_inc(stats_in.sem, 1)
                    for t in range(NT):
                        dve.wait_ge(stats_in.sem, stats_in.take())
                        nc.vector.bn_aggr(mv[:, t, :], bn[:, t, :]).then_inc(aggr_in.sem, 1)
                    dve.wait_ge(aggr_in.sem, aggr_in.take(NT))
                    if rms:
                        nc.vector.tensor_tensor(ms[:, :], mv[:, :, 0], mv[:, :, 0], ALU.mult)\
                            .then_inc(aggr_in.sem, 1)
                        dve.wait_ge(aggr_in.sem, aggr_in.take())
                        nc.vector.scalar_tensor_tensor(ve[:, :], ms[:, :], eps, mv[:, :, 1],
                                                       ALU.add, ALU.add).then_inc(var_in.sem, 1)
                    else:
                        nc.vector.tensor_scalar(ve[:, :], mv[:, :, 1], eps, None, ALU.add)\
                            .then_inc(var_in.sem, 1)
                    dve.wait_ge(rstd_in.sem, rstd_in.take())
                    for t in range(NT):
                        done = ntok_in if dst is not None else res_in
                        if rms:
                            nc.vector.tensor_scalar(NTOK[:, t, :], src(t), rstd[:, t:t + 1], None,
                                                    ALU.mult).then_inc(done.sem, 1)
                        else:
                            nc.vector.tensor_scalar(NTOK[:, t, :], src(t), mv[:, t, 0:1],
                                                    rstd[:, t:t + 1], ALU.subtract, ALU.mult)\
                                .then_inc(done.sem, 1)
                    if residual is not None:
                        dve.wait_ge(res_in.sem, res_in.take(NT))
                        nc.vector.tensor_tensor(residual, residual, NTOK[:, :, :], ALU.add)
                    for f in (to_tokens, stats_in, aggr_in, rstd_in, res_in):
                        f.settle(dve)

                @block.gpsimd
                def _(pool):
                    pool.wait_ge(var_in.sem, var_in.take())
                    nc.gpsimd.tensor_tensor(rstd[:, :], ve[:, :], minus_half[:, 0:NT], ALU.pow)\
                        .then_inc(rstd_in.sem, 1)
                    var_in.settle(pool)

                @block.scalar
                def _(act):
                    if dst is not None:
                        for h in range(NH):
                            act.wait_ge(nfeat_in.sem, nfeat_in.take())
                            nc.scalar.activation(dst[:, h * HALF:(h + 1) * HALF], PS[:, 2 + h, :],
                                                 ACT.Identity if bias is not None else ACT.Copy,
                                                 scale=1.0 if scale is None else scale,
                                                 bias=0.0 if bias is None else bias)
                    nfeat_in.settle(act)

        def x_tiles(b):
            return lambda t: X[:, bass.ds(b * NT + t, 1), :].rearrange("p o d -> p (o d)")

        def x_batch(b):
            return X[:, bass.ds(b * NT, NT), :]

        if "A" in stages:
            W3 = BIG[:, 0:3 * D].rearrange("p (k n) -> p k n", k=3)
            WGA = BIG[:, 384:384 + FA]
            WUA = BIG[:, 768:768 + FA]
            WOA = BIG[:, 1152:1152 + FA].rearrange("p (j n) -> p j n", j=3)
            PA = BIG[:, 1536:1541]
            SIG = BIG[:, 2048:2048 + S]
            TAN = BIG[:, 3072:3072 + S]
            SCA = BIG[:, 4096:4096 + S]
            SCX = BIG[:, 5120:5120 + S]
            X1 = BIG[:, 6144:6144 + S]
            HT = BIG[:, 2048:2048 + 3 * S].rearrange("p (j n) -> p j n", j=3)
            SGA = SQ[:, :, :, :].rearrange("p k a b -> p k (a b)")
            GSA = [r[:, :, :].rearrange("p a b -> p (a b)") for r in (R1, R2)]
            gates_in = flow("gates_in_psum")
            ups_in = flow("ups_in_psum")
            ffn_in = flow("ffn_in_psum")
            gates_act = flow("gates_activated")
            scan_in = flow("scan_operands_ready")
            silu_in = flow("gate_times_sigmoid_ready")
            hidden_in = flow("hidden_ready")
            with nc.Block() as block:
                @block.sync
                def _(sp):
                    sp.dma_start(W3, a["w3"]).then_inc(s_in, 16)
                    sp.dma_start(WGA, a["wga"]).then_inc(s_in, 16)
                    sp.dma_start(WUA, a["wua"]).then_inc(s_in, 16)
                    sp.dma_start(WOA, a["woa"]).then_inc(s_in, 16)
                    sp.dma_start(PA, a["pa"]).then_inc(s_in, 16)
                    sp.wait_ge(s_in, 64 + 80)
            with nc.Fori(0, B) as b:
                norm(tokens=x_tiles(b), dst=XS[:, :])
                norm(features=XS, rms=True, eps=1e-6, dst=XN[:, :], scale=PA[:, 0:1])
                with nc.Block() as block:
                    @block.tensor
                    def _(pe):
                        for h in range(NH):
                            for k in range(3):
                                nc.tensor.matmul(PS[:, 3 * h + k, :], W3[:, k, :],
                                                 XN[:, h * HALF:(h + 1) * HALF],
                                                 start=True, stop=True).then_inc(gates_in.sem, 1)

                    @block.scalar
                    def _(act):
                        for h in range(NH):
                            cols = slice(h * HALF, (h + 1) * HALF)
                            for k, (f, dst) in enumerate(((ACT.Sigmoid, SIG), (ACT.Tanh, TAN),
                                                          (ACT.Sigmoid, SCA))):
                                act.wait_ge(gates_in.sem, gates_in.take())
                                nc.scalar.activation(dst[:, cols], PS[:, 3 * h + k, :], f,
                                                     bias=PA[:, 2 + k:3 + k]).then_inc(gates_act.sem, 1)
                        gates_in.settle(act)

                    @block.vector
                    def _(dve):
                        for h in range(NH):
                            cols = slice(h * HALF, (h + 1) * HALF)
                            dve.wait_ge(gates_act.sem, gates_act.take(2))
                            nc.vector.tensor_tensor(SCX[:, cols], SIG[:, cols], TAN[:, cols], ALU.mult)\
                                .then_inc(scan_in.sem, 1)
                            dve.wait_ge(gates_act.sem, gates_act.take())
                            nc.vector.tensor_scalar(SCA[:, cols], SCA[:, cols], 0.998, 0.001,
                                                    ALU.mult, ALU.add).then_inc(scan_in.sem, 1)
                        dve.wait_ge(scan_in.sem, scan_in.take(4))
                        nc.vector.tensor_tensor_scan(YT[:, :], SCA, SCX, 0.0, ALU.mult, ALU.add)\
                            .then_inc(scan_in.sem, 1)
                        dve.wait_ge(scan_in.sem, scan_in.take())
                        nc.vector.tensor_tensor(X1, YT[:, :], XS[:, :], ALU.add)
                        gates_act.settle(dve)
                        scan_in.settle(dve)
                norm(features=X1, rms=True, eps=1e-6, dst=XN[:, :], scale=PA[:, 1:2])
                with nc.Block() as block:
                    @block.tensor
                    def _(pe):
                        for h in range(NH):
                            cols = slice(h * HALF, (h + 1) * HALF)
                            for j in range(3):
                                i = 3 * h + j
                                if i >= 2:
                                    pe.wait_ge(hidden_in.sem, hidden_in.peek(i - 1))
                                nc.tensor.matmul(PS[:, 2 * (i % 2), :], WGA[:, j * P:(j + 1) * P],
                                                 XN[:, cols], start=True, stop=True)\
                                    .then_inc(gates_in.sem, 1)
                                nc.tensor.matmul(PS[:, 2 * (i % 2) + 1, :], WUA[:, j * P:(j + 1) * P],
                                                 XN[:, cols], start=True, stop=True)\
                                    .then_inc(ups_in.sem, 1)
                        for h in range(NH):
                            pe.wait_ge(hidden_in.sem, hidden_in.take(3))
                            for j in range(3):
                                mm = nc.tensor.matmul(PS[:, 4 + h, :], WOA[:, j, :],
                                                      HT[:, j, h * HALF:(h + 1) * HALF],
                                                      start=j == 0, stop=j == 2)
                            mm.then_inc(ffn_in.sem, 1)
                        hidden_in.settle(pe)

                    @block.scalar
                    def _(act):
                        for i in range(3 * NH):
                            act.wait_ge(gates_in.sem, gates_in.take())
                            nc.scalar.activation(SGA[:, i % 2, :], PS[:, 2 * (i % 2), :], ACT.Sigmoid)\
                                .then_inc(gates_act.sem, 1)
                        gates_in.settle(act)

                    @block.vector
                    def _(dve):
                        for i in range(3 * NH):
                            h, j = i // 3, i % 3
                            dve.wait_ge(gates_act.sem, gates_act.take())
                            nc.vector.tensor_tensor(GSA[i % 2], PS[:, 2 * (i % 2), :], SGA[:, i % 2, :],
                                                    ALU.mult).then_inc(silu_in.sem, 1)
                            dve.wait_ge(ups_in.sem, ups_in.take())
                            dve.wait_ge(silu_in.sem, silu_in.take())
                            nc.vector.tensor_tensor(HT[:, j, h * HALF:(h + 1) * HALF], GSA[i % 2],
                                                    PS[:, 2 * (i % 2) + 1, :], ALU.mult)\
                                .then_inc(hidden_in.sem, 1)
                        for h in range(NH):
                            dve.wait_ge(ffn_in.sem, ffn_in.take())
                            nc.vector.tensor_tensor(YT[:, h * HALF:(h + 1) * HALF], PS[:, 4 + h, :],
                                                    X1[:, h * HALF:(h + 1) * HALF], ALU.add)
                        for f in (gates_act, silu_in, ups_in, ffn_in):
                            f.settle(dve)
                norm(features=YT, residual=x_batch(b))

        if "B" in stages:
            XTf = XT[:, :, :].rearrange("p b s -> p (b s)")
            WQf = WQ[:, :, :].rearrange("p k n -> p (k n)")
            BIGf = BIG[:, :]
            Vb = V[:, :, :, :, :].rearrange("p c j h d -> p (c j) (h d)")
            VPb = VP[:, :, :, :, :].rearrange("p c j h d -> p (c j) (h d)")
            COSLb, SINLb = COSL[:, :, :], SINL[:, :, :]
            SQv = SQ[:, :, :, :].rearrange("p k (j g) d -> p k j (g d)", j=CB)
            R2s = R2[:, :, :].rearrange("p j (g v d) -> p j g v d", v=2, d=DH // 2)
            SINs = SINL[:, :, :].rearrange("p t (g v d) -> p t g v d", v=2, d=DH // 2)
            RRg = RR[:, :, :].rearrange("p j (g d) -> p (j g) d", d=DH)
            QKg = [QK[:, k, :, :, :].rearrange("p j k (h d) -> p (j k h) d", d=DH) for k in range(2)]
            PQ, TQ, SC, PT, PO, OT = PS[:, 0:2, :], PS[:, 2, :], PS[:, 3:5, :], PS[:, 5, :], PS[:, 6, :], PS[:, 7, :]
            POu = PS[:, 6, 0:4 * (DH + 1)].rearrange("p (u d) -> p u d", d=DH + 1)
            wq_in = flow("next_wqkv_in")
            layer_in = flow("layer_weights_in")
            proj_in = flow("qkv_in_psum")
            rot_in = flow("rotation_products_ready")
            sq_in = flow("squares_ready")
            pq_free = flow("qkv_banks_read")
            n2_in = flow("square_norms_ready")
            n2g_in = flow("square_norms_guarded")
            rr_in = flow("rotated_and_rnorm_ready")
            qk_in = flow("rotated_scaled_ready")
            qkt_ps = flow("qk_transposed_in_psum")
            qkt_in = flow("qk_feature_major_ready")
            sc_in = flow("head_scores_in_psum")
            nmx_in = flow("head_max_ready")
            p_in = flow("probabilities_ready")
            p_tail = flow("probabilities_complete")
            pt_ps = flow("probabilities_transposed_in_psum")
            pts_in = flow("probabilities_transposed")
            pps_in = flow("previous_window_transposed")
            o_ps = flow("attention_out_in_psum")
            ro_in = flow("softmax_sums_inverted")
            on_in = flow("attention_out_normalised")
            ot_ps = flow("attention_out_transposed")
            ot_free = flow("transposed_out_copied")
            wo_in = flow("projected_half_in_psum")
            table_in = flow("cos_table_ready")
            gelu_free = flow("gate_tile_used")

            for b in range(B):
                norm(tokens=x_tiles(b), dst=XT[:, b, :])
            with nc.Block() as block:
                @block.vector
                def _(dve):
                    nc.vector.memset(XS[D // 2:P, 0:1], 0.0)

            def shift_tokens(b):
                with nc.Block() as block:
                    @block.vector
                    def _(dve):
                        nc.vector.tensor_copy(XS[0:D // 2, :], XTf[0:D // 2, bass.ds(b * S, S)])

                    @block.scalar
                    def _(act):
                        nc.scalar.activation(XS[D // 2:P, 1:S], XTf[D // 2:P, bass.ds(b * S, S - 1)],
                                             ACT.Copy)

            N = PAIRS * CH

            def run(eng, step, flows):
                def settle():
                    for f in flows:
                        f.settle(eng)
                for n in range(-3, 2):
                    step(n, 0)
                settle()
                with eng.Fori(0, PAIRS - 2) as i:
                    for n in range(2, 2 + CH):
                        step(n, i)
                    settle()
                for n in range(N + 2 - 2 * CH, N + 2):
                    step(n, 0)
                return settle

            def attention(l, b):
                par = (l % 2) * (PAIRS * 384)

                with nc.Block() as block:
                    @block.tensor
                    def _(pe):
                        def step(n, i):
                            if 0 <= n - 1 < N:
                                pe.wait_ge(p_in.sem, p_in.take(4))
                                for u in range(4):
                                    tr = nc.tensor.transpose(PT[:, u * P:(u + 1) * P],
                                                             PR[:, (n - 1) % 2, u, WIN:KW], ident[:, :])
                                    if u == 0:
                                        tr.then_inc(p_tail.sem, 1)
                                tr.then_inc(pt_ps.sem, 1)
                            if 0 <= n < N:
                                c = n % CH
                                pe.wait_ge(qkt_in.sem, qkt_in.take())
                                for h in range(2):
                                    rows = slice(DH * h, DH * h + DH)
                                    first = 0 if c == 0 else 1
                                    nc.tensor.matmul(
                                        SC[:, h, 0:CB * KW], identb[:, :],
                                        bandmask[:, first:first + CB, :].rearrange("p j k -> p (j k)"),
                                        start=True, stop=False)
                                    for j in range(CB):
                                        t0 = (CB * c + j) * P
                                        mm = nc.tensor.matmul(SC[:, h, j * KW:(j + 1) * KW],
                                                              QKT[rows, 0, WIN + t0:WIN + t0 + P],
                                                              QKT[rows, 1, t0:t0 + KW],
                                                              start=False, stop=j == CB - 1)
                                    mm.then_inc(sc_in.sem, 1)
                            if 0 <= n - 2 < N:
                                pe.wait_ge(on_in.sem, on_in.take())
                                if n >= N:
                                    pe.wait_ge(ot_free.sem, ot_free.take())
                                for j in range(CB):
                                    tr = nc.tensor.transpose(OT[:, j * P:(j + 1) * P], ON[:, j, :],
                                                             ident[:, :])
                                tr.then_inc(ot_ps.sem, 1)
                            if 0 <= n - 1 < N:
                                c = (n - 1) % CH
                                pe.wait_ge(pts_in.sem, pts_in.take())
                                for j in range(CB):
                                    for h in range(2):
                                        u, o = 2 * h + j, 2 * j + h
                                        mm = nc.tensor.matmul(POu[:, o, :], PTS[:, u, :], V[:, c, j, h, :],
                                                              start=o == 0, stop=o == 3,
                                                              skip_group_check=True)
                                pe.wait_ge(pps_in.sem, pps_in.take())
                                for j in range(CB):
                                    for h in range(2):
                                        u, o = 2 * h + j, 2 * j + h
                                        if c > 0 or j > 0:
                                            mm = nc.tensor.matmul(POu[0:WIN, o, :], PPS[:, u, :],
                                                                  VP[:, c, j, h, :], start=False,
                                                                  stop=True, skip_group_check=True)
                                mm.then_inc(o_ps.sem, 1)
                            if 0 <= n + 1 < N:
                                pe.wait_ge(qk_in.sem, qk_in.take())
                                for k in range(2):
                                    for j in range(CB):
                                        tr = nc.tensor.transpose(TQ[:, (2 * k + j) * P:(2 * k + j + 1) * P],
                                                                 QK[:, (n + 1) % 2, j, k, :], ident[:, :])
                                tr.then_inc(qkt_ps.sem, 1)
                            if 0 <= n + 3 < N:
                                c = (n + 3) % CH
                                if n + 3 > 0:
                                    pe.wait_ge(pq_free.sem, pq_free.take())
                                w0 = par + ((n + 3) // CH + i) * 384
                                for j in range(CB):
                                    t0 = (CB * c + j) * P
                                    mm = nc.tensor.matmul(PQ[:, j, 0:384], XS[:, t0:t0 + P],
                                                          WQf[:, bass.ds(w0, 384)], start=True, stop=True)
                                mm.then_inc(proj_in.sem, 1)
                        settle = run(pe, step, [ot_free, qkt_in, p_in, on_in, pq_free, pts_in, pps_in, qk_in])
                        pe.wait_ge(pq_free.sem, pq_free.take())
                        settle()

                    @block.scalar
                    def _(act):
                        PQv = PQ[:, :, 256:384].rearrange("p j (h d) -> p j h d", h=2)

                        def step(n, i):
                            if 0 <= n - 1 < N:
                                act.wait_ge(pt_ps.sem, pt_ps.take())
                                nc.scalar.activation(PTS[:, :, :].rearrange("p u k -> p (u k)"), PT,
                                                     ACT.Copy).then_inc(pts_in.sem, 1)
                            if 0 <= n < N:
                                for h in range(2):
                                    act.wait_ge(nmx_in.sem, nmx_in.take())
                                    for j in range(CB):
                                        u = 2 * h + j
                                        nc.scalar.activation(PR[:, n % 2, u, :],
                                                             SC[:, h, j * KW:(j + 1) * KW], ACT.Exp,
                                                             bias=NMX[:, u:u + 1]).then_inc(p_in.sem, 1)
                            if 0 <= n - 2 < N:
                                c = (n - 2) % CH
                                act.wait_ge(ot_ps.sem, ot_ps.take())
                                cp = nc.scalar.activation(
                                    BIGf[:, bass.ds(((n - 2) // CH + i) * S + c * CB * P, CB * P)],
                                    OT[:, 0:CB * P], ACT.Copy)
                                if N - 1 <= n <= N:
                                    cp.then_inc(ot_free.sem, 1)
                            if 0 <= n + 1 < N:
                                c = (n + 1) % CH
                                lo = 0 if c else 1
                                act.wait_ge(qkt_ps.sem, qkt_ps.take())
                                nc.scalar.activation(
                                    QKT[:, :, WIN + c * CB * P:WIN + (c + 1) * CB * P],
                                    TQ.rearrange("p (k s) -> p k s", k=2), ACT.Copy).then_inc(qkt_in.sem, 1)
                                nc.scalar.activation(VPb[:, CB * c + lo:CB * c + CB, :],
                                                     Vb[P - WIN:P, CB * c + lo - 1:CB * c + CB - 1, :],
                                                     ACT.Copy)
                            if 0 <= n + 3 < N:
                                c = (n + 3) % CH
                                act.wait_ge(proj_in.sem, proj_in.take())
                                nc.scalar.activation(SQv[:, (n + 3) % 2, :, :], PQ[:, :, 0:256], ACT.Square)
                                nc.scalar.activation(V[:, c, :, :, 0:DH], PQv, ACT.Copy)\
                                    .then_inc(sq_in.sem, 1)
                        run(act, step, [nmx_in, ot_ps, pt_ps, proj_in, qkt_ps])()

                    @block.vector
                    def _(dve):
                        def step(n, i):
                            if 0 <= n - 1 < N:
                                dve.wait_ge(p_tail.sem, p_tail.take())
                                nc.vector.transpose(PPS[:, :, :], PR[0:WIN, (n - 1) % 2, :, 0:WIN])\
                                    .then_inc(pps_in.sem, 1)
                            if 0 <= n + 1 < N:
                                dve.wait_ge(rr_in.sem, rr_in.take())
                                nc.vector.tensor_tensor(QKg[(n + 1) % 2], RRg, RN[:, :].unsqueeze(2)
                                                        .to_broadcast([P, 8, DH]), ALU.mult)\
                                    .then_inc(qk_in.sem, 1)
                            if 0 <= n + 2 < N:
                                c = (n + 2) % CH
                                t = slice(CB * c, CB * c + CB)
                                qk5 = PQ[:, :, 0:256].rearrange("p j (g v d) -> p j g v d", v=2, d=DH // 2)
                                dve.wait_ge(sq_in.sem, sq_in.take())
                                nc.vector.tensor_reduce(N2[:, :], SQ[:, n % 2, :, :], AX.X, ALU.add)\
                                    .then_inc(n2_in.sem, 1)
                                nc.vector.tensor_tensor(R1[:, :, :], PQ[:, :, 0:256], COSLb[:, t, :],
                                                        ALU.mult)
                                for v in range(2):
                                    rot = nc.vector.tensor_tensor(R2s[:, :, :, v, :], qk5[:, :, :, 1 - v, :],
                                                                  SINs[:, t, :, v, :], ALU.mult)
                                rot.then_inc(rot_in.sem, 1)
                            if 0 <= n < N:
                                for h in range(2):
                                    dve.wait_ge(sc_in.sem, sc_in.take())
                                    nc.vector.tensor_reduce(
                                        NMX[:, 2 * h:2 * h + 2],
                                        SC[:, h, 0:CB * KW].rearrange("p (j k) -> p j k", k=KW),
                                        AX.X, ALU.max, negate=True).then_inc(nmx_in.sem, 1)
                            if 0 <= n - 1 < N:
                                dve.wait_ge(o_ps.sem, o_ps.take())
                                nc.vector.reciprocal(RO[:, :], POu[:, :, DH]).then_inc(ro_in.sem, 1)
                                dve.wait_ge(ro_in.sem, ro_in.take())
                                nc.vector.tensor_tensor(
                                    ON[:, :, :].rearrange("p j (h d) -> p (j h) d", h=2), POu[:, :, 0:DH],
                                    RO[:, :].unsqueeze(2).to_broadcast([P, 4, DH]), ALU.mult)\
                                    .then_inc(on_in.sem, 1)
                        run(dve, step, [sc_in, p_tail, rr_in, sq_in, o_ps, ro_in])()

                    @block.gpsimd
                    def _(pool):
                        def step(n, i):
                            if 0 <= n + 2 < N:
                                pool.wait_ge(n2_in.sem, n2_in.take())
                                nc.gpsimd.tensor_scalar(N2G[:, :], N2[:, :], 1e-24, None, ALU.max)\
                                    .then_inc(n2g_in.sem, 1)
                                pool.wait_ge(n2g_in.sem, n2g_in.take())
                                nc.gpsimd.tensor_tensor(RN[:, :], N2G[:, :], minus_half[:, :], ALU.pow)
                                pool.wait_ge(rot_in.sem, rot_in.take())
                                pool.sem_inc(pq_free.sem, 1)
                                nc.gpsimd.tensor_tensor(RR[:, :, :], R1[:, :, :], R2[:, :, :], ALU.add)\
                                    .then_inc(rr_in.sem, 1)
                        run(pool, step, [n2_in, n2g_in, rot_in])()

            def project(b):
                with nc.Block() as block:
                    @block.tensor
                    def _(pe):
                        for h in range(NH):
                            for hp in range(PAIRS):
                                mm = nc.tensor.matmul(PS[:, h, :], WO[:, hp, :],
                                                      OTS[:, hp, h * HALF:(h + 1) * HALF],
                                                      start=hp == 0, stop=hp == PAIRS - 1)
                            mm.then_inc(wo_in.sem, 1)

                    @block.vector
                    def _(dve):
                        for h in range(NH):
                            dve.wait_ge(wo_in.sem, wo_in.take())
                            cols = bass.ds(b * S + h * HALF, HALF)
                            nc.vector.tensor_tensor(XTf[:, cols], XTf[:, cols], PS[:, h, :], ALU.add)
                        wo_in.settle(dve)

            GL = [BIG[:, k * HALF:(k + 1) * HALF] for k in range(2)]
            HB = BIG[:, 2 * HALF:2 * HALF + 3 * S].rearrange("p (j s) -> p j s", j=3)

            def geglu(b):
                with nc.Block() as block:
                    @block.tensor
                    def _(pe):
                        for i in range(3 * NH):
                            h, j = i // 3, i % 3
                            cols = slice(h * HALF, (h + 1) * HALF)
                            w = FJ[j]
                            if i >= 2:
                                pe.wait_ge(gelu_free.sem, gelu_free.peek(i - 1))
                            nc.tensor.matmul(PS[0:w, 2 * (i % 2), :], W1[:, FI + j * P:FI + j * P + w],
                                             XN[:, cols], start=True, stop=True).then_inc(proj_in.sem, 1)
                            nc.tensor.matmul(PS[0:w, 2 * (i % 2) + 1, :], W1[:, j * P:j * P + w],
                                             XN[:, cols], start=True, stop=True).then_inc(sc_in.sem, 1)
                        for h in range(NH):
                            pe.wait_ge(gelu_free.sem, gelu_free.take(3))
                            for j, w in enumerate(FJ):
                                mm = nc.tensor.matmul(PS[:, 4 + h, :], W2[0:w, j, :],
                                                      HB[0:w, j, h * HALF:(h + 1) * HALF],
                                                      start=j == 0, stop=j == 2)
                            mm.then_inc(wo_in.sem, 1)
                        gelu_free.settle(pe)

                    @block.scalar
                    def _(act):
                        for i in range(3 * NH):
                            w, j = FJ[i % 3], i % 3
                            act.wait_ge(proj_in.sem, proj_in.take())
                            nc.scalar.activation(GL[i % 2][0:w, :], PS[0:w, 2 * (i % 2), :], ACT.Gelu,
                                                 bias=PL[0:w, 5 + j:6 + j]).then_inc(nmx_in.sem, 1)
                        proj_in.settle(act)

                    @block.vector
                    def _(dve):
                        for i in range(3 * NH):
                            h, j, w = i // 3, i % 3, FJ[i % 3]
                            dve.wait_ge(nmx_in.sem, nmx_in.take())
                            dve.wait_ge(sc_in.sem, sc_in.take())
                            nc.vector.scalar_tensor_tensor(
                                HB[0:w, j, h * HALF:(h + 1) * HALF], PS[0:w, 2 * (i % 2) + 1, :],
                                PL[0:w, 2 + j:3 + j], GL[i % 2][0:w, :], ALU.add, ALU.mult)\
                                .then_inc(gelu_free.sem, 1)
                        for h in range(NH):
                            dve.wait_ge(wo_in.sem, wo_in.take())
                            cols = bass.ds(b * S + h * HALF, HALF)
                            nc.vector.scalar_tensor_tensor(XTf[:, cols], PS[:, 4 + h, :], PL[:, 8:9],
                                                           XTf[:, cols], ALU.add, ALU.add)
                        for f in (nmx_in, sc_in, wo_in):
                            f.settle(dve)

            with nc.Fori(0, LAYERS) as l:
                with nc.Block() as block:
                    @block.sync
                    def _(sp):
                        for dst, name in ((QKS[:, :, :], "qks"), (PL[:, :], "pl"), (WO[:, :, :], "wo"),
                                          (W1[:, :], "w1"), (W2[:, :, :], "w2")):
                            src = a[name]
                            if name == "qks":
                                src = src[bass.ds(l, 1), :, :].partition_broadcast(P)
                                src = src.rearrange("p o k n -> p (o k) n")
                            elif len(src.shape) == 4:
                                src = src[bass.ds(l, 1), :, :, :].rearrange("o p j n -> (o p) j n")
                            else:
                                src = src[bass.ds(l, 1), :, :].rearrange("o p n -> (o p) n")
                            sp.dma_start(dst, src).then_inc(layer_in.sem, 16)
                            if name == "qks":
                                sp.wait_ge(layer_in.sem, layer_in.take(16))
                                sp.sem_inc(table_in.sem, 1)
                        sp.wait_ge(layer_in.sem, layer_in.take(64))
                        layer_in.settle(sp)
                        nl = (l + 1) % LAYERS
                        sp.dma_start(WQf[:, bass.ds(((l + 1) % 2) * (PAIRS * 384), PAIRS * 384)],
                                     a["wqkv"][bass.ds(nl, 1), :, :].rearrange("o p n -> (o p) n"))\
                            .then_inc(wq_in.sem, 16)

                    @block.vector
                    def _(dve):
                        dve.wait_ge(table_in.sem, table_in.take())
                        for k, (dst, src) in enumerate(((COSL, COS0), (SINL, SIN0))):
                            nc.vector.tensor_tensor(dst[:, :, :], src[:, :, :],
                                                    QKS[:, k, :].unsqueeze(1).to_broadcast([P, NT, 256]),
                                                    ALU.mult)
                        table_in.settle(dve)
                with nc.Fori(0, B) as b:
                    shift_tokens(b)
                    attention(l, b)
                    project(b)
                    shift_tokens(b)
                    norm(features=XS, dst=XN[:, :], scale=PL[:, 0:1], bias=PL[:, 1:2])
                    geglu(b)
                with nc.Block() as block:
                    @block.sync
                    def _(sp):
                        sp.wait_ge(wq_in.sem, wq_in.take(16))
                        wq_in.settle(sp)
            with nc.Fori(0, B) as b:
                with nc.Block() as block:
                    @block.scalar
                    def _(act):
                        nc.scalar.activation(YT[:, :], XTf[:, bass.ds(b * S, S)], ACT.Copy)
                norm(features=YT, residual=x_batch(b))
        if "C" in stages:
            WC = BIG[:, 0:384]
            WOC = BIG[:, 384:512]
            HM = BIG[:, 512:516]
            BDM = BIG[:, 640:768]
            CAU = BIG[:, 768:896]
            BD = BIG[:, 896:1024]
            BDT = BIG[:, 1024:1152]
            KE = COSL[:, 0:4, :].rearrange("p a b -> p (a b)")
            ZR = COSL[:, 4:8, :].rearrange("p a b -> p (a b)")
            KET = SINL[:, 0:4, :].rearrange("p a (c n) -> p (a c) n", n=P)
            QP = SINL[:, 4:8, :].rearrange("p a b -> p (a b)")
            QV = BIG[:, 1152:1152 + NT * 256].rearrange("p (t n) -> p t n", n=256)
            QM = BIG[:, 3200:3200 + 4 * S].rearrange("p (j s) -> p j s", j=4)
            AM = COS0[:, :, :].rearrange("p a b -> p (a b)").rearrange("p (g n) -> p g n", g=4)
            OCT = SIN0[:, 0:4, :].rearrange("p a b -> p (a b)")
            ONES = SIN0[:, 4:8, :].rearrange("p a b -> p (a b)")
            OC = R1[:, 0, 0:P]
            qm = RR[:, 0, 0:P]
            qsum = RR[:, 0, P:2 * P]
            qr = RR[:, 1, 0:P]
            kmx = NMX[:, 0:1]
            layer_c = flow("stage_c_weights_in")
            am_free = flow("masked_scores_used")
            st_free = flow("state_used")
            SQ8 = [t[:, :, 0:P].rearrange("p t (h c) -> p t h c", c=LC) for t in (QV,)][0]
            qv_ps = flow("qv_tile_in_psum")
            qv_in = flow("qv_tile_copied")
            qv_free = flow("qv_bank_copied")
            k_ps = flow("k_in_psum")
            kmx_in = flow("k_max_ready")
            ke_in = flow("k_exp_ready")
            ke_pe = flow("k_exp_ready_for_transposes")
            z_in = flow("k_cumulated")
            qs_in = flow("q_softmax_step")
            qe_in = flow("q_shifted")
            qx_in = flow("q_exp_ready")
            qn_in = flow("q_normalised")
            qt_ps = flow("q_transposed")
            kt_ps = flow("k_transposed")
            kt_in = flow("k_token_major")
            qm_in = flow("q_masks_ready")
            a_ps = flow("scores_in_psum")
            a_in = flow("scores_masked")
            st_ps = flow("state_update_in_psum")
            bdt_in = flow("state_update_masked")
            bd_in = flow("state_ready")
            oc_ps = flow("linear_out_in_psum")
            oc_in = flow("linear_out_copied")
            oct_ps = flow("linear_out_transposed")
            oct_in = flow("linear_out_feature_major")
            yc_ps = flow("projection_in_psum")
            with nc.Block() as block:
                @block.sync
                def _(sp):
                    for dst, n in ((WC, "wc"), (WOC, "woc"), (HM, "headmask"), (BDM, "blockdiag"),
                                   (CAU, "causal")):
                        sp.dma_start(dst, a[n]).then_inc(layer_c.sem, 16)
                    sp.wait_ge(layer_c.sem, layer_c.take(80))
                    layer_c.settle(sp)

                @block.vector
                def _(dve):
                    nc.vector.memset(ONES, 1.0)
            with nc.Fori(0, B) as b:
                norm(tokens=x_tiles(b), dst=XN[:, :])
                with nc.Block() as block:
                    @block.tensor
                    def _(pe):
                        for h in range(NH):
                            mm = nc.tensor.matmul(PS[:, h, :], WC[:, 256:384], XN[:, h * HALF:(h + 1) * HALF],
                                                  start=True, stop=True)
                        mm.then_inc(k_ps.sem, 1)
                        for t in range(NT):
                            if t >= 2:
                                pe.wait_ge(qv_free.sem, qv_free.peek(t - 1))
                            nc.tensor.matmul(PS[:, 2 + t % 2, 0:256], XN[:, t * P:(t + 1) * P], WC[:, 0:256],
                                             start=True, stop=True).then_inc(qv_ps.sem, 1)
                        pe.wait_ge(qv_free.sem, qv_free.take(NT))
                        pe.wait_ge(ke_pe.sem, ke_pe.take())
                        for t in range(NT):
                            tr = nc.tensor.transpose(bank_tiles(4, t), KE[:, t * P:(t + 1) * P], ident[:, :])
                        tr.then_inc(kt_ps.sem, 1)
                        pe.wait_ge(qn_in.sem, qn_in.take())
                        for t in range(NT):
                            tr = nc.tensor.transpose(bank_tiles(6, t), QV[:, t, 0:P], ident[:, :])
                        tr.then_inc(qt_ps.sem, 1)
                        for f in (qv_free, ke_pe, qn_in):
                            f.settle(pe)

                    @block.scalar
                    def _(act):
                        for t in range(NT):
                            act.wait_ge(qv_ps.sem, qv_ps.take())
                            nc.scalar.activation(QV[:, t, :], PS[:, 2 + t % 2, 0:256], ACT.Copy)\
                                .then_inc(qv_free.sem, 1)
                        act.drain().then_inc(qv_in.sem, 1)
                        act.wait_ge(kmx_in.sem, kmx_in.take())
                        nc.scalar.activation(KE.rearrange("p (h s) -> p h s", h=NH), PS[:, 0:2, :], ACT.Exp,
                                             bias=kmx).then_inc(ke_in.sem, 1)
                        act.drain().then_inc(ke_pe.sem, 1)
                        act.wait_ge(qe_in.sem, qe_in.take())
                        nc.scalar.activation(SQ8, SQ8, ACT.Exp).then_inc(qx_in.sem, 1)
                        act.wait_ge(kt_ps.sem, kt_ps.take())
                        nc.scalar.activation(KET.rearrange("p (h t) n -> p h (t n)", h=2), PS[:, 4:6, :],
                                             ACT.Copy)
                        for f in (qv_ps, kmx_in, qe_in, kt_ps):
                            f.settle(act)

                    @block.vector
                    def _(dve):
                        dve.wait_ge(k_ps.sem, k_ps.take())
                        nc.vector.tensor_reduce(kmx, PS[:, 0:2, :], AX.XY, ALU.max, negate=True)\
                            .then_inc(kmx_in.sem, 1)
                        dve.wait_ge(qv_in.sem, qv_in.take())
                        qh = qm.rearrange("p (t h) -> p t h", h=LH)
                        nc.vector.tensor_reduce(qh, SQ8, AX.X, ALU.max).then_inc(qs_in.sem, 1)
                        dve.wait_ge(qs_in.sem, qs_in.take())
                        for half in range(2):
                            t = slice(4 * half, 4 * half + 4)
                            sub = nc.vector.tensor_tensor(
                                SQ8[:, t, :, :].rearrange("p t h c -> p t (h c)").rearrange("p t (h c) -> p t h c", c=LC),
                                SQ8[:, t, :, :],
                                qh[:, t, :].unsqueeze(3).to_broadcast([P, 4, LH, LC]), ALU.subtract)
                        sub.then_inc(qe_in.sem, 1)
                        dve.wait_ge(ke_in.sem, ke_in.take())
                        nc.vector.tensor_tensor_scan(ZR, ONES, KE, 0.0, ALU.mult, ALU.add).then_inc(z_in.sem, 1)
                        dve.wait_ge(z_in.sem, z_in.take())
                        nc.vector.tensor_scalar(XS[:, :], ZR, 1e-9, None, ALU.add).then_inc(z_in.sem, 1)
                        dve.wait_ge(z_in.sem, z_in.take())
                        nc.vector.reciprocal(ZR, XS[:, :]).then_inc(z_in.sem, 1)
                        dve.wait_ge(qx_in.sem, qx_in.take())
                        nc.vector.tensor_reduce(qsum.rearrange("p (t h) -> p t h", h=LH), SQ8, AX.X, ALU.add)\
                            .then_inc(qs_in.sem, 1)
                        dve.wait_ge(qs_in.sem, qs_in.take())
                        nc.vector.reciprocal(qr, qsum).then_inc(qs_in.sem, 1)
                        dve.wait_ge(qs_in.sem, qs_in.take())
                        qrh = qr.rearrange("p (t h) -> p t h", h=LH)
                        for half in range(2):
                            t = slice(4 * half, 4 * half + 4)
                            mul = nc.vector.tensor_tensor(SQ8[:, t, :, :], SQ8[:, t, :, :],
                                                          qrh[:, t, :].unsqueeze(3)
                                                          .to_broadcast([P, 4, LH, LC]), ALU.mult)
                        mul.then_inc(qn_in.sem, 1)
                        dve.wait_ge(qt_ps.sem, qt_ps.take())
                        dve.wait_ge(z_in.sem, z_in.take())
                        nc.vector.scalar_tensor_tensor(QP.rearrange("p (h s) -> p h s", h=NH), PS[:, 6:8, :],
                                                       float(LC) ** -0.5, ZR.rearrange("p (h s) -> p h s", h=NH),
                                                       ALU.mult, ALU.mult).then_inc(qm_in.sem, 1)
                        dve.wait_ge(qm_in.sem, qm_in.take())
                        for j in range(4):
                            nc.vector.tensor_scalar(QM[:, j, :], QP, HM[:, j:j + 1], None, ALU.mult)
                        nc.vector.memset(BD, 0.0)
                        for f in (k_ps, qv_in, qs_in, ke_in, z_in, qx_in, qt_ps, qm_in):
                            f.settle(dve)
                with nc.Block() as block:
                    @block.tensor
                    def _(pe):
                        for t in range(NT):
                            ts = slice(t * P, (t + 1) * P)
                            if t:
                                pe.wait_ge(a_in.sem, a_in.take())
                            for g in range(4):
                                rows = slice(32 * g, 32 * g + 32)
                                mm = nc.tensor.matmul(PS[:, g, :].rearrange("p (j s) -> p j s", j=4),
                                                      KE[rows, ts], QM[rows, :, ts], start=True, stop=True,
                                                      tile_position=(32 * g, 0))
                            mm.then_inc(a_ps.sem, 1)
                            if t:
                                pe.wait_ge(bd_in.sem, bd_in.take())
                            mm = nc.tensor.matmul(PS[:, 4, 0:P], KET[:, t, :], QV[:, t, P:2 * P],
                                                  start=True, stop=True)
                            mm.then_inc(st_ps.sem, 1)
                            if t:
                                pe.wait_ge(oc_in.sem, oc_in.peek(t))
                            nc.tensor.matmul(PS[:, 5, 0:P], QP[:, ts], BD, start=True, stop=False)
                            pe.wait_ge(a_in.sem, a_in.peek(1))
                            for h in range(LH):
                                mm = nc.tensor.matmul(PS[:, 5, LC * h:LC * h + LC],
                                                      AM[:, h // 4, (h % 4) * P:(h % 4 + 1) * P],
                                                      QV[:, t, P + LC * h:P + LC * h + LC],
                                                      start=False, stop=h == LH - 1)
                            mm.then_inc(oc_ps.sem, 1)
                            pe.wait_ge(oc_in.sem, oc_in.peek(t + 1))
                            if t:
                                pe.wait_ge(oct_in.sem, oct_in.peek(t))
                            nc.tensor.transpose(PS[:, 6, 0:P], OC, ident[:, :]).then_inc(oct_ps.sem, 1)
                        pe.wait_ge(a_in.sem, a_in.take())
                        pe.wait_ge(bd_in.sem, bd_in.take())
                        pe.wait_ge(oc_in.sem, oc_in.take(NT))
                        pe.wait_ge(oct_in.sem, oct_in.take(NT))
                        for h in range(NH):
                            nc.tensor.matmul(PS[:, h, :], WOC, OCT[:, h * HALF:(h + 1) * HALF],
                                             start=True, stop=True).then_inc(yc_ps.sem, 1)
                        for f in (a_in, bd_in, oc_in, oct_in):
                            f.settle(pe)

                    @block.vector
                    def _(dve):
                        for t in range(NT):
                            dve.wait_ge(a_ps.sem, a_ps.take())
                            if t:
                                dve.wait_ge(am_free.sem, am_free.take())
                            nc.vector.tensor_tensor(AM[:, :, :].rearrange("p g (j s) -> p (g j) s", s=P),
                                                    PS[:, 0:4, :].rearrange("p g (j s) -> p (g j) s", s=P),
                                                    CAU.unsqueeze(1).to_broadcast([P, 16, P]), ALU.mult)\
                                .then_inc(a_in.sem, 1)
                            dve.wait_ge(st_ps.sem, st_ps.take())
                            nc.vector.tensor_tensor(BDT, PS[:, 4, 0:P], BDM, ALU.mult).then_inc(bdt_in.sem, 1)
                            dve.wait_ge(bdt_in.sem, bdt_in.take())
                            if t < NT - 1:
                                dve.wait_ge(st_free.sem, st_free.take())
                            else:
                                dve.wait_ge(st_free.sem, st_free.take())
                            nc.vector.tensor_tensor(BD, BD, BDT, ALU.add).then_inc(bd_in.sem, 1)
                        for f in (a_ps, st_ps, bdt_in, am_free, st_free):
                            f.settle(dve)

                    @block.scalar
                    def _(act):
                        for t in range(NT):
                            act.wait_ge(oc_ps.sem, oc_ps.take())
                            nc.scalar.activation(OC, PS[:, 5, 0:P], ACT.Copy).then_inc(oc_in.sem, 1)
                            if t < NT - 1:
                                act.sem_inc(am_free.sem, 1)
                            act.sem_inc(st_free.sem, 1)
                            act.wait_ge(oct_ps.sem, oct_ps.take())
                            nc.scalar.activation(OCT[:, t * P:(t + 1) * P], PS[:, 6, 0:P], ACT.Copy)\
                                .then_inc(oct_in.sem, 1)
                        for h in range(NH):
                            act.wait_ge(yc_ps.sem, yc_ps.take())
                            nc.scalar.activation(YT[:, h * HALF:(h + 1) * HALF], PS[:, h, :], ACT.Copy)
                        for f in (oc_ps, oct_ps, yc_ps):
                            f.settle(act)
                norm(features=YT, residual=x_batch(b))
        if "D" in stages:
            WGU = BIG[:, 0:NE * 2 * EI]
            WD = BIG[:, 4096:4096 + NE * 2 * D]
            GW = BIG[:, 6144:6144 + NE]
            AF = BIG[:, 6160:6160 + NT * B * NE].rearrange("p (t n) -> p t n", n=B * NE)
            GT = BIG[:, 6300:6300 + NT * B * NE].rearrange("p (t n) -> p t n", n=B * NE)
            LG = BIG[:, 6432:6432 + NT * NE].rearrange("p (t e) -> p t e", e=NE)
            LE = BIG[:, 6496:6496 + NT * NE].rearrange("p (t e) -> p t e", e=NE)
            GB = BIG[:, 6560:6560 + NT * NE].rearrange("p (t e) -> p t e", e=NE)
            AT = COS0[0:B * NE, 0:4, :].rearrange("p a b -> p (a b)")
            WK = [COS0[0:B * NE, 4:8, :].rearrange("p a b -> p (a b)"),
                  SIN0[0:B * NE, 0:4, :].rearrange("p a b -> p (a b)")]
            GG = SIN0[0:B * NE, 4:8, :].rearrange("p a b -> p (a b)")
            SGD = SQ[:, :, :, :].rearrange("p k a b -> p k (a b)")[:, :, 0:EI]
            GSD = [R1[:, 0, :], R1[:, 1, :]]
            HD = R2
            HTD = RR
            ACC = YT[:, :].rearrange("p (t n) -> p t n", n=D)
            top8 = [mv[0:B * NE, 4 * k:4 * k + 4, :].rearrange("p a b -> p (a b)") for k in range(2)]
            layer_d = flow("stage_d_weights_in")
            lg_ps = flow("logits_in_psum")
            lg_in = flow("logit_step")
            le_in = flow("logits_shifted")
            lx_in = flow("logits_exp_ready")
            at_ps = flow("affinities_transposed")
            top_in = flow("top8_step")
            gg_in = flow("gates_by_expert_ready")
            gt_ps = flow("gates_transposed")
            up_ps = flow("gate_up_in_psum")
            sg_in = flow("sigmoid_ready")
            gs_in = flow("silu_ready")
            hd_in = flow("hidden_tile_ready")
            ht_ps = flow("hidden_transposed")
            ht_in = flow("hidden_feature_major")
            dn_ps = flow("down_in_psum")
            acc_in = flow("down_accumulated")
            with nc.Block() as block:
                @block.sync
                def _(sp):
                    sp.dma_start(GW, a["gw"]).then_inc(layer_d.sem, 16)
                    sp.dma_start(WGU.rearrange("p (e n) -> p e n", e=NE), a["wgu"]).then_inc(layer_d.sem, 16)
                    sp.dma_start(WD.rearrange("p (e k n) -> p e k n", e=NE, k=2), a["wd"])\
                        .then_inc(layer_d.sem, 16)
                    sp.wait_ge(layer_d.sem, layer_d.take(48))
                    layer_d.settle(sp)
            XTd = XT[:, :, :].rearrange("p b s -> p (b s)")
            with nc.Fori(0, B) as b:
                norm(tokens=x_tiles(b), dst=XN[:, :])
                with nc.Block() as block:
                    @block.tensor
                    def _(pe):
                        for t in range(NT):
                            mm = nc.tensor.matmul(PS[:, 0, NE * t:NE * t + NE], XN[:, t * P:(t + 1) * P], GW,
                                                  start=True, stop=True)
                        mm.then_inc(lg_ps.sem, 1)

                    @block.scalar
                    def _(act):
                        nc.scalar.activation(XTd[:, bass.ds(b * S, S)], XN[:, :], ACT.Copy)
                        act.wait_ge(le_in.sem, le_in.take())
                        nc.scalar.activation(LE, LG, ACT.Exp).then_inc(lx_in.sem, 1)
                        le_in.settle(act)

                    @block.vector
                    def _(dve):
                        pl = PS[:, 0, 0:NT * NE].rearrange("p (t e) -> p t e", e=NE)

                        def per_token(col):
                            return col.unsqueeze(2).to_broadcast([P, NT, NE])
                        dve.wait_ge(lg_ps.sem, lg_ps.take())
                        nc.vector.tensor_reduce(ms[:, :], pl, AX.X, ALU.max).then_inc(lg_in.sem, 1)
                        dve.wait_ge(lg_in.sem, lg_in.take())
                        nc.vector.tensor_tensor(LG, pl, per_token(ms[:, :]), ALU.subtract)\
                            .then_inc(le_in.sem, 1)
                        dve.wait_ge(lx_in.sem, lx_in.take())
                        nc.vector.tensor_reduce(ve[:, :], LE, AX.X, ALU.add).then_inc(lg_in.sem, 1)
                        dve.wait_ge(lg_in.sem, lg_in.take())
                        nc.vector.reciprocal(rstd[:, :], ve[:, :]).then_inc(lg_in.sem, 1)
                        dve.wait_ge(lg_in.sem, lg_in.take())
                        nc.vector.tensor_tensor(AF[:, :, bass.ds(b * NE, NE)], LE, per_token(rstd[:, :]),
                                                ALU.mult)
                        for f in (lg_ps, lg_in, lx_in):
                            f.settle(dve)
            with nc.Block() as block:
                @block.tensor
                def _(pe):
                    for t in range(NT):
                        tr = nc.tensor.transpose(PS[0:B * NE, t // 4, (t % 4) * P:(t % 4 + 1) * P],
                                                 AF[:, t, :], ident[:, :])
                    tr.then_inc(at_ps.sem, 1)
                    pe.wait_ge(gg_in.sem, gg_in.take())
                    for t in range(NT):
                        tr = nc.tensor.transpose(PS[:, 2, B * NE * t:B * NE * (t + 1)],
                                                 GG[:, t * P:(t + 1) * P], ident[0:B * NE, 0:B * NE])
                    tr.then_inc(gt_ps.sem, 1)
                    gg_in.settle(pe)

                @block.vector
                def _(dve):
                    dve.wait_ge(at_ps.sem, at_ps.take())
                    nc.vector.tensor_copy(AT.rearrange("p (h s) -> p h s", h=2), PS[0:B * NE, 0:2, :])\
                        .then_inc(top_in.sem, 1)
                    dve.wait_ge(top_in.sem, top_in.take())
                    src = AT
                    for r in range(TOPK // 8):
                        nc.vector.max(top8[r % 2], src).then_inc(top_in.sem, 1)
                        dve.wait_ge(top_in.sem, top_in.take())
                        nc.vector.match_replace(WK[r % 2], top8[r % 2], src, -1.0)\
                            .then_inc(top_in.sem, 1)
                        dve.wait_ge(top_in.sem, top_in.take())
                        src = WK[r % 2]
                    nc.vector.scalar_tensor_tensor(GG, src, 0.0, AT, ALU.is_lt, ALU.mult)\
                        .then_inc(gg_in.sem, 1)
                    dve.wait_ge(gt_ps.sem, gt_ps.take())
                    nc.vector.tensor_copy(GT.rearrange("p t n -> p (t n)"), PS[:, 2, 0:NT * B * NE])
                    for f in (at_ps, top_in, gt_ps):
                        f.settle(dve)
            with nc.Fori(0, B) as b:
                with nc.Block() as block:
                    @block.scalar
                    def _(act):
                        nc.scalar.activation(XN[:, :], XTd[:, bass.ds(b * S, S)], ACT.Copy)

                    @block.vector
                    def _(dve):
                        nc.vector.tensor_copy(GB, GT[:, :, bass.ds(b * NE, NE)])
                        nc.vector.memset(YT[:, :], 0.0)
                with nc.Block() as block:
                    @block.tensor
                    def _(pe):
                        with pe.Fori(0, NE) as e:
                            def up(t):
                                if t > 1:
                                    pe.wait_ge(hd_in.sem, hd_in.peek(t - 1))
                                nc.tensor.matmul(PS[:, t % 2, :], XN[:, t * P:(t + 1) * P],
                                                 WGU[:, bass.ds(e * 2 * EI, 2 * EI)],
                                                 start=True, stop=True).then_inc(up_ps.sem, 1)
                            up(0)
                            for t in range(NT):
                                if t < NT - 1:
                                    up(t + 1)
                                pe.wait_ge(hd_in.sem, hd_in.peek(t + 1))
                                if t > 1:
                                    pe.wait_ge(ht_in.sem, ht_in.peek(t - 1))
                                for k in range(2):
                                    tr = nc.tensor.transpose(PS[:, 2 + t % 2, k * P:(k + 1) * P],
                                                             HD[:, t % 2, k * P:(k + 1) * P], ident[:, :])
                                tr.then_inc(ht_ps.sem, 1)
                                pe.wait_ge(ht_in.sem, ht_in.peek(t + 1))
                                if t > 1:
                                    pe.wait_ge(acc_in.sem, acc_in.peek(t - 1))
                                for k in range(2):
                                    mm = nc.tensor.matmul(PS[:, 4 + t % 2, 0:D],
                                                          HTD[:, t % 2, k * P:(k + 1) * P],
                                                          WD[:, bass.ds((e * 2 + k) * D, D)],
                                                          start=k == 0, stop=k == 1)
                                mm.then_inc(dn_ps.sem, 1)
                            for f in (hd_in, ht_in, acc_in):
                                pe.wait_ge(f.sem, f.take(NT))
                                f.settle(pe)

                    @block.scalar
                    def _(act):
                        with act.Fori(0, NE) as e:
                            for t in range(NT):
                                act.wait_ge(up_ps.sem, up_ps.take())
                                nc.scalar.activation(SGD[:, t % 2, :], PS[:, t % 2, 0:EI], ACT.Sigmoid)\
                                    .then_inc(sg_in.sem, 1)
                                if t >= 1:
                                    act.wait_ge(ht_ps.sem, ht_ps.take())
                                    nc.scalar.activation(HTD[:, (t - 1) % 2, :], PS[:, 2 + (t - 1) % 2, 0:EI],
                                                         ACT.Copy).then_inc(ht_in.sem, 1)
                            act.wait_ge(ht_ps.sem, ht_ps.take())
                            nc.scalar.activation(HTD[:, (NT - 1) % 2, :], PS[:, 2 + (NT - 1) % 2, 0:EI],
                                                 ACT.Copy).then_inc(ht_in.sem, 1)
                            up_ps.settle(act)
                            ht_ps.settle(act)

                    @block.vector
                    def _(dve):
                        with dve.Fori(0, NE) as e:
                            def accumulate(t):
                                dve.wait_ge(dn_ps.sem, dn_ps.take())
                                nc.vector.tensor_tensor(ACC[:, t, :], ACC[:, t, :], PS[:, 4 + t % 2, 0:D],
                                                        ALU.add).then_inc(acc_in.sem, 1)
                            for t in range(NT):
                                dve.wait_ge(sg_in.sem, sg_in.take())
                                nc.vector.tensor_tensor(GSD[t % 2], PS[:, t % 2, 0:EI], SGD[:, t % 2, :],
                                                        ALU.mult).then_inc(gs_in.sem, 1)
                                dve.wait_ge(gs_in.sem, gs_in.take())
                                nc.vector.scalar_tensor_tensor(
                                    HD[:, t % 2, :], PS[:, t % 2, EI:2 * EI],
                                    GB[:, t:t + 1, bass.ds(e, 1)].rearrange("p o n -> p (o n)"),
                                    GSD[t % 2], ALU.mult, ALU.mult).then_inc(hd_in.sem, 1)
                                if t >= 1:
                                    accumulate(t - 1)
                            accumulate(NT - 1)
                            for f in (sg_in, gs_in, dn_ps):
                                f.settle(dve)
                norm(tokens=lambda t: ACC[:, t, :], residual=x_batch(b))
        with nc.Block() as block:
            @block.sync
            def _(sp):
                sp.dma_start(out.rearrange("(t p) d -> p t d", p=P), X[:, :, :]).then_inc(s_out, 16)
                sp.wait_ge(s_out, 16)


def _rotary_tables():
    f = np.float32
    half = np.arange(0, DH, 2, dtype=f)
    inv_freq = (f(1.0) / f(10000.0) ** (half / f(DH))).astype(f)
    t = np.arange(S, dtype=f)
    freqs = t[:, None] * inv_freq[None, :]
    base = ((half + f(0.4 * DH)) / f(1.4 * DH)).astype(f)
    power = ((t - S // 2) / (WIN // 2)).astype(f)
    scale = (base[None, :].astype(np.float64) ** power[:, None]).astype(f)
    cos, sin = np.cos(freqs.astype(np.float64)), np.sin(freqs.astype(np.float64))
    tables = []
    for fn, sign in ((cos, 1.0), (sin, -1.0)):
        q = np.concatenate([sign * fn * scale * 8.0, fn * scale * 8.0], 1)
        k = np.concatenate([sign * fn / scale, fn / scale], 1)
        full = np.concatenate([q, q, k, k], 1).astype(f)
        tables.append(np.ascontiguousarray(full.reshape(NT, P, 256).transpose(1, 0, 2)))
    return tables


def _band_mask():
    i = np.arange(P)[:, None]
    j = np.arange(KW)[None, :] - WIN
    rest = (j <= i) & (j >= i - WIN)
    masks = [rest & (j >= 0), rest, rest]
    return np.stack([np.where(m, 0.0, NEG) for m in masks], 1).astype(np.float32)


def kernel(**inputs):
    import concourse.bacc as _bacc
    from concourse.bass_utils import run_bass_kernel_spmd as _run

    g = {k: np.asarray(v) for k, v in inputs.items()}
    cos, sin = _rotary_tables()

    def cols(*vs):
        return np.stack(vs, 1)

    def features(w, n):
        return np.ascontiguousarray(w.reshape(n, P, -1).transpose(1, 0, 2))

    wqkv = g["L0_ffn_Wqkv"].reshape(DEPTH, D, 3, PAIRS, P).transpose(0, 1, 3, 2, 4).reshape(DEPTH, D, -1)
    qs, ks = g["L0_ffn_q_scale"], g["L0_ffn_k_scale"]
    qks = np.concatenate([qs, qs, ks, ks], 1)
    swapped = qks.reshape(DEPTH, 4, 2, DH // 2)[:, :, ::-1].reshape(DEPTH, 256)
    b1 = np.zeros((DEPTH, P, 6), np.float32)
    w2 = np.zeros((DEPTH, P, 3, D), np.float32)
    for j, w in enumerate(FJ):
        b1[:, :w, j] = g["L0_ffn_b1"][:, j * P:j * P + w]
        b1[:, :w, 3 + j] = g["L0_ffn_b1"][:, FI + j * P:FI + j * P + w]
        w2[:, :w, j] = g["L0_ffn_W2"][:, j * P:j * P + w]
    pl = np.concatenate([g["L0_ffn_ln_g"][:, :, None], g["L0_ffn_ln_b"][:, :, None], b1,
                         g["L0_ffn_b2"][:, :, None]], 2)
    c_idx = np.arange(P)
    arrays = {
        "x": g["L0_attn_x"].reshape(B * S, D), "cos": cos, "sin": sin, "bandmask": _band_mask(),
        "w3": np.stack([g["L0_attn_Wg"], g["L0_attn_Wv"], g["L0_attn_Wd"]], 1),
        "wga": g["L0_attn_W_gate"], "wua": g["L0_attn_W_up"], "woa": features(g["L0_attn_W_out"], 3),
        "pa": cols(g["L0_attn_w_rms_mix"], g["L0_attn_w_rms_ffn"], g["L0_attn_bg"], g["L0_attn_bv"],
                   g["L0_attn_bd"]),
        "wqkv": wqkv, "wo": g["L0_ffn_Wo"].reshape(DEPTH, PAIRS, P, D).transpose(0, 2, 1, 3),
        "w1": g["L0_ffn_W1"], "w2": w2, "pl": pl,
        "qks": np.stack([qks, swapped], 1),
        "wc": np.concatenate([g["L1_attn_W_qkv"].T[:, 0:P], g["L1_attn_W_qkv"].T[:, 2 * P:],
                              g["L1_attn_W_qkv"].T[:, P:2 * P]], 1),
        "woc": g["L1_attn_W_out"].T,
        "headmask": (c_idx[:, None] // LC % 4 == np.arange(4)[None, :]).astype(np.float32),
        "blockdiag": (c_idx[:, None] // LC == c_idx[None, :] // LC).astype(np.float32),
        "causal": (c_idx[None, :] >= c_idx[:, None]).astype(np.float32),
        "gw": g["L1_ffn_gate_w"],
        "wgu": np.concatenate([g["L1_ffn_Wg"], g["L1_ffn_Wu"]], 2).transpose(1, 0, 2),
        "wd": g["L1_ffn_Wd"].reshape(NE, 2, P, D).transpose(2, 0, 1, 3),
    }
    arrays = {k: np.ascontiguousarray(v) for k, v in arrays.items()}
    nc = _bacc.Bacc("TRN2", target_bir_lowering=False, num_devices=1)
    aps = {k: nc.dram_tensor(f"in_{k}", v.shape, mybir.dt.from_np(v.dtype), kind="ExternalInput").ap()
           for k, v in arrays.items()}
    o = nc.dram_tensor("out_x", (B * S, D), F32, kind="ExternalOutput").ap()
    mixed_layers_kernel(nc, aps, o, STAGES)
    r = _run(nc, [{f"in_{k}": v for k, v in arrays.items()}], core_ids=[0])
    return r.results[0]["out_x"].reshape(B, S, D)
```

```python
import concourse.bass as bass
import numpy as np
from concourse import mybir
from contextlib import ExitStack

F32 = mybir.dt.float32
BF16 = mybir.dt.bfloat16
ALU = mybir.AluOpType
ACT = mybir.ActivationFunctionType
AX = mybir.AxisListType

P = 128
B, S, D = 2, 1024, 128
NT = S // P
HALF = 512
NH = S // HALF
DEPTH, HEADS, DH, WIN = 6, 16, 64, 32
PAIRS = HEADS // 2
CH = 4
CB = NT // CH
KW = WIN + P
FA = 384
FI = 341
FJ = [128, 128, FI - 256]
NE, EI, TOPK = 8, 256, 128
LH, LC = 16, 8
NEG = -2.0 ** 100
STAGES = "ABCD"
LAYERS = 6


class Flow:

    def __init__(self, ctx, nc, name):
        self.sem = ctx.enter_context(nc.semaphore(name))
        self.used = 0

    def take(self, n=1):
        self.used += n
        return self.used

    def peek(self, n):
        return self.used + n

    def settle(self, eng):
        if self.used:
            eng.sem_inc(self.sem, -self.used)
        self.used = 0


def mixed_layers_kernel(nc, a, out, stages):
    ctx = ExitStack()
    with ctx:
        def sb(name, shape, dt=F32):
            return ctx.enter_context(nc.sbuf_tensor(name, shape, dt))

        def flow(name):
            return Flow(ctx, nc, name)

        X = sb("X", [P, B * NT, D])
        XT = sb("XT", [P, B, S])
        XN = sb("XN", [P, S])
        YT = sb("YT", [P, S])
        NTOK = sb("NTOK", [P, NT, D])
        XS = sb("XS", [P, S])
        ident = sb("ident", [P, P])
        identb = sb("identb", [P, P], BF16)
        bandmask = sb("bandmask", [P, 3, KW], BF16)
        minus_half = sb("minus_half", [P, 8])
        eps_tile = sb("eps_tile", [P, 4])
        bn = sb("bn", [P, NT, 6])
        mv = sb("mv", [P, NT, 2])
        ms = sb("ms", [P, NT])
        ve = sb("ve", [P, NT])
        rstd = sb("rstd", [P, NT])
        WQ = sb("WQ", [P, 2, PAIRS * 384])
        WO = sb("WO", [P, PAIRS, D])
        W1 = sb("W1", [P, 2 * FI])
        W2 = sb("W2", [P, 3, D])
        PL = sb("PL", [P, 9])
        QKS = sb("QKS", [P, 2, 256])
        COS0 = sb("COS0", [P, NT, 256])
        SIN0 = sb("SIN0", [P, NT, 256])
        COSL = sb("COSL", [P, NT, 256])
        SINL = sb("SINL", [P, NT, 256])
        QKT = sb("QKT", [P, 2, WIN + S])
        V = sb("V", [P, CH, CB, 2, DH + 1])
        VP = sb("VP", [WIN, CH, CB, 2, DH + 1])
        SQ = sb("SQ", [P, 2, 8, DH])
        N2 = sb("N2", [P, 8])
        N2G = sb("N2G", [P, 8])
        RN = sb("RN", [P, 8])
        R1 = sb("R1", [P, CB, 256])
        R2 = sb("R2", [P, CB, 256])
        RR = sb("RR", [P, CB, 256])
        QK = sb("QK", [P, 2, CB, 2, P])
        NMX = sb("NMX", [P, 4])
        PR = sb("PR", [P, 2, 4, KW])
        PTS = sb("PTS", [P, 4, P])
        PPS = sb("PPS", [WIN, 4, WIN])
        RO = sb("RO", [P, 4])
        ON = sb("ON", [P, CB, P])
        RKB = sb("RKB", [B * NE, S], BF16)
        BIG = sb("BIG", [P, PAIRS * S])
        OTS = BIG[:, :].rearrange("p (h s) -> p h s", h=PAIRS)

        PS = ctx.enter_context(nc.psum_tensor("PS", [P, 8, HALF], F32))

        s_in, s_w, s_wq, s_out = (ctx.enter_context(nc.semaphore(n)) for n in
                                  ("inputs_in", "layer_in", "first_wqkv_in", "out_written"))

        def bank_tiles(bank, t):
            return PS[:, bank + t // 4, (t % 4) * P:(t % 4 + 1) * P]

        made = flow("constants_made")
        bandmask_f32 = BIG[:, 0:3 * KW].rearrange("p (m k) -> p m k", m=3)
        with nc.Block() as block:
            @block.sync
            def _(sp):
                sp.dma_start(X[:, :, :], a["x"].rearrange("(t p) d -> p t d", p=P)).then_inc(s_in, 16)
                sp.dma_start(COS0[:, :, :], a["cos"]).then_inc(s_in, 16)
                sp.dma_start(SIN0[:, :, :], a["sin"]).then_inc(s_in, 16)
                sp.dma_start(bandmask_f32, a["bandmask"]).then_inc(s_in, 16)
                sp.dma_start(WQ[:, 0, :], a["wqkv"][0, :, :]).then_inc(s_wq, 16)
                sp.wait_ge(s_in, 64)
                sp.wait_ge(s_wq, 16)

            @block.scalar
            def _(act):
                act.wait_ge(s_in, 64)
                nc.scalar.activation(bandmask[:, :, :], bandmask_f32, ACT.Copy)

            @block.gpsimd
            def _(pool):
                pool.memset(ident[:, :], 0.0).then_inc(made.sem, 1)
                pool.memset(identb[:, :], 0.0).then_inc(made.sem, 1)
                pool.memset(minus_half[:, :], -0.5)
                pool.memset(V[:, :, :, :, DH:DH + 1], 1.0)
                pool.memset(VP[:, :, :, :, DH:DH + 1], 1.0)
                pool.memset(QKT[:, 1, 0:WIN], 0.0)
                pool.wait_ge(made.sem, made.take(2))
                for m in (ident, identb):
                    pool.affine_select(out=m[:, :], in_=m[:, :], compare_op=ALU.not_equal, fill=1.0,
                                       base=0, pattern=[[-1, P]], channel_multiplier=1)
                made.settle(pool)

        to_tokens = flow("tile_transposed_to_tokens")
        stats_in = flow("bn_stats_done")
        aggr_in = flow("mean_var_done")
        var_in = flow("variance_ready")
        rstd_in = flow("rstd_ready")
        ntok_in = flow("normalised_tile_ready")
        nfeat_in = flow("normalised_half_in_psum")
        res_in = flow("normalised_tile_for_residual")

        def norm(tokens=None, features=None, rms=False, eps=1e-5, dst=None, scale=None, bias=None,
                 residual=None):
            src = tokens if tokens is not None else (lambda t: bank_tiles(0, t))
            with nc.Block() as block:
                @block.tensor
                def _(pe):
                    if features is not None:
                        for t in range(NT):
                            tr = nc.tensor.transpose(bank_tiles(0, t), features[:, t * P:(t + 1) * P],
                                                     ident[:, :])
                            if t % 4 == 3:
                                tr.then_inc(to_tokens.sem, 1)
                    if dst is not None:
                        for t in range(NT):
                            pe.wait_ge(ntok_in.sem, ntok_in.take())
                            tr = nc.tensor.transpose(bank_tiles(2, t), NTOK[:, t, :], ident[:, :])
                            if t % 4 == 3:
                                tr.then_inc(nfeat_in.sem, 1)
                    ntok_in.settle(pe)

                @block.vector
                def _(dve):
                    for t in range(NT):
                        if features is not None and t % 4 == 0:
                            dve.wait_ge(to_tokens.sem, to_tokens.take())
                        nc.vector.bn_stats(bn[:, t, :], src(t)).then_inc(stats_in.sem, 1)
                    for t in range(NT):
                        dve.wait_ge(stats_in.sem, stats_in.take())
                        nc.vector.bn_aggr(mv[:, t, :], bn[:, t, :]).then_inc(aggr_in.sem, 1)
                    dve.wait_ge(aggr_in.sem, aggr_in.take(NT))
                    if rms:
                        nc.vector.tensor_tensor(ms[:, :], mv[:, :, 0], mv[:, :, 0], ALU.mult)\
                            .then_inc(aggr_in.sem, 1)
                        dve.wait_ge(aggr_in.sem, aggr_in.take())
                        nc.vector.scalar_tensor_tensor(ve[:, :], ms[:, :], eps, mv[:, :, 1],
                                                       ALU.add, ALU.add).then_inc(var_in.sem, 1)
                    else:
                        nc.vector.tensor_scalar(ve[:, :], mv[:, :, 1], eps, None, ALU.add)\
                            .then_inc(var_in.sem, 1)
                    dve.wait_ge(rstd_in.sem, rstd_in.take())
                    for t in range(NT):
                        done = ntok_in if dst is not None else res_in
                        if rms:
                            nc.vector.tensor_scalar(NTOK[:, t, :], src(t), rstd[:, t:t + 1], None,
                                                    ALU.mult).then_inc(done.sem, 1)
                        else:
                            nc.vector.tensor_scalar(NTOK[:, t, :], src(t), mv[:, t, 0:1],
                                                    rstd[:, t:t + 1], ALU.subtract, ALU.mult)\
                                .then_inc(done.sem, 1)
                    if residual is not None:
                        dve.wait_ge(res_in.sem, res_in.take(NT))
                        nc.vector.tensor_tensor(residual, residual, NTOK[:, :, :], ALU.add)
                    for f in (to_tokens, stats_in, aggr_in, rstd_in, res_in):
                        f.settle(dve)

                @block.gpsimd
                def _(pool):
                    pool.wait_ge(var_in.sem, var_in.take())
                    nc.gpsimd.tensor_tensor(rstd[:, :], ve[:, :], minus_half[:, 0:NT], ALU.pow)\
                        .then_inc(rstd_in.sem, 1)
                    var_in.settle(pool)

                @block.scalar
                def _(act):
                    if dst is not None:
                        for h in range(NH):
                            act.wait_ge(nfeat_in.sem, nfeat_in.take())
                            nc.scalar.activation(dst[:, h * HALF:(h + 1) * HALF], PS[:, 2 + h, :],
                                                 ACT.Identity if bias is not None else ACT.Copy,
                                                 scale=1.0 if scale is None else scale,
                                                 bias=0.0 if bias is None else bias)
                    nfeat_in.settle(act)

        def x_tiles(b):
            return lambda t: X[:, bass.ds(b * NT + t, 1), :].rearrange("p o d -> p (o d)")

        def x_batch(b):
            return X[:, bass.ds(b * NT, NT), :]

        if "A" in stages:
            W3 = BIG[:, 0:3 * D].rearrange("p (k n) -> p k n", k=3)
            WGA = BIG[:, 384:384 + FA]
            WUA = BIG[:, 768:768 + FA]
            WOA = BIG[:, 1152:1152 + FA].rearrange("p (j n) -> p j n", j=3)
            PA = BIG[:, 1536:1541]
            SIG = BIG[:, 2048:2048 + S]
            TAN = BIG[:, 3072:3072 + S]
            SCA = BIG[:, 4096:4096 + S]
            SCX = BIG[:, 5120:5120 + S]
            X1 = BIG[:, 6144:6144 + S]
            HT = BIG[:, 2048:2048 + 3 * S].rearrange("p (j n) -> p j n", j=3)
            SGA = SQ[:, :, :, :].rearrange("p k a b -> p k (a b)")
            GSA = [r[:, :, :].rearrange("p a b -> p (a b)") for r in (R1, R2)]
            gates_in = flow("gates_in_psum")
            ups_in = flow("ups_in_psum")
            ffn_in = flow("ffn_in_psum")
            gates_act = flow("gates_activated")
            scan_in = flow("scan_operands_ready")
            silu_in = flow("gate_times_sigmoid_ready")
            hidden_in = flow("hidden_ready")
            with nc.Block() as block:
                @block.sync
                def _(sp):
                    sp.dma_start(W3, a["w3"]).then_inc(s_in, 16)
                    sp.dma_start(WGA, a["wga"]).then_inc(s_in, 16)
                    sp.dma_start(WUA, a["wua"]).then_inc(s_in, 16)
                    sp.dma_start(WOA, a["woa"]).then_inc(s_in, 16)
                    sp.dma_start(PA, a["pa"]).then_inc(s_in, 16)
                    sp.wait_ge(s_in, 64 + 80)
            with nc.Fori(0, B) as b:
                norm(tokens=x_tiles(b), dst=XS[:, :])
                norm(features=XS, rms=True, eps=1e-6, dst=XN[:, :], scale=PA[:, 0:1])
                with nc.Block() as block:
                    @block.tensor
                    def _(pe):
                        for h in range(NH):
                            for k in range(3):
                                nc.tensor.matmul(PS[:, 3 * h + k, :], W3[:, k, :],
                                                 XN[:, h * HALF:(h + 1) * HALF],
                                                 start=True, stop=True).then_inc(gates_in.sem, 1)

                    @block.scalar
                    def _(act):
                        for h in range(NH):
                            cols = slice(h * HALF, (h + 1) * HALF)
                            for k, (f, dst) in enumerate(((ACT.Sigmoid, SIG), (ACT.Tanh, TAN),
                                                          (ACT.Sigmoid, SCA))):
                                act.wait_ge(gates_in.sem, gates_in.take())
                                nc.scalar.activation(dst[:, cols], PS[:, 3 * h + k, :], f,
                                                     bias=PA[:, 2 + k:3 + k]).then_inc(gates_act.sem, 1)
                        gates_in.settle(act)

                    @block.vector
                    def _(dve):
                        for h in range(NH):
                            cols = slice(h * HALF, (h + 1) * HALF)
                            dve.wait_ge(gates_act.sem, gates_act.take(2))
                            nc.vector.tensor_tensor(SCX[:, cols], SIG[:, cols], TAN[:, cols], ALU.mult)\
                                .then_inc(scan_in.sem, 1)
                            dve.wait_ge(gates_act.sem, gates_act.take())
                            nc.vector.tensor_scalar(SCA[:, cols], SCA[:, cols], 0.998, 0.001,
                                                    ALU.mult, ALU.add).then_inc(scan_in.sem, 1)
                        dve.wait_ge(scan_in.sem, scan_in.take(4))
                        nc.vector.tensor_tensor_scan(YT[:, :], SCA, SCX, 0.0, ALU.mult, ALU.add)\
                            .then_inc(scan_in.sem, 1)
                        dve.wait_ge(scan_in.sem, scan_in.take())
                        nc.vector.tensor_tensor(X1, YT[:, :], XS[:, :], ALU.add)
                        gates_act.settle(dve)
                        scan_in.settle(dve)
                norm(features=X1, rms=True, eps=1e-6, dst=XN[:, :], scale=PA[:, 1:2])
                with nc.Block() as block:
                    @block.tensor
                    def _(pe):
                        for h in range(NH):
                            cols = slice(h * HALF, (h + 1) * HALF)
                            for j in range(3):
                                i = 3 * h + j
                                if i >= 2:
                                    pe.wait_ge(hidden_in.sem, hidden_in.peek(i - 1))
                                nc.tensor.matmul(PS[:, 2 * (i % 2), :], WGA[:, j * P:(j + 1) * P],
                                                 XN[:, cols], start=True, stop=True)\
                                    .then_inc(gates_in.sem, 1)
                                nc.tensor.matmul(PS[:, 2 * (i % 2) + 1, :], WUA[:, j * P:(j + 1) * P],
                                                 XN[:, cols], start=True, stop=True)\
                                    .then_inc(ups_in.sem, 1)
                        for h in range(NH):
                            pe.wait_ge(hidden_in.sem, hidden_in.take(3))
                            for j in range(3):
                                mm = nc.tensor.matmul(PS[:, 4 + h, :], WOA[:, j, :],
                                                      HT[:, j, h * HALF:(h + 1) * HALF],
                                                      start=j == 0, stop=j == 2)
                            mm.then_inc(ffn_in.sem, 1)
                        hidden_in.settle(pe)

                    @block.scalar
                    def _(act):
                        for i in range(3 * NH):
                            act.wait_ge(gates_in.sem, gates_in.take())
                            nc.scalar.activation(SGA[:, i % 2, :], PS[:, 2 * (i % 2), :], ACT.Sigmoid)\
                                .then_inc(gates_act.sem, 1)
                        gates_in.settle(act)

                    @block.vector
                    def _(dve):
                        for i in range(3 * NH):
                            h, j = i // 3, i % 3
                            dve.wait_ge(gates_act.sem, gates_act.take())
                            nc.vector.tensor_tensor(GSA[i % 2], PS[:, 2 * (i % 2), :], SGA[:, i % 2, :],
                                                    ALU.mult).then_inc(silu_in.sem, 1)
                            dve.wait_ge(ups_in.sem, ups_in.take())
                            dve.wait_ge(silu_in.sem, silu_in.take())
                            nc.vector.tensor_tensor(HT[:, j, h * HALF:(h + 1) * HALF], GSA[i % 2],
                                                    PS[:, 2 * (i % 2) + 1, :], ALU.mult)\
                                .then_inc(hidden_in.sem, 1)
                        for h in range(NH):
                            dve.wait_ge(ffn_in.sem, ffn_in.take())
                            nc.vector.tensor_tensor(YT[:, h * HALF:(h + 1) * HALF], PS[:, 4 + h, :],
                                                    X1[:, h * HALF:(h + 1) * HALF], ALU.add)
                        for f in (gates_act, silu_in, ups_in, ffn_in):
                            f.settle(dve)
                norm(features=YT, residual=x_batch(b))

        if "B" in stages:
            XTf = XT[:, :, :].rearrange("p b s -> p (b s)")
            WQf = WQ[:, :, :].rearrange("p k n -> p (k n)")
            BIGf = BIG[:, :]
            Vb = V[:, :, :, :, :].rearrange("p c j h d -> p (c j) (h d)")
            VPb = VP[:, :, :, :, :].rearrange("p c j h d -> p (c j) (h d)")
            COSLb, SINLb = COSL[:, :, :], SINL[:, :, :]
            SQv = SQ[:, :, :, :].rearrange("p k (j g) d -> p k j (g d)", j=CB)
            R2s = R2[:, :, :].rearrange("p j (g v d) -> p j g v d", v=2, d=DH // 2)
            SINs = SINL[:, :, :].rearrange("p t (g v d) -> p t g v d", v=2, d=DH // 2)
            RRg = RR[:, :, :].rearrange("p j (g d) -> p (j g) d", d=DH)
            QKg = [QK[:, k, :, :, :].rearrange("p j k (h d) -> p (j k h) d", d=DH) for k in range(2)]
            PQ, TQ, SC, PT, PO, OT = PS[:, 0:2, :], PS[:, 2, :], PS[:, 3:5, :], PS[:, 5, :], PS[:, 6, :], PS[:, 7, :]
            POu = PS[:, 6, 0:4 * (DH + 1)].rearrange("p (u d) -> p u d", d=DH + 1)
            wq_in = flow("next_wqkv_in")
            layer_in = flow("layer_weights_in")
            proj_in = flow("qkv_in_psum")
            rot_in = flow("rotation_products_ready")
            sq_in = flow("squares_ready")
            pq_free = flow("qkv_banks_read")
            n2_in = flow("square_norms_ready")
            n2g_in = flow("square_norms_guarded")
            rr_in = flow("rotated_and_rnorm_ready")
            qk_in = flow("rotated_scaled_ready")
            qkt_ps = flow("qk_transposed_in_psum")
            qkt_in = flow("qk_feature_major_ready")
            sc_in = flow("head_scores_in_psum")
            nmx_in = flow("head_max_ready")
            p_in = flow("probabilities_ready")
            p_tail = flow("probabilities_complete")
            pt_ps = flow("probabilities_transposed_in_psum")
            pts_in = flow("probabilities_transposed")
            pps_in = flow("previous_window_transposed")
            o_ps = flow("attention_out_in_psum")
            ro_in = flow("softmax_sums_inverted")
            on_in = flow("attention_out_normalised")
            ot_ps = flow("attention_out_transposed")
            x_in = flow("attention_residual_added")
            x_in_dve = flow("attention_residual_written")
            shift_in = flow("shifted_half_ready")
            xn_in = flow("normalised_half_ready")
            ot_free = flow("transposed_out_copied")
            wo_in = flow("projected_half_in_psum")
            table_in = flow("cos_table_ready")
            gelu_free = flow("gate_tile_used")

            for b in range(B):
                norm(tokens=x_tiles(b), dst=XT[:, b, :])
            with nc.Block() as block:
                @block.vector
                def _(dve):
                    for shifted in (XS, YT):
                        nc.vector.memset(shifted[D // 2:P, 0:1], 0.0)

            def shift_tokens(b):
                with nc.Block() as block:
                    @block.vector
                    def _(dve):
                        nc.vector.tensor_copy(XS[0:D // 2, :], XTf[0:D // 2, bass.ds(b * S, S)])

                    @block.scalar
                    def _(act):
                        nc.scalar.activation(XS[D // 2:P, 1:S], XTf[D // 2:P, bass.ds(b * S, S - 1)],
                                             ACT.Copy)

            N = PAIRS * CH

            def run(eng, step, flows):
                def settle():
                    for f in flows:
                        f.settle(eng)
                for n in range(-3, 2):
                    step(n, 0)
                settle()
                with eng.Fori(0, PAIRS - 2) as i:
                    for n in range(2, 2 + CH):
                        step(n, i)
                    settle()
                for n in range(N + 2 - 2 * CH, N + 2):
                    step(n, 0)
                return settle

            def attention(l, b):
                par = (l % 2) * (PAIRS * 384)

                with nc.Block() as block:
                    @block.tensor
                    def _(pe):
                        def step(n, i):
                            if 0 <= n - 1 < N:
                                pe.wait_ge(p_in.sem, p_in.take(4))
                                for u in range(4):
                                    tr = nc.tensor.transpose(PT[:, u * P:(u + 1) * P],
                                                             PR[:, (n - 1) % 2, u, WIN:KW], ident[:, :])
                                    if u == 0:
                                        tr.then_inc(p_tail.sem, 1)
                                tr.then_inc(pt_ps.sem, 1)
                            if 0 <= n < N:
                                c = n % CH
                                pe.wait_ge(qkt_in.sem, qkt_in.take())
                                for h in range(2):
                                    rows = slice(DH * h, DH * h + DH)
                                    first = 0 if c == 0 else 1
                                    nc.tensor.matmul(
                                        SC[:, h, 0:CB * KW], identb[:, :],
                                        bandmask[:, first:first + CB, :].rearrange("p j k -> p (j k)"),
                                        start=True, stop=False)
                                    for j in range(CB):
                                        t0 = (CB * c + j) * P
                                        mm = nc.tensor.matmul(SC[:, h, j * KW:(j + 1) * KW],
                                                              QKT[rows, 0, WIN + t0:WIN + t0 + P],
                                                              QKT[rows, 1, t0:t0 + KW],
                                                              start=False, stop=j == CB - 1)
                                    mm.then_inc(sc_in.sem, 1)
                            if 0 <= n - 2 < N:
                                pe.wait_ge(on_in.sem, on_in.take())
                                if n - 1 < N:
                                    pe.wait_ge(pts_in.sem, pts_in.take())
                                else:
                                    pe.wait_ge(ot_free.sem, ot_free.take())
                                for j in range(CB):
                                    tr = nc.tensor.transpose(OT[:, j * P:(j + 1) * P], ON[:, j, :],
                                                             ident[:, :])
                                tr.then_inc(ot_ps.sem, 1)
                            if 0 <= n - 1 < N:
                                c = (n - 1) % CH
                                if n - 2 < 0:
                                    pe.wait_ge(pts_in.sem, pts_in.take())
                                for j in range(CB):
                                    for h in range(2):
                                        u, o = 2 * h + j, 2 * j + h
                                        mm = nc.tensor.matmul(POu[:, o, :], PTS[:, u, :], V[:, c, j, h, :],
                                                              start=o == 0, stop=o == 3,
                                                              skip_group_check=True)
                                pe.wait_ge(pps_in.sem, pps_in.take())
                                for j in range(CB):
                                    for h in range(2):
                                        u, o = 2 * h + j, 2 * j + h
                                        if c > 0 or j > 0:
                                            mm = nc.tensor.matmul(POu[0:WIN, o, :], PPS[:, u, :],
                                                                  VP[:, c, j, h, :], start=False,
                                                                  stop=True, skip_group_check=True)
                                mm.then_inc(o_ps.sem, 1)
                            if 0 <= n + 1 < N:
                                pe.wait_ge(qk_in.sem, qk_in.take())
                                for k in range(2):
                                    for j in range(CB):
                                        tr = nc.tensor.transpose(TQ[:, (2 * k + j) * P:(2 * k + j + 1) * P],
                                                                 QK[:, (n + 1) % 2, j, k, :], ident[:, :])
                                tr.then_inc(qkt_ps.sem, 1)
                            if 0 <= n + 3 < N:
                                c = (n + 3) % CH
                                if n + 3 > 0:
                                    pe.wait_ge(pq_free.sem, pq_free.take())
                                w0 = par + ((n + 3) // CH + i) * 384
                                for j in range(CB):
                                    t0 = (CB * c + j) * P
                                    mm = nc.tensor.matmul(PQ[:, j, 0:384], XS[:, t0:t0 + P],
                                                          WQf[:, bass.ds(w0, 384)], start=True, stop=True)
                                mm.then_inc(proj_in.sem, 1)
                        settle = run(pe, step, [ot_free, qkt_in, p_in, on_in, pq_free, pts_in, pps_in, qk_in])
                        pe.wait_ge(pq_free.sem, pq_free.take())
                        settle()

                    @block.scalar
                    def _(act):
                        PQv = PQ[:, :, 256:384].rearrange("p j (h d) -> p j h d", h=2)

                        def step(n, i):
                            if 0 <= n - 1 < N:
                                act.wait_ge(pt_ps.sem, pt_ps.take())
                                nc.scalar.activation(PTS[:, :, :].rearrange("p u k -> p (u k)"), PT,
                                                     ACT.Copy).then_inc(pts_in.sem, 1)
                            if 0 <= n + 1 < N:
                                c = (n + 1) % CH
                                lo = 0 if c else 1
                                nc.scalar.activation(VPb[:, CB * c + lo:CB * c + CB, :],
                                                     Vb[P - WIN:P, CB * c + lo - 1:CB * c + CB - 1, :],
                                                     ACT.Copy)
                            if 0 <= n < N:
                                for h in range(2):
                                    act.wait_ge(nmx_in.sem, nmx_in.take())
                                    for j in range(CB):
                                        u = 2 * h + j
                                        nc.scalar.activation(PR[:, n % 2, u, :],
                                                             SC[:, h, j * KW:(j + 1) * KW], ACT.Exp,
                                                             bias=NMX[:, u:u + 1]).then_inc(p_in.sem, 1)
                            if 0 <= n + 1 < N:
                                c = (n + 1) % CH
                                act.wait_ge(qkt_ps.sem, qkt_ps.take())
                                nc.scalar.activation(
                                    QKT[:, :, WIN + c * CB * P:WIN + (c + 1) * CB * P],
                                    TQ.rearrange("p (k s) -> p k s", k=2), ACT.Copy).then_inc(qkt_in.sem, 1)
                            if 0 <= n + 3 < N:
                                c = (n + 3) % CH
                                act.wait_ge(proj_in.sem, proj_in.take())
                                nc.scalar.activation(SQv[:, (n + 3) % 2, :, :], PQ[:, :, 0:256], ACT.Square)
                                nc.scalar.activation(V[:, c, :, :, 0:DH], PQv, ACT.Copy)\
                                    .then_inc(sq_in.sem, 1)
                            if 0 <= n - 2 < N:
                                c = (n - 2) % CH
                                act.wait_ge(ot_ps.sem, ot_ps.take())
                                cp = nc.scalar.activation(
                                    BIGf[:, bass.ds(((n - 2) // CH + i) * S + c * CB * P, CB * P)],
                                    OT[:, 0:CB * P], ACT.Copy)
                                if n == N:
                                    cp.then_inc(ot_free.sem, 1)
                        run(act, step, [nmx_in, ot_ps, pt_ps, proj_in, qkt_ps])()

                    @block.vector
                    def _(dve):
                        def step(n, i):
                            if 0 <= n - 1 < N:
                                dve.wait_ge(p_tail.sem, p_tail.take())
                                nc.vector.transpose(PPS[:, :, :], PR[0:WIN, (n - 1) % 2, :, 0:WIN])\
                                    .then_inc(pps_in.sem, 1)
                            if 0 <= n + 1 < N:
                                dve.wait_ge(rr_in.sem, rr_in.take())
                                nc.vector.tensor_tensor(QKg[(n + 1) % 2], RRg, RN[:, :].unsqueeze(2)
                                                        .to_broadcast([P, 8, DH]), ALU.mult)\
                                    .then_inc(qk_in.sem, 1)
                            if 0 <= n + 2 < N:
                                c = (n + 2) % CH
                                t = slice(CB * c, CB * c + CB)
                                qk5 = PQ[:, :, 0:256].rearrange("p j (g v d) -> p j g v d", v=2, d=DH // 2)
                                dve.wait_ge(sq_in.sem, sq_in.take())
                                nc.vector.tensor_reduce(N2[:, :], SQ[:, n % 2, :, :], AX.X, ALU.add)\
                                    .then_inc(n2_in.sem, 1)
                                nc.vector.tensor_tensor(R1[:, :, :], PQ[:, :, 0:256], COSLb[:, t, :],
                                                        ALU.mult)
                                for v in range(2):
                                    rot = nc.vector.tensor_tensor(R2s[:, :, :, v, :], qk5[:, :, :, 1 - v, :],
                                                                  SINs[:, t, :, v, :], ALU.mult)
                                rot.then_inc(rot_in.sem, 1)
                            if 0 <= n < N:
                                for h in range(2):
                                    dve.wait_ge(sc_in.sem, sc_in.take())
                                    nc.vector.tensor_reduce(
                                        NMX[:, 2 * h:2 * h + 2],
                                        SC[:, h, 0:CB * KW].rearrange("p (j k) -> p j k", k=KW),
                                        AX.X, ALU.max, negate=True).then_inc(nmx_in.sem, 1)
                            if 0 <= n - 1 < N:
                                dve.wait_ge(o_ps.sem, o_ps.take())
                                nc.vector.reciprocal(RO[:, :], POu[:, :, DH]).then_inc(ro_in.sem, 1)
                                dve.wait_ge(ro_in.sem, ro_in.take())
                                nc.vector.tensor_tensor(
                                    ON[:, :, :].rearrange("p j (h d) -> p (j h) d", h=2), POu[:, :, 0:DH],
                                    RO[:, :].unsqueeze(2).to_broadcast([P, 4, DH]), ALU.mult)\
                                    .then_inc(on_in.sem, 1)
                        run(dve, step, [sc_in, p_tail, rr_in, sq_in, o_ps, ro_in])()

                    @block.gpsimd
                    def _(pool):
                        def step(n, i):
                            if 0 <= n + 2 < N:
                                pool.wait_ge(n2_in.sem, n2_in.take())
                                nc.gpsimd.tensor_scalar(N2G[:, :], N2[:, :], 1e-24, None, ALU.max)\
                                    .then_inc(n2g_in.sem, 1)
                                pool.wait_ge(n2g_in.sem, n2g_in.take())
                                nc.gpsimd.tensor_tensor(RN[:, :], N2G[:, :], minus_half[:, :], ALU.pow)
                                pool.wait_ge(rot_in.sem, rot_in.take())
                                pool.sem_inc(pq_free.sem, 1)
                                nc.gpsimd.tensor_tensor(RR[:, :, :], R1[:, :, :], R2[:, :, :], ALU.add)\
                                    .then_inc(rr_in.sem, 1)
                        run(pool, step, [n2_in, n2g_in, rot_in])()

            GL = [BIG[:, k * HALF:(k + 1) * HALF] for k in range(2)]
            HB = BIG[:, 2 * HALF:2 * HALF + 3 * S].rearrange("p (j s) -> p j s", j=3)
            GU = [PS[:, 6:8, :], PS[:, 0:2, :]]

            def feed_forward(b):
                with nc.Block() as block:
                    def tokens_of(h):
                        return [(t, PS[:, 2 + h, (t % 4) * P:(t % 4 + 1) * P])
                                for t in range(4 * h, 4 * h + 4)]

                    @block.tensor
                    def _(pe):
                        def project(h, heads):
                            for hp in heads:
                                mm = nc.tensor.matmul(PS[:, h, :], WO[:, hp, :],
                                                      OTS[:, hp, h * HALF:(h + 1) * HALF],
                                                      start=hp == 0, stop=hp == PAIRS - 1)
                            if hp == PAIRS - 1:
                                mm.then_inc(wo_in.sem, 1)

                        def to_token_major(h):
                            pe.wait_ge(shift_in.sem, shift_in.take(2))
                            for t, tile in tokens_of(h):
                                tr = nc.tensor.transpose(tile, YT[:, t * P:(t + 1) * P], ident[:, :])
                            tr.then_inc(to_tokens.sem, 1)

                        def to_feature_major(h):
                            for t in range(4):
                                pe.wait_ge(ntok_in.sem, ntok_in.take())
                                tr = nc.tensor.transpose(PS[:, 4 + h, t * P:(t + 1) * P],
                                                         NTOK[:, 4 * h + t, :], ident[:, :])
                            tr.then_inc(nfeat_in.sem, 1)

                        def gate_and_up(i):
                            h, j = i // 3, i % 3
                            cols, w = slice(h * HALF, (h + 1) * HALF), FJ[j]
                            if j == 0:
                                pe.wait_ge(xn_in.sem, xn_in.take())
                            if i >= 2:
                                used = i - 1 if i < 4 else i - 4
                                pe.wait_ge(gelu_free.sem, gelu_free.peek(used))
                            nc.tensor.matmul(GU[i % 2][0:w, 0, :], W1[:, FI + j * P:FI + j * P + w],
                                             XN[:, cols], start=True, stop=True).then_inc(proj_in.sem, 1)
                            nc.tensor.matmul(GU[i % 2][0:w, 1, :], W1[:, j * P:j * P + w],
                                             XN[:, cols], start=True, stop=True).then_inc(sc_in.sem, 1)

                        def down(h):
                            pe.wait_ge(gelu_free.sem, gelu_free.take(3))
                            for j, w in enumerate(FJ):
                                mm = nc.tensor.matmul(PS[:, 2 + h, :], W2[0:w, j, :],
                                                      HB[0:w, j, h * HALF:(h + 1) * HALF],
                                                      start=j == 0, stop=j == 2)
                            mm.then_inc(wo_in.sem, 1)

                        project(0, range(PAIRS))
                        project(1, range(3))
                        to_token_major(0)
                        project(1, range(3, PAIRS))
                        to_feature_major(0)
                        gate_and_up(0)
                        to_token_major(1)
                        gate_and_up(1)
                        gate_and_up(2)
                        to_feature_major(1)
                        gate_and_up(3)
                        down(0)
                        gate_and_up(4)
                        gate_and_up(5)
                        down(1)
                        for f in (shift_in, ntok_in, xn_in, gelu_free):
                            f.settle(pe)

                    @block.scalar
                    def _(act):
                        def shift(h):
                            act.wait_ge(x_in.sem, x_in.take())
                            first = 1 if h == 0 else 0
                            nc.scalar.activation(
                                YT[D // 2:P, h * HALF + first:(h + 1) * HALF],
                                XTf[D // 2:P, bass.ds(b * S + h * HALF - 1 + first, HALF - first)],
                                ACT.Copy).then_inc(shift_in.sem, 1)

                        def affine(h):
                            act.wait_ge(nfeat_in.sem, nfeat_in.take())
                            nc.scalar.activation(XN[:, h * HALF:(h + 1) * HALF], PS[:, 4 + h, :],
                                                 ACT.Identity, scale=PL[:, 0:1], bias=PL[:, 1:2])\
                                .then_inc(xn_in.sem, 1)

                        def gelu(i):
                            w, j = FJ[i % 3], i % 3
                            act.wait_ge(proj_in.sem, proj_in.take())
                            nc.scalar.activation(GL[i % 2][0:w, :], GU[i % 2][0:w, 0, :], ACT.Gelu,
                                                 bias=PL[0:w, 5 + j:6 + j]).then_inc(nmx_in.sem, 1)

                        nc.scalar.activation(XS[D // 2:P, 1:S], XTf[D // 2:P, bass.ds((b + 1) % B * S, S - 1)],
                                             ACT.Copy)
                        shift(0)
                        affine(0)
                        shift(1)
                        for i in range(3):
                            gelu(i)
                        affine(1)
                        for i in range(3, 6):
                            gelu(i)
                        for f in (x_in, nfeat_in, proj_in):
                            f.settle(act)

                    @block.vector
                    def _(dve):
                        def residual(h):
                            dve.wait_ge(wo_in.sem, wo_in.take())
                            cols = bass.ds(b * S + h * HALF, HALF)
                            nc.vector.tensor_tensor(XTf[:, cols], XTf[:, cols], PS[:, h, :], ALU.add)\
                                .then_inc(x_in_dve.sem, 1)
                            dve.wait_ge(x_in_dve.sem, x_in_dve.take())
                            dve.sem_inc(x_in.sem, 1)
                            nc.vector.tensor_copy(YT[0:D // 2, h * HALF:(h + 1) * HALF],
                                                  XTf[0:D // 2, cols]).then_inc(shift_in.sem, 1)

                        def normalise(h):
                            dve.wait_ge(to_tokens.sem, to_tokens.take())
                            for t, tile in tokens_of(h):
                                nc.vector.bn_stats(bn[:, t, :], tile).then_inc(stats_in.sem, 1)
                            for t, tile in tokens_of(h):
                                dve.wait_ge(stats_in.sem, stats_in.take())
                                nc.vector.bn_aggr(mv[:, t, :], bn[:, t, :]).then_inc(aggr_in.sem, 1)
                            dve.wait_ge(aggr_in.sem, aggr_in.take(4))
                            nc.vector.tensor_scalar(ve[:, 4 * h:4 * h + 4], mv[:, 4 * h:4 * h + 4, 1],
                                                    1e-5, None, ALU.add).then_inc(var_in.sem, 1)
                            dve.wait_ge(rstd_in.sem, rstd_in.take())
                            for t, tile in tokens_of(h):
                                nc.vector.tensor_scalar(NTOK[:, t, :], tile, mv[:, t, 0:1],
                                                        rstd[:, t:t + 1], ALU.subtract, ALU.mult)\
                                    .then_inc(ntok_in.sem, 1)

                        def gated(i):
                            h, j, w = i // 3, i % 3, FJ[i % 3]
                            dve.wait_ge(nmx_in.sem, nmx_in.take())
                            dve.wait_ge(sc_in.sem, sc_in.take())
                            nc.vector.scalar_tensor_tensor(
                                HB[0:w, j, h * HALF:(h + 1) * HALF], GU[i % 2][0:w, 1, :],
                                PL[0:w, 2 + j:3 + j], GL[i % 2][0:w, :], ALU.add, ALU.mult)\
                                .then_inc(gelu_free.sem, 1)

                        def add_out(h):
                            dve.wait_ge(wo_in.sem, wo_in.take())
                            cols = bass.ds(b * S + h * HALF, HALF)
                            nc.vector.scalar_tensor_tensor(XTf[:, cols], PS[:, 2 + h, :], PL[:, 8:9],
                                                           XTf[:, cols], ALU.add, ALU.add)

                        nc.vector.tensor_copy(XS[0:D // 2, :], XTf[0:D // 2, bass.ds((b + 1) % B * S, S)])
                        residual(0)
                        normalise(0)
                        residual(1)
                        gated(0)
                        normalise(1)
                        for i in range(1, 4):
                            gated(i)
                        add_out(0)
                        gated(4)
                        gated(5)
                        add_out(1)
                        for f in (wo_in, x_in_dve, to_tokens, stats_in, aggr_in, rstd_in, nmx_in, sc_in):
                            f.settle(dve)

                    @block.gpsimd
                    def _(pool):
                        for h in range(NH):
                            pool.wait_ge(var_in.sem, var_in.take())
                            nc.gpsimd.tensor_tensor(rstd[:, 4 * h:4 * h + 4], ve[:, 4 * h:4 * h + 4],
                                                    minus_half[:, 0:4], ALU.pow).then_inc(rstd_in.sem, 1)
                        var_in.settle(pool)

            shift_tokens(0)
            with nc.Fori(0, LAYERS) as l:
                with nc.Block() as block:
                    @block.sync
                    def _(sp):
                        for dst, name in ((QKS[:, :, :], "qks"), (PL[:, :], "pl"), (WO[:, :, :], "wo"),
                                          (W1[:, :], "w1"), (W2[:, :, :], "w2")):
                            src = a[name]
                            if name == "qks":
                                src = src[bass.ds(l, 1), :, :].partition_broadcast(P)
                                src = src.rearrange("p o k n -> p (o k) n")
                            elif len(src.shape) == 4:
                                src = src[bass.ds(l, 1), :, :, :].rearrange("o p j n -> (o p) j n")
                            else:
                                src = src[bass.ds(l, 1), :, :].rearrange("o p n -> (o p) n")
                            sp.dma_start(dst, src).then_inc(layer_in.sem, 16)
                            if name == "qks":
                                sp.wait_ge(layer_in.sem, layer_in.take(16))
                                sp.sem_inc(table_in.sem, 1)
                        sp.wait_ge(layer_in.sem, layer_in.take(64))
                        layer_in.settle(sp)
                        nl = (l + 1) % LAYERS
                        sp.dma_start(WQf[:, bass.ds(((l + 1) % 2) * (PAIRS * 384), PAIRS * 384)],
                                     a["wqkv"][bass.ds(nl, 1), :, :].rearrange("o p n -> (o p) n"))\
                            .then_inc(wq_in.sem, 16)

                    @block.vector
                    def _(dve):
                        dve.wait_ge(table_in.sem, table_in.take())
                        for k, (dst, src) in enumerate(((COSL, COS0), (SINL, SIN0))):
                            nc.vector.tensor_tensor(dst[:, :, :], src[:, :, :],
                                                    QKS[:, k, :].unsqueeze(1).to_broadcast([P, NT, 256]),
                                                    ALU.mult)
                        table_in.settle(dve)
                with nc.Fori(0, B) as b:
                    attention(l, b)
                    feed_forward(b)
                with nc.Block() as block:
                    @block.sync
                    def _(sp):
                        sp.wait_ge(wq_in.sem, wq_in.take(16))
                        wq_in.settle(sp)
            with nc.Fori(0, B) as b:
                with nc.Block() as block:
                    @block.scalar
                    def _(act):
                        nc.scalar.activation(YT[:, :], XTf[:, bass.ds(b * S, S)], ACT.Copy)
                norm(features=YT, residual=x_batch(b))
        if "C" in stages:
            WC = BIG[:, 0:384]
            WOC = BIG[:, 384:512]
            HM = BIG[:, 512:516]
            BDM = BIG[:, 640:768]
            CAU = BIG[:, 768:896]
            BD = BIG[:, 896:1024]
            BDT = BIG[:, 1024:1152]
            KE = COSL[:, 0:4, :].rearrange("p a b -> p (a b)")
            ZR = COSL[:, 4:8, :].rearrange("p a b -> p (a b)")
            KET = SINL[:, 0:4, :].rearrange("p a (c n) -> p (a c) n", n=P)
            QP = SINL[:, 4:8, :].rearrange("p a b -> p (a b)")
            QV = BIG[:, 1152:1152 + NT * 256].rearrange("p (t n) -> p t n", n=256)
            QM = BIG[:, 3200:3200 + 4 * S].rearrange("p (j s) -> p j s", j=4)
            AM = COS0[:, :, :].rearrange("p a b -> p (a b)").rearrange("p (g n) -> p g n", g=4)
            OCT = SIN0[:, 0:4, :].rearrange("p a b -> p (a b)")
            ONES = SIN0[:, 4:8, :].rearrange("p a b -> p (a b)")
            OC = R1[:, 0, 0:P]
            qm = RR[:, 0, 0:P]
            qsum = RR[:, 0, P:2 * P]
            qr = RR[:, 1, 0:P]
            kmx = NMX[:, 0:1]
            layer_c = flow("stage_c_weights_in")
            am_free = flow("masked_scores_used")
            st_free = flow("state_used")
            SQ8 = [t[:, :, 0:P].rearrange("p t (h c) -> p t h c", c=LC) for t in (QV,)][0]
            qv_ps = flow("qv_tile_in_psum")
            qv_in = flow("qv_tile_copied")
            qv_free = flow("qv_bank_copied")
            k_ps = flow("k_in_psum")
            kmx_in = flow("k_max_ready")
            ke_in = flow("k_exp_ready")
            ke_pe = flow("k_exp_ready_for_transposes")
            z_in = flow("k_cumulated")
            qs_in = flow("q_softmax_step")
            qe_in = flow("q_shifted")
            qx_in = flow("q_exp_ready")
            qn_in = flow("q_normalised")
            qt_ps = flow("q_transposed")
            kt_ps = flow("k_transposed")
            kt_in = flow("k_token_major")
            qm_in = flow("q_masks_ready")
            a_ps = flow("scores_in_psum")
            a_in = flow("scores_masked")
            st_ps = flow("state_update_in_psum")
            bdt_in = flow("state_update_masked")
            bd_in = flow("state_ready")
            oc_ps = flow("linear_out_in_psum")
            oc_in = flow("linear_out_copied")
            oct_ps = flow("linear_out_transposed")
            oct_in = flow("linear_out_feature_major")
            yc_ps = flow("projection_in_psum")
            with nc.Block() as block:
                @block.sync
                def _(sp):
                    for dst, n in ((WC, "wc"), (WOC, "woc"), (HM, "headmask"), (BDM, "blockdiag"),
                                   (CAU, "causal")):
                        sp.dma_start(dst, a[n]).then_inc(layer_c.sem, 16)
                    sp.wait_ge(layer_c.sem, layer_c.take(80))
                    layer_c.settle(sp)

                @block.vector
                def _(dve):
                    nc.vector.memset(ONES, 1.0)
            with nc.Fori(0, B) as b:
                norm(tokens=x_tiles(b), dst=XN[:, :])
                with nc.Block() as block:
                    @block.tensor
                    def _(pe):
                        for h in range(NH):
                            mm = nc.tensor.matmul(PS[:, h, :], WC[:, 256:384], XN[:, h * HALF:(h + 1) * HALF],
                                                  start=True, stop=True)
                        mm.then_inc(k_ps.sem, 1)
                        for t in range(NT):
                            if t >= 2:
                                pe.wait_ge(qv_free.sem, qv_free.peek(t - 1))
                            nc.tensor.matmul(PS[:, 2 + t % 2, 0:256], XN[:, t * P:(t + 1) * P], WC[:, 0:256],
                                             start=True, stop=True).then_inc(qv_ps.sem, 1)
                        pe.wait_ge(qv_free.sem, qv_free.take(NT))
                        pe.wait_ge(ke_pe.sem, ke_pe.take())
                        for t in range(NT):
                            tr = nc.tensor.transpose(bank_tiles(4, t), KE[:, t * P:(t + 1) * P], ident[:, :])
                        tr.then_inc(kt_ps.sem, 1)
                        pe.wait_ge(qn_in.sem, qn_in.take())
                        for t in range(NT):
                            tr = nc.tensor.transpose(bank_tiles(6, t), QV[:, t, 0:P], ident[:, :])
                        tr.then_inc(qt_ps.sem, 1)
                        for f in (qv_free, ke_pe, qn_in):
                            f.settle(pe)

                    @block.scalar
                    def _(act):
                        for t in range(NT):
                            act.wait_ge(qv_ps.sem, qv_ps.take())
                            nc.scalar.activation(QV[:, t, :], PS[:, 2 + t % 2, 0:256], ACT.Copy)\
                                .then_inc(qv_free.sem, 1)
                        act.drain().then_inc(qv_in.sem, 1)
                        act.wait_ge(kmx_in.sem, kmx_in.take())
                        nc.scalar.activation(KE.rearrange("p (h s) -> p h s", h=NH), PS[:, 0:2, :], ACT.Exp,
                                             bias=kmx).then_inc(ke_in.sem, 1)
                        act.drain().then_inc(ke_pe.sem, 1)
                        act.wait_ge(qe_in.sem, qe_in.take())
                        nc.scalar.activation(SQ8, SQ8, ACT.Exp).then_inc(qx_in.sem, 1)
                        act.wait_ge(kt_ps.sem, kt_ps.take())
                        nc.scalar.activation(KET.rearrange("p (h t) n -> p h (t n)", h=2), PS[:, 4:6, :],
                                             ACT.Copy)
                        for f in (qv_ps, kmx_in, qe_in, kt_ps):
                            f.settle(act)

                    @block.vector
                    def _(dve):
                        dve.wait_ge(k_ps.sem, k_ps.take())
                        nc.vector.tensor_reduce(kmx, PS[:, 0:2, :], AX.XY, ALU.max, negate=True)\
                            .then_inc(kmx_in.sem, 1)
                        dve.wait_ge(qv_in.sem, qv_in.take())
                        qh = qm.rearrange("p (t h) -> p t h", h=LH)
                        nc.vector.tensor_reduce(qh, SQ8, AX.X, ALU.max).then_inc(qs_in.sem, 1)
                        dve.wait_ge(qs_in.sem, qs_in.take())
                        for half in range(2):
                            t = slice(4 * half, 4 * half + 4)
                            sub = nc.vector.tensor_tensor(
                                SQ8[:, t, :, :].rearrange("p t h c -> p t (h c)").rearrange("p t (h c) -> p t h c", c=LC),
                                SQ8[:, t, :, :],
                                qh[:, t, :].unsqueeze(3).to_broadcast([P, 4, LH, LC]), ALU.subtract)
                        sub.then_inc(qe_in.sem, 1)
                        dve.wait_ge(ke_in.sem, ke_in.take())
                        nc.vector.tensor_tensor_scan(ZR, ONES, KE, 0.0, ALU.mult, ALU.add).then_inc(z_in.sem, 1)
                        dve.wait_ge(z_in.sem, z_in.take())
                        nc.vector.tensor_scalar(XS[:, :], ZR, 1e-9, None, ALU.add).then_inc(z_in.sem, 1)
                        dve.wait_ge(z_in.sem, z_in.take())
                        nc.vector.reciprocal(ZR, XS[:, :]).then_inc(z_in.sem, 1)
                        dve.wait_ge(qx_in.sem, qx_in.take())
                        nc.vector.tensor_reduce(qsum.rearrange("p (t h) -> p t h", h=LH), SQ8, AX.X, ALU.add)\
                            .then_inc(qs_in.sem, 1)
                        dve.wait_ge(qs_in.sem, qs_in.take())
                        nc.vector.reciprocal(qr, qsum).then_inc(qs_in.sem, 1)
                        dve.wait_ge(qs_in.sem, qs_in.take())
                        qrh = qr.rearrange("p (t h) -> p t h", h=LH)
                        for half in range(2):
                            t = slice(4 * half, 4 * half + 4)
                            mul = nc.vector.tensor_tensor(SQ8[:, t, :, :], SQ8[:, t, :, :],
                                                          qrh[:, t, :].unsqueeze(3)
                                                          .to_broadcast([P, 4, LH, LC]), ALU.mult)
                        mul.then_inc(qn_in.sem, 1)
                        dve.wait_ge(qt_ps.sem, qt_ps.take())
                        dve.wait_ge(z_in.sem, z_in.take())
                        nc.vector.scalar_tensor_tensor(QP.rearrange("p (h s) -> p h s", h=NH), PS[:, 6:8, :],
                                                       float(LC) ** -0.5, ZR.rearrange("p (h s) -> p h s", h=NH),
                                                       ALU.mult, ALU.mult).then_inc(qm_in.sem, 1)
                        dve.wait_ge(qm_in.sem, qm_in.take())
                        for j in range(4):
                            nc.vector.tensor_scalar(QM[:, j, :], QP, HM[:, j:j + 1], None, ALU.mult)
                        nc.vector.memset(BD, 0.0)
                        for f in (k_ps, qv_in, qs_in, ke_in, z_in, qx_in, qt_ps, qm_in):
                            f.settle(dve)
                with nc.Block() as block:
                    @block.tensor
                    def _(pe):
                        for t in range(NT):
                            ts = slice(t * P, (t + 1) * P)
                            if t:
                                pe.wait_ge(a_in.sem, a_in.take())
                            for g in range(4):
                                rows = slice(32 * g, 32 * g + 32)
                                mm = nc.tensor.matmul(PS[:, g, :].rearrange("p (j s) -> p j s", j=4),
                                                      KE[rows, ts], QM[rows, :, ts], start=True, stop=True,
                                                      tile_position=(32 * g, 0))
                            mm.then_inc(a_ps.sem, 1)
                            if t:
                                pe.wait_ge(bd_in.sem, bd_in.take())
                            mm = nc.tensor.matmul(PS[:, 4, 0:P], KET[:, t, :], QV[:, t, P:2 * P],
                                                  start=True, stop=True)
                            mm.then_inc(st_ps.sem, 1)
                            if t:
                                pe.wait_ge(oc_in.sem, oc_in.peek(t))
                            nc.tensor.matmul(PS[:, 5, 0:P], QP[:, ts], BD, start=True, stop=False)
                            pe.wait_ge(a_in.sem, a_in.peek(1))
                            for h in range(LH):
                                mm = nc.tensor.matmul(PS[:, 5, LC * h:LC * h + LC],
                                                      AM[:, h // 4, (h % 4) * P:(h % 4 + 1) * P],
                                                      QV[:, t, P + LC * h:P + LC * h + LC],
                                                      start=False, stop=h == LH - 1)
                            mm.then_inc(oc_ps.sem, 1)
                            pe.wait_ge(oc_in.sem, oc_in.peek(t + 1))
                            if t:
                                pe.wait_ge(oct_in.sem, oct_in.peek(t))
                            nc.tensor.transpose(PS[:, 6, 0:P], OC, ident[:, :]).then_inc(oct_ps.sem, 1)
                        pe.wait_ge(a_in.sem, a_in.take())
                        pe.wait_ge(bd_in.sem, bd_in.take())
                        pe.wait_ge(oc_in.sem, oc_in.take(NT))
                        pe.wait_ge(oct_in.sem, oct_in.take(NT))
                        for h in range(NH):
                            nc.tensor.matmul(PS[:, h, :], WOC, OCT[:, h * HALF:(h + 1) * HALF],
                                             start=True, stop=True).then_inc(yc_ps.sem, 1)
                        for f in (a_in, bd_in, oc_in, oct_in):
                            f.settle(pe)

                    @block.vector
                    def _(dve):
                        for t in range(NT):
                            dve.wait_ge(a_ps.sem, a_ps.take())
                            if t:
                                dve.wait_ge(am_free.sem, am_free.take())
                            nc.vector.tensor_tensor(AM[:, :, :].rearrange("p g (j s) -> p (g j) s", s=P),
                                                    PS[:, 0:4, :].rearrange("p g (j s) -> p (g j) s", s=P),
                                                    CAU.unsqueeze(1).to_broadcast([P, 16, P]), ALU.mult)\
                                .then_inc(a_in.sem, 1)
                            dve.wait_ge(st_ps.sem, st_ps.take())
                            nc.vector.tensor_tensor(BDT, PS[:, 4, 0:P], BDM, ALU.mult).then_inc(bdt_in.sem, 1)
                            dve.wait_ge(bdt_in.sem, bdt_in.take())
                            if t < NT - 1:
                                dve.wait_ge(st_free.sem, st_free.take())
                            else:
                                dve.wait_ge(st_free.sem, st_free.take())
                            nc.vector.tensor_tensor(BD, BD, BDT, ALU.add).then_inc(bd_in.sem, 1)
                        for f in (a_ps, st_ps, bdt_in, am_free, st_free):
                            f.settle(dve)

                    @block.scalar
                    def _(act):
                        for t in range(NT):
                            act.wait_ge(oc_ps.sem, oc_ps.take())
                            nc.scalar.activation(OC, PS[:, 5, 0:P], ACT.Copy).then_inc(oc_in.sem, 1)
                            if t < NT - 1:
                                act.sem_inc(am_free.sem, 1)
                            act.sem_inc(st_free.sem, 1)
                            act.wait_ge(oct_ps.sem, oct_ps.take())
                            nc.scalar.activation(OCT[:, t * P:(t + 1) * P], PS[:, 6, 0:P], ACT.Copy)\
                                .then_inc(oct_in.sem, 1)
                        for h in range(NH):
                            act.wait_ge(yc_ps.sem, yc_ps.take())
                            nc.scalar.activation(YT[:, h * HALF:(h + 1) * HALF], PS[:, h, :], ACT.Copy)
                        for f in (oc_ps, oct_ps, yc_ps):
                            f.settle(act)
                norm(features=YT, residual=x_batch(b))
        if "D" in stages:
            WGU = BIG[:, 0:NE * 2 * EI]
            WD = BIG[:, 4096:4096 + NE * 2 * D]
            GW = BIG[:, 6144:6144 + NE]
            AF = BIG[:, 6160:6160 + NT * B * NE].rearrange("p (t n) -> p t n", n=B * NE)
            GT = BIG[:, 6300:6300 + NT * B * NE].rearrange("p (t n) -> p t n", n=B * NE)
            LG = BIG[:, 6432:6432 + NT * NE].rearrange("p (t e) -> p t e", e=NE)
            LE = BIG[:, 6496:6496 + NT * NE].rearrange("p (t e) -> p t e", e=NE)
            GB = BIG[:, 6560:6560 + NT * NE].rearrange("p (t e) -> p t e", e=NE)
            AT = COS0[0:B * NE, 0:4, :].rearrange("p a b -> p (a b)")
            WK = [COS0[0:B * NE, 4:8, :].rearrange("p a b -> p (a b)"),
                  SIN0[0:B * NE, 0:4, :].rearrange("p a b -> p (a b)")]
            GG = SIN0[0:B * NE, 4:8, :].rearrange("p a b -> p (a b)")
            RK = COS0[0:B * NE, 4:8, :].rearrange("p a b -> p (a b)")
            SEL = SIN0[0:B * NE, 4:8, :].rearrange("p a b -> p (a b)")
            ONESD = XS[0:B * NE, :]
            XTOK = XT[:, :, :].rearrange("p b s -> p (b s)").rearrange("p (t n) -> p t n", n=D)
            TOK = QKT[:, :, :].rearrange("p k s -> p (k s)")[:, 0:NT * (D + NE)]\
                .rearrange("p (t n) -> p t n", n=D + NE)
            ONEHOT = COSL[:, 0:4, :].rearrange("p a (c n) -> p (a c) n", n=P)
            ONEHOT_T = COSL[:, 4:8, :].rearrange("p a b -> p (a b)")
            PLACES = SINL[:, 0, 0:TOPK]
            PLACE = SINL[:, 1, 0:1]
            CHOSEN = [SINL[:, 2 + k, 0:D + NE] for k in range(2)]
            CHOSEN_T = SINL[:, 4, 0:TOPK]
            SGD, GSD, HD, HTD = SQ[:, 0, 0:4, :].rearrange("p a b -> p (a b)"), R1[:, 0, :], \
                R2[:, 0, :], RR[:, 0, :]
            OE = R1[:, 1, 0:D]
            top8 = [mv[0:B * NE, 4 * k:4 * k + 4, :].rearrange("p a b -> p (a b)") for k in range(2)]
            layer_d = flow("stage_d_weights_in")
            lg_ps = flow("logits_in_psum")
            lg_in = flow("logit_step")
            le_in = flow("logits_shifted")
            lx_in = flow("logits_exp_ready")
            at_ps = flow("affinities_transposed")
            top_in = flow("top8_step")
            rk_in = flow("places_ready")
            rkt_ps = flow("places_token_major")
            hot_in = flow("one_hot_ready")
            hot_used = flow("one_hot_used")
            place_ps = flow("places_broadcast")
            hott_in = flow("one_hot_transposed_ready")
            hott_used = flow("expert_output_scattered")
            ch_ps = flow("chosen_tokens_in_psum")
            ch_in = flow("chosen_tokens_ready")
            cht_ps = flow("chosen_tokens_transposed")
            cht_in = flow("chosen_tokens_feature_major")
            oe_in = flow("expert_output_ready")
            up_ps = flow("gate_up_in_psum")
            sg_in = flow("sigmoid_ready")
            gs_in = flow("silu_ready")
            hd_in = flow("hidden_tile_ready")
            ht_ps = flow("hidden_transposed")
            ht_in = flow("hidden_feature_major")
            dn_ps = flow("down_in_psum")
            with nc.Block() as block:
                @block.sync
                def _(sp):
                    sp.dma_start(GW, a["gw"]).then_inc(layer_d.sem, 16)
                    sp.dma_start(WGU.rearrange("p (e n) -> p e n", e=NE), a["wgu"]).then_inc(layer_d.sem, 16)
                    sp.dma_start(WD.rearrange("p (e k n) -> p e k n", e=NE, k=2), a["wd"])\
                        .then_inc(layer_d.sem, 16)
                    sp.dma_start(PLACES, a["places"]).then_inc(layer_d.sem, 16)
                    sp.dma_start(PLACE, a["places"][0:1, :].rearrange("o p -> p o")).then_inc(layer_d.sem, 16)
                    sp.wait_ge(layer_d.sem, layer_d.take(80))
                    layer_d.settle(sp)
            with nc.Fori(0, B) as b:
                norm(tokens=x_tiles(b), dst=XN[:, :])
                with nc.Block() as block:
                    @block.tensor
                    def _(pe):
                        for t in range(NT):
                            mm = nc.tensor.matmul(PS[:, 0, NE * t:NE * t + NE], XN[:, t * P:(t + 1) * P], GW,
                                                  start=True, stop=True)
                        mm.then_inc(lg_ps.sem, 1)

                    @block.scalar
                    def _(act):
                        nc.scalar.activation(XTOK[:, bass.ds(b * NT, NT), :], NTOK[:, :, :], ACT.Copy)
                        act.wait_ge(le_in.sem, le_in.take())
                        nc.scalar.activation(LE, LG, ACT.Exp).then_inc(lx_in.sem, 1)
                        le_in.settle(act)

                    @block.vector
                    def _(dve):
                        pl = PS[:, 0, 0:NT * NE].rearrange("p (t e) -> p t e", e=NE)

                        def per_token(col):
                            return col.unsqueeze(2).to_broadcast([P, NT, NE])
                        dve.wait_ge(lg_ps.sem, lg_ps.take())
                        nc.vector.tensor_reduce(ms[:, :], pl, AX.X, ALU.max).then_inc(lg_in.sem, 1)
                        dve.wait_ge(lg_in.sem, lg_in.take())
                        nc.vector.tensor_tensor(LG, pl, per_token(ms[:, :]), ALU.subtract)\
                            .then_inc(le_in.sem, 1)
                        dve.wait_ge(lx_in.sem, lx_in.take())
                        nc.vector.tensor_reduce(ve[:, :], LE, AX.X, ALU.add).then_inc(lg_in.sem, 1)
                        dve.wait_ge(lg_in.sem, lg_in.take())
                        nc.vector.reciprocal(rstd[:, :], ve[:, :]).then_inc(lg_in.sem, 1)
                        dve.wait_ge(lg_in.sem, lg_in.take())
                        nc.vector.tensor_tensor(AF[:, :, bass.ds(b * NE, NE)], LE, per_token(rstd[:, :]),
                                                ALU.mult)
                        for f in (lg_ps, lg_in, lx_in):
                            f.settle(dve)
            with nc.Block() as block:
                @block.tensor
                def _(pe):
                    for t in range(NT):
                        tr = nc.tensor.transpose(PS[0:B * NE, t // 4, (t % 4) * P:(t % 4 + 1) * P],
                                                 AF[:, t, :], ident[:, :])
                    tr.then_inc(at_ps.sem, 1)
                    pe.wait_ge(rk_in.sem, rk_in.take())
                    for t in range(NT):
                        tr = nc.tensor.transpose(PS[:, 2, B * NE * t:B * NE * (t + 1)],
                                                 RK[:, t * P:(t + 1) * P], ident[0:B * NE, 0:B * NE])
                    tr.then_inc(rkt_ps.sem, 1)
                    rk_in.settle(pe)

                @block.vector
                def _(dve):
                    dve.wait_ge(at_ps.sem, at_ps.take())
                    nc.vector.tensor_copy(AT.rearrange("p (h s) -> p h s", h=2), PS[0:B * NE, 0:2, :])\
                        .then_inc(top_in.sem, 1)
                    nc.vector.memset(ONESD, 1.0).then_inc(top_in.sem, 1)
                    dve.wait_ge(top_in.sem, top_in.take(2))
                    src = AT
                    for r in range(TOPK // 8):
                        nc.vector.max(top8[r % 2], src).then_inc(top_in.sem, 1)
                        dve.wait_ge(top_in.sem, top_in.take())
                        nc.vector.match_replace(WK[r % 2], top8[r % 2], src, -1.0)\
                            .then_inc(top_in.sem, 1)
                        dve.wait_ge(top_in.sem, top_in.take())
                        src = WK[r % 2]
                    nc.vector.tensor_scalar(SEL, src, 0.0, None, ALU.is_lt).then_inc(top_in.sem, 1)
                    dve.wait_ge(top_in.sem, top_in.take())
                    nc.vector.tensor_tensor_scan(AT, ONESD, SEL, 0.0, ALU.mult, ALU.add)\
                        .then_inc(top_in.sem, 1)
                    dve.wait_ge(top_in.sem, top_in.take())
                    nc.vector.tensor_tensor(RK, AT, SEL, ALU.mult).then_inc(rk_in.sem, 1)
                    nc.vector.tensor_tensor(RKB[:, :], AT, SEL, ALU.mult)
                    dve.wait_ge(rkt_ps.sem, rkt_ps.take())
                    nc.vector.tensor_copy(GT.rearrange("p t n -> p (t n)"), PS[:, 2, 0:NT * B * NE])
                    for f in (at_ps, top_in, rkt_ps):
                        f.settle(dve)
            with nc.Fori(0, B) as b:
                def run(eng, step, flows):
                    def settle():
                        for f in flows:
                            f.settle(eng)
                    for n in range(-2, 0):
                        step(n, 0)
                    settle()
                    with eng.Fori(0, NE // 2 - 1) as i:
                        for n in range(2):
                            step(n, i)
                        settle()
                    for n in range(NE - 2, NE):
                        step(n, 0)
                    settle()

                def expert(n, i):
                    return n + 2 * i

                with nc.Block() as block:
                    @block.scalar
                    def _(act):
                        nc.scalar.activation(TOK[:, :, 0:D], XTOK[:, bass.ds(b * NT, NT), :], ACT.Copy)

                    @block.vector
                    def _(dve):
                        nc.vector.tensor_copy(TOK[:, :, D:D + NE], AF[:, :, bass.ds(b * NE, NE)])
                        nc.vector.memset(YT[:, 0:HALF], 0.0)
                with nc.Block() as block:
                    @block.tensor
                    def _(pe):
                        def step(n, i):
                            now, coming = 0 <= n, 0 <= n + 1 < NE
                            if coming:
                                pe.wait_ge(hot_in.sem, hot_in.take())
                                for t in range(NT):
                                    mm = nc.tensor.matmul(
                                        PS[:, 2, 0:D + NE], ONEHOT[:, t, :], TOK[:, t, :],
                                        start=t == 0, stop=t == NT - 1)
                                mm.then_inc(ch_ps.sem, 1)
                            if now:
                                pe.wait_ge(hd_in.sem, hd_in.take())
                                for k in range(2):
                                    tr = nc.tensor.transpose(PS[:, 5, k * P:(k + 1) * P],
                                                             HD[:, k * P:(k + 1) * P], ident[:, :])
                                tr.then_inc(ht_ps.sem, 1)
                            if coming:
                                pe.wait_ge(ch_in.sem, ch_in.take())
                                nc.tensor.transpose(PS[:, 3, 0:P], CHOSEN[(n + 1) % 2][:, 0:D], ident[:, :])\
                                    .then_inc(cht_ps.sem, 1)
                            if now:
                                pe.wait_ge(ht_in.sem, ht_in.take())
                                for k in range(2):
                                    mm = nc.tensor.matmul(PS[:, 5, 0:D], HTD[:, k * P:(k + 1) * P],
                                                          WD[:, bass.ds((expert(n, i) * 2 + k) * D, D)],
                                                          start=k == 0, stop=k == 1)
                                mm.then_inc(dn_ps.sem, 1)
                            if coming:
                                pe.wait_ge(cht_in.sem, cht_in.take())
                                nc.tensor.matmul(PS[:, 4, :], CHOSEN_T,
                                                 WGU[:, bass.ds(expert(n + 1, i) * 2 * EI, 2 * EI)],
                                                 start=True, stop=True).then_inc(up_ps.sem, 1)
                            if now:
                                pe.wait_ge(hott_in.sem, hott_in.take())
                            if coming:
                                which = identb[0:B * NE, bass.ds(b * NE + expert(n + 1, i), 1)]
                                for h in range(NH):
                                    mm = nc.tensor.matmul(PS[:, h, :], which.to_broadcast([B * NE, P]),
                                                          RKB[:, h * HALF:(h + 1) * HALF],
                                                          start=True, stop=True)
                                mm.then_inc(place_ps.sem, 1)
                            if now:
                                pe.wait_ge(oe_in.sem, oe_in.take())
                                for t in range(NT):
                                    mm = nc.tensor.matmul(bank_tiles(6, t), ONEHOT_T[:, t * P:(t + 1) * P],
                                                          OE, start=False, stop=False,
                                                          skip_group_check=True)
                                mm.then_inc(hott_used.sem, 1)

                        for h in range(NH):
                            nc.tensor.matmul(PS[:, 6 + h, :], ident[:, :], YT[:, 0:HALF], start=True,
                                             stop=False)
                        run(pe, step, [hot_in, hd_in, ch_in, ht_in, cht_in, hott_in, oe_in])
                        for h in range(NH):
                            nc.tensor.matmul(PS[:, 6 + h, :], ident[:, :], YT[:, 0:HALF], start=False,
                                             stop=True)

                    @block.scalar
                    def _(act):
                        def step(n, i):
                            now, coming = 0 <= n, 0 <= n + 1 < NE
                            if now:
                                act.wait_ge(up_ps.sem, up_ps.take())
                                nc.scalar.activation(SGD, PS[:, 4, 0:EI], ACT.Sigmoid).then_inc(sg_in.sem, 1)
                            if coming:
                                act.wait_ge(ch_ps.sem, ch_ps.take())
                                act.sem_inc(hot_used.sem, 1)
                                nc.scalar.activation(CHOSEN[(n + 1) % 2], PS[:, 2, 0:D + NE], ACT.Copy)\
                                    .then_inc(ch_in.sem, 1)
                            if now:
                                act.wait_ge(ht_ps.sem, ht_ps.take())
                                nc.scalar.activation(HTD, PS[:, 5, 0:EI], ACT.Copy).then_inc(ht_in.sem, 1)
                            if coming:
                                act.wait_ge(cht_ps.sem, cht_ps.take())
                                nc.scalar.activation(CHOSEN_T, PS[:, 3, 0:P], ACT.Copy)\
                                    .then_inc(cht_in.sem, 1)
                            if now:
                                act.wait_ge(dn_ps.sem, dn_ps.take())
                                nc.scalar.activation(OE, PS[:, 5, 0:D], ACT.Copy).then_inc(oe_in.sem, 1)
                        run(act, step, [up_ps, ch_ps, ht_ps, cht_ps, dn_ps])

                    @block.vector
                    def _(dve):
                        def step(n, i):
                            if 0 <= n:
                                dve.wait_ge(sg_in.sem, sg_in.take())
                                nc.vector.tensor_tensor(GSD, PS[:, 4, 0:EI], SGD, ALU.mult)\
                                    .then_inc(gs_in.sem, 1)
                                dve.wait_ge(gs_in.sem, gs_in.take())
                                nc.vector.scalar_tensor_tensor(HD, PS[:, 4, EI:2 * EI],
                                                               CHOSEN[n % 2][:, bass.ds(D + expert(n, i), 1)],
                                                               GSD,
                                                               ALU.mult, ALU.mult).then_inc(hd_in.sem, 1)
                                dve.wait_ge(hott_used.sem, hott_used.take())
                                dve.wait_ge(place_ps.sem, place_ps.take())
                                nc.vector.tensor_scalar(ONEHOT_T.rearrange("p (h s) -> p h s", h=NH),
                                                        PS[:, 0:2, :], PLACE, None, ALU.is_equal)\
                                    .then_inc(hott_in.sem, 1)
                            if 0 <= n + 2 < NE:
                                if n + 2 > 0:
                                    dve.wait_ge(hot_used.sem, hot_used.take())
                                col = GT[:, :, bass.ds(b * NE + expert(n + 2, i), 1)]
                                nc.vector.tensor_tensor(ONEHOT,
                                                        PLACES.unsqueeze(1).to_broadcast([P, NT, TOPK]),
                                                        col.to_broadcast([P, NT, TOPK]), ALU.is_equal)\
                                    .then_inc(hot_in.sem, 1)
                        dve.sem_inc(hott_used.sem, 1)
                        run(dve, step, [sg_in, gs_in, hott_used, place_ps, hot_used])
                        dve.wait_ge(hott_used.sem, hott_used.take())
                        dve.wait_ge(hot_used.sem, hot_used.take())
                        for f in (hott_used, hot_used):
                            f.settle(dve)
                norm(tokens=lambda t: bank_tiles(6, t), residual=x_batch(b))
        with nc.Block() as block:
            @block.sync
            def _(sp):
                sp.dma_start(out.rearrange("(t p) d -> p t d", p=P), X[:, :, :]).then_inc(s_out, 16)
                sp.wait_ge(s_out, 16)


def _rotary_tables():
    f = np.float32
    half = np.arange(0, DH, 2, dtype=f)
    inv_freq = (f(1.0) / f(10000.0) ** (half / f(DH))).astype(f)
    t = np.arange(S, dtype=f)
    freqs = t[:, None] * inv_freq[None, :]
    base = ((half + f(0.4 * DH)) / f(1.4 * DH)).astype(f)
    power = ((t - S // 2) / (WIN // 2)).astype(f)
    scale = (base[None, :].astype(np.float64) ** power[:, None]).astype(f)
    cos, sin = np.cos(freqs.astype(np.float64)), np.sin(freqs.astype(np.float64))
    tables = []
    for fn, sign in ((cos, 1.0), (sin, -1.0)):
        q = np.concatenate([sign * fn * scale * 8.0, fn * scale * 8.0], 1)
        k = np.concatenate([sign * fn / scale, fn / scale], 1)
        full = np.concatenate([q, q, k, k], 1).astype(f)
        tables.append(np.ascontiguousarray(full.reshape(NT, P, 256).transpose(1, 0, 2)))
    return tables


def _band_mask():
    i = np.arange(P)[:, None]
    j = np.arange(KW)[None, :] - WIN
    rest = (j <= i) & (j >= i - WIN)
    masks = [rest & (j >= 0), rest, rest]
    return np.stack([np.where(m, 0.0, NEG) for m in masks], 1).astype(np.float32)


def kernel(**inputs):
    import concourse.bacc as _bacc
    from concourse.bass_utils import run_bass_kernel_spmd as _run

    g = {k: np.asarray(v) for k, v in inputs.items()}
    cos, sin = _rotary_tables()

    def cols(*vs):
        return np.stack(vs, 1)

    def features(w, n):
        return np.ascontiguousarray(w.reshape(n, P, -1).transpose(1, 0, 2))

    wqkv = g["L0_ffn_Wqkv"].reshape(DEPTH, D, 3, PAIRS, P).transpose(0, 1, 3, 2, 4).reshape(DEPTH, D, -1)
    qs, ks = g["L0_ffn_q_scale"], g["L0_ffn_k_scale"]
    qks = np.concatenate([qs, qs, ks, ks], 1)
    swapped = qks.reshape(DEPTH, 4, 2, DH // 2)[:, :, ::-1].reshape(DEPTH, 256)
    b1 = np.zeros((DEPTH, P, 6), np.float32)
    w2 = np.zeros((DEPTH, P, 3, D), np.float32)
    for j, w in enumerate(FJ):
        b1[:, :w, j] = g["L0_ffn_b1"][:, j * P:j * P + w]
        b1[:, :w, 3 + j] = g["L0_ffn_b1"][:, FI + j * P:FI + j * P + w]
        w2[:, :w, j] = g["L0_ffn_W2"][:, j * P:j * P + w]
    pl = np.concatenate([g["L0_ffn_ln_g"][:, :, None], g["L0_ffn_ln_b"][:, :, None], b1,
                         g["L0_ffn_b2"][:, :, None]], 2)
    c_idx = np.arange(P)
    arrays = {
        "x": g["L0_attn_x"].reshape(B * S, D), "cos": cos, "sin": sin, "bandmask": _band_mask(),
        "w3": np.stack([g["L0_attn_Wg"], g["L0_attn_Wv"], g["L0_attn_Wd"]], 1),
        "wga": g["L0_attn_W_gate"], "wua": g["L0_attn_W_up"], "woa": features(g["L0_attn_W_out"], 3),
        "pa": cols(g["L0_attn_w_rms_mix"], g["L0_attn_w_rms_ffn"], g["L0_attn_bg"], g["L0_attn_bv"],
                   g["L0_attn_bd"]),
        "wqkv": wqkv, "wo": g["L0_ffn_Wo"].reshape(DEPTH, PAIRS, P, D).transpose(0, 2, 1, 3),
        "w1": g["L0_ffn_W1"], "w2": w2, "pl": pl,
        "qks": np.stack([qks, swapped], 1),
        "wc": np.concatenate([g["L1_attn_W_qkv"].T[:, 0:P], g["L1_attn_W_qkv"].T[:, 2 * P:],
                              g["L1_attn_W_qkv"].T[:, P:2 * P]], 1),
        "woc": g["L1_attn_W_out"].T,
        "headmask": (c_idx[:, None] // LC % 4 == np.arange(4)[None, :]).astype(np.float32),
        "blockdiag": (c_idx[:, None] // LC == c_idx[None, :] // LC).astype(np.float32),
        "causal": (c_idx[None, :] >= c_idx[:, None]).astype(np.float32),
        "places": np.tile(c_idx + 1, (P, 1)).astype(np.float32),
        "gw": g["L1_ffn_gate_w"],
        "wgu": np.concatenate([g["L1_ffn_Wg"], g["L1_ffn_Wu"]], 2).transpose(1, 0, 2),
        "wd": g["L1_ffn_Wd"].reshape(NE, 2, P, D).transpose(2, 0, 1, 3),
    }
    arrays = {k: np.ascontiguousarray(v) for k, v in arrays.items()}
    nc = _bacc.Bacc("TRN2", target_bir_lowering=False, num_devices=1)
    aps = {k: nc.dram_tensor(f"in_{k}", v.shape, mybir.dt.from_np(v.dtype), kind="ExternalInput").ap()
           for k, v in arrays.items()}
    o = nc.dram_tensor("out_x", (B * S, D), F32, kind="ExternalOutput").ap()
    mixed_layers_kernel(nc, aps, o, STAGES)
    r = _run(nc, [{f"in_{k}": v for k, v in arrays.items()}], core_ids=[0])
    return r.results[0]["out_x"].reshape(B, S, D)
```

```python
import concourse.bass as bass
import numpy as np
from concourse import mybir
from contextlib import ExitStack

F32 = mybir.dt.float32
BF16 = mybir.dt.bfloat16
ALU = mybir.AluOpType
ACT = mybir.ActivationFunctionType
AX = mybir.AxisListType

P = 128
B, S, D = 2, 1024, 128
NT = S // P
HALF = 512
NH = S // HALF
DEPTH, HEADS, DH, WIN = 6, 16, 64, 32
PAIRS = HEADS // 2
CH = 4
CB = NT // CH
KW = WIN + P
FA = 384
FI = 341
FJ = [128, 128, FI - 256]
NE, EI, TOPK = 8, 256, 128
LH, LC = 16, 8
NEG = -2.0 ** 100
STAGES = "ABCD"
LAYERS = 6


class Flow:

    def __init__(self, ctx, nc, name):
        self.sem = ctx.enter_context(nc.semaphore(name))
        self.used = 0

    def take(self, n=1):
        self.used += n
        return self.used

    def peek(self, n):
        return self.used + n

    def settle(self, eng):
        if self.used:
            eng.sem_inc(self.sem, -self.used)
        self.used = 0


def mixed_layers_kernel(nc, a, out, stages):
    ctx = ExitStack()
    with ctx:
        def sb(name, shape, dt=F32):
            return ctx.enter_context(nc.sbuf_tensor(name, shape, dt))

        def flow(name):
            return Flow(ctx, nc, name)

        X = sb("X", [P, B * NT, D])
        XT = sb("XT", [P, B, S])
        XN = sb("XN", [P, S])
        YT = sb("YT", [P, S])
        NTOK = sb("NTOK", [P, NT, D])
        XS = sb("XS", [P, S])
        ident = sb("ident", [P, P])
        identb = sb("identb", [P, P], BF16)
        bandmask = sb("bandmask", [P, 3, KW], BF16)
        minus_half = sb("minus_half", [P, 8])
        eps_tile = sb("eps_tile", [P, 4])
        bn = sb("bn", [P, NT, 6])
        mv = sb("mv", [P, NT, 2])
        ms = sb("ms", [P, NT])
        ve = sb("ve", [P, NT])
        rstd = sb("rstd", [P, NT])
        WQ = sb("WQ", [P, 2, PAIRS * 384])
        WO = sb("WO", [P, PAIRS, D])
        W1 = sb("W1", [P, 2 * FI])
        W2 = sb("W2", [P, 3, D])
        PL = sb("PL", [P, 9])
        QKS = sb("QKS", [P, 2, 256])
        COS0 = sb("COS0", [P, NT, 256])
        SIN0 = sb("SIN0", [P, NT, 256])
        COSL = sb("COSL", [P, NT, 256])
        SINL = sb("SINL", [P, NT, 256])
        QKT = sb("QKT", [P, 2, WIN + S])
        V = sb("V", [P, CH, CB, 2, DH + 1])
        VP = sb("VP", [WIN, CH, CB, 2, DH + 1])
        SQ = sb("SQ", [P, 2, 8, DH])
        N2 = sb("N2", [P, 8])
        N2G = sb("N2G", [P, 8])
        RN = sb("RN", [P, 8])
        R1 = sb("R1", [P, CB, 256])
        R2 = sb("R2", [P, CB, 256])
        RR = sb("RR", [P, CB, 256])
        QK = sb("QK", [P, 2, CB, 2, P])
        NMX = sb("NMX", [P, 4])
        PR = sb("PR", [P, 2, 4, KW])
        PTS = sb("PTS", [P, 4, P])
        PPS = sb("PPS", [WIN, 4, WIN])
        RO = sb("RO", [P, 4])
        ON = sb("ON", [P, CB, P])
        RKB = sb("RKB", [B * NE, S], BF16)
        BIG = sb("BIG", [P, PAIRS * S])
        OTS = BIG[:, :].rearrange("p (h s) -> p h s", h=PAIRS)

        PS = ctx.enter_context(nc.psum_tensor("PS", [P, 8, HALF], F32))

        x_loaded, mask_loaded, stage_a_loaded, tables_loaded, s_out = (
            ctx.enter_context(nc.semaphore(n)) for n in
            ("x_loaded", "mask_loaded", "stage_a_loaded", "tables_loaded", "out_written"))

        def bank_tiles(bank, t):
            return PS[:, bank + t // 4, (t % 4) * P:(t % 4 + 1) * P]

        made = flow("constants_made")
        W3 = BIG[:, 0:3 * D].rearrange("p (k n) -> p k n", k=3)
        WGA = BIG[:, 384:384 + FA]
        WUA = BIG[:, 768:768 + FA]
        WOA = BIG[:, 1152:1152 + FA].rearrange("p (j n) -> p j n", j=3)
        PA = BIG[:, 1536:1541]
        bandmask_f32 = BIG[:, 7168:7168 + 3 * KW].rearrange("p (m k) -> p m k", m=3)
        with nc.Block() as block:
            @block.sync
            def _(sp):
                sp.dma_start(X[:, :, :], a["x"].rearrange("(t p) d -> p t d", p=P)).then_inc(x_loaded, 16)
                sp.dma_start(bandmask_f32, a["bandmask"]).then_inc(mask_loaded, 16)
                for dst, name in ((W3, "w3"), (WGA, "wga"), (WUA, "wua"), (WOA, "woa"), (PA, "pa")):
                    sp.dma_start(dst, a[name]).then_inc(stage_a_loaded, 16)
                sp.dma_start(COS0[:, :, :], a["cos"]).then_inc(tables_loaded, 16)
                sp.dma_start(SIN0[:, :, :], a["sin"]).then_inc(tables_loaded, 16)
                sp.dma_start(WQ[:, 0, :], a["wqkv"][0, :, :]).then_inc(tables_loaded, 16)
                sp.wait_ge(x_loaded, 16)
                sp.wait_ge(mask_loaded, 16)
                sp.wait_ge(stage_a_loaded, 5 * 16)

            @block.scalar
            def _(act):
                act.wait_ge(mask_loaded, 16)
                nc.scalar.activation(bandmask[:, :, :], bandmask_f32, ACT.Copy)

            @block.gpsimd
            def _(pool):
                pool.memset(ident[:, :], 0.0).then_inc(made.sem, 1)
                pool.memset(identb[:, :], 0.0).then_inc(made.sem, 1)
                pool.memset(minus_half[:, :], -0.5)
                pool.memset(V[:, :, :, :, DH:DH + 1], 1.0)
                pool.memset(VP[:, :, :, :, DH:DH + 1], 1.0)
                pool.memset(QKT[:, 1, 0:WIN], 0.0)
                pool.wait_ge(made.sem, made.take(2))
                for m in (ident, identb):
                    pool.affine_select(out=m[:, :], in_=m[:, :], compare_op=ALU.not_equal, fill=1.0,
                                       base=0, pattern=[[-1, P]], channel_multiplier=1)
                made.settle(pool)

        to_tokens = flow("tile_transposed_to_tokens")
        stats_in = flow("bn_stats_done")
        aggr_in = flow("mean_var_done")
        var_in = flow("variance_ready")
        rstd_in = flow("rstd_ready")
        ntok_in = flow("normalised_tile_ready")
        nfeat_in = flow("normalised_half_in_psum")
        res_in = flow("normalised_tile_for_residual")

        def norm(tokens=None, features=None, rms=False, eps=1e-5, dst=None, scale=None, bias=None,
                 residual=None):
            src = tokens if tokens is not None else (lambda t: bank_tiles(0, t))
            with nc.Block() as block:
                @block.tensor
                def _(pe):
                    if features is not None:
                        for t in range(NT):
                            tr = nc.tensor.transpose(bank_tiles(0, t), features[:, t * P:(t + 1) * P],
                                                     ident[:, :])
                            if t % 4 == 3:
                                tr.then_inc(to_tokens.sem, 1)
                    if dst is not None:
                        for t in range(NT):
                            pe.wait_ge(ntok_in.sem, ntok_in.take())
                            tr = nc.tensor.transpose(bank_tiles(2, t), NTOK[:, t, :], ident[:, :])
                            if t % 4 == 3:
                                tr.then_inc(nfeat_in.sem, 1)
                    ntok_in.settle(pe)

                @block.vector
                def _(dve):
                    def statistics(tiles):
                        if features is not None:
                            dve.wait_ge(to_tokens.sem, to_tokens.take())
                        for t in tiles:
                            nc.vector.bn_stats(bn[:, t, :], src(t)).then_inc(stats_in.sem, 1)
                        for t in tiles:
                            dve.wait_ge(stats_in.sem, stats_in.take())
                            nc.vector.bn_aggr(mv[:, t, :], bn[:, t, :]).then_inc(aggr_in.sem, 1)
                        dve.wait_ge(aggr_in.sem, aggr_in.take(4))
                        cols = slice(tiles[0], tiles[0] + 4)
                        if rms:
                            nc.vector.tensor_tensor(ms[:, cols], mv[:, cols, 0], mv[:, cols, 0], ALU.mult)\
                                .then_inc(aggr_in.sem, 1)
                            dve.wait_ge(aggr_in.sem, aggr_in.take())
                            nc.vector.scalar_tensor_tensor(ve[:, cols], ms[:, cols], eps, mv[:, cols, 1],
                                                           ALU.add, ALU.add).then_inc(var_in.sem, 1)
                        else:
                            nc.vector.tensor_scalar(ve[:, cols], mv[:, cols, 1], eps, None, ALU.add)\
                                .then_inc(var_in.sem, 1)

                    def normalise(tiles):
                        dve.wait_ge(rstd_in.sem, rstd_in.take())
                        done = ntok_in if dst is not None else res_in
                        for t in tiles:
                            if rms:
                                nc.vector.tensor_scalar(NTOK[:, t, :], src(t), rstd[:, t:t + 1], None,
                                                        ALU.mult).then_inc(done.sem, 1)
                            else:
                                nc.vector.tensor_scalar(NTOK[:, t, :], src(t), mv[:, t, 0:1],
                                                        rstd[:, t:t + 1], ALU.subtract, ALU.mult)\
                                    .then_inc(done.sem, 1)

                    for h in range(NH):
                        statistics(range(4 * h, 4 * h + 4))
                    for h in range(NH):
                        normalise(range(4 * h, 4 * h + 4))
                    if residual is not None:
                        dve.wait_ge(res_in.sem, res_in.take(NT))
                        nc.vector.tensor_tensor(residual, residual, NTOK[:, :, :], ALU.add)
                    for f in (to_tokens, stats_in, aggr_in, rstd_in, res_in):
                        f.settle(dve)

                @block.gpsimd
                def _(pool):
                    for h in range(NH):
                        cols = slice(4 * h, 4 * h + 4)
                        pool.wait_ge(var_in.sem, var_in.take())
                        nc.gpsimd.tensor_tensor(rstd[:, cols], ve[:, cols], minus_half[:, 0:4], ALU.pow)\
                            .then_inc(rstd_in.sem, 1)
                    var_in.settle(pool)

                @block.scalar
                def _(act):
                    if dst is not None:
                        for h in range(NH):
                            act.wait_ge(nfeat_in.sem, nfeat_in.take())
                            nc.scalar.activation(dst[:, h * HALF:(h + 1) * HALF], PS[:, 2 + h, :],
                                                 ACT.Identity if bias is not None else ACT.Copy,
                                                 scale=1.0 if scale is None else scale,
                                                 bias=0.0 if bias is None else bias)
                    nfeat_in.settle(act)

        def x_tiles(b):
            return lambda t: X[:, bass.ds(b * NT + t, 1), :].rearrange("p o d -> p (o d)")

        def x_batch(b):
            return X[:, bass.ds(b * NT, NT), :]

        if "A" in stages:
            SIG = BIG[:, 2048:2048 + S]
            TAN = BIG[:, 3072:3072 + S]
            SCA = BIG[:, 4096:4096 + S]
            SCX = BIG[:, 5120:5120 + S]
            X1 = BIG[:, 6144:6144 + S]
            HT = BIG[:, 2048:2048 + 3 * S].rearrange("p (j n) -> p j n", j=3)
            SGA = SQ[:, :, :, :].rearrange("p k a b -> p k (a b)")
            GSA = [r[:, :, :].rearrange("p a b -> p (a b)") for r in (R1, R2)]
            gates_in = flow("gates_in_psum")
            ups_in = flow("ups_in_psum")
            ffn_in = flow("ffn_in_psum")
            gates_act = flow("gates_activated")
            scan_in = flow("scan_operands_ready")
            silu_in = flow("gate_times_sigmoid_ready")
            hidden_in = flow("hidden_ready")
            with nc.Fori(0, B) as b:
                norm(tokens=x_tiles(b), dst=XS[:, :])
                norm(features=XS, rms=True, eps=1e-6, dst=XN[:, :], scale=PA[:, 0:1])
                with nc.Block() as block:
                    @block.tensor
                    def _(pe):
                        for h in range(NH):
                            for k in range(3):
                                nc.tensor.matmul(PS[:, 3 * h + k, :], W3[:, k, :],
                                                 XN[:, h * HALF:(h + 1) * HALF],
                                                 start=True, stop=True).then_inc(gates_in.sem, 1)

                    @block.scalar
                    def _(act):
                        for h in range(NH):
                            cols = slice(h * HALF, (h + 1) * HALF)
                            for k, (f, dst) in enumerate(((ACT.Sigmoid, SIG), (ACT.Tanh, TAN),
                                                          (ACT.Sigmoid, SCA))):
                                act.wait_ge(gates_in.sem, gates_in.take())
                                nc.scalar.activation(dst[:, cols], PS[:, 3 * h + k, :], f,
                                                     bias=PA[:, 2 + k:3 + k]).then_inc(gates_act.sem, 1)
                        gates_in.settle(act)

                    @block.vector
                    def _(dve):
                        for h in range(NH):
                            cols = slice(h * HALF, (h + 1) * HALF)
                            dve.wait_ge(gates_act.sem, gates_act.take(2))
                            nc.vector.tensor_tensor(SCX[:, cols], SIG[:, cols], TAN[:, cols], ALU.mult)\
                                .then_inc(scan_in.sem, 1)
                            dve.wait_ge(gates_act.sem, gates_act.take())
                            nc.vector.tensor_scalar(SCA[:, cols], SCA[:, cols], 0.998, 0.001,
                                                    ALU.mult, ALU.add).then_inc(scan_in.sem, 1)
                        dve.wait_ge(scan_in.sem, scan_in.take(4))
                        nc.vector.tensor_tensor_scan(YT[:, :], SCA, SCX, 0.0, ALU.mult, ALU.add)\
                            .then_inc(scan_in.sem, 1)
                        dve.wait_ge(scan_in.sem, scan_in.take())
                        nc.vector.tensor_tensor(X1, YT[:, :], XS[:, :], ALU.add)
                        gates_act.settle(dve)
                        scan_in.settle(dve)
                norm(features=X1, rms=True, eps=1e-6, dst=XN[:, :], scale=PA[:, 1:2])
                with nc.Block() as block:
                    @block.tensor
                    def _(pe):
                        for h in range(NH):
                            cols = slice(h * HALF, (h + 1) * HALF)
                            for j in range(3):
                                i = 3 * h + j
                                if i >= 2:
                                    pe.wait_ge(hidden_in.sem, hidden_in.peek(i - 1))
                                nc.tensor.matmul(PS[:, 2 * (i % 2), :], WGA[:, j * P:(j + 1) * P],
                                                 XN[:, cols], start=True, stop=True)\
                                    .then_inc(gates_in.sem, 1)
                                nc.tensor.matmul(PS[:, 2 * (i % 2) + 1, :], WUA[:, j * P:(j + 1) * P],
                                                 XN[:, cols], start=True, stop=True)\
                                    .then_inc(ups_in.sem, 1)
                        for h in range(NH):
                            pe.wait_ge(hidden_in.sem, hidden_in.take(3))
                            for j in range(3):
                                mm = nc.tensor.matmul(PS[:, 4 + h, :], WOA[:, j, :],
                                                      HT[:, j, h * HALF:(h + 1) * HALF],
                                                      start=j == 0, stop=j == 2)
                            mm.then_inc(ffn_in.sem, 1)
                        hidden_in.settle(pe)

                    @block.scalar
                    def _(act):
                        for i in range(3 * NH):
                            act.wait_ge(gates_in.sem, gates_in.take())
                            nc.scalar.activation(SGA[:, i % 2, :], PS[:, 2 * (i % 2), :], ACT.Sigmoid)\
                                .then_inc(gates_act.sem, 1)
                        gates_in.settle(act)

                    @block.vector
                    def _(dve):
                        for i in range(3 * NH):
                            h, j = i // 3, i % 3
                            dve.wait_ge(gates_act.sem, gates_act.take())
                            nc.vector.tensor_tensor(GSA[i % 2], PS[:, 2 * (i % 2), :], SGA[:, i % 2, :],
                                                    ALU.mult).then_inc(silu_in.sem, 1)
                            dve.wait_ge(ups_in.sem, ups_in.take())
                            dve.wait_ge(silu_in.sem, silu_in.take())
                            nc.vector.tensor_tensor(HT[:, j, h * HALF:(h + 1) * HALF], GSA[i % 2],
                                                    PS[:, 2 * (i % 2) + 1, :], ALU.mult)\
                                .then_inc(hidden_in.sem, 1)
                        for h in range(NH):
                            dve.wait_ge(ffn_in.sem, ffn_in.take())
                            nc.vector.tensor_tensor(YT[:, h * HALF:(h + 1) * HALF], PS[:, 4 + h, :],
                                                    X1[:, h * HALF:(h + 1) * HALF], ALU.add)
                        for f in (gates_act, silu_in, ups_in, ffn_in):
                            f.settle(dve)
                norm(features=YT, residual=x_batch(b))

        if "B" in stages:
            XTf = XT[:, :, :].rearrange("p b s -> p (b s)")
            WQf = WQ[:, :, :].rearrange("p k n -> p (k n)")
            BIGf = BIG[:, :]
            Vb = V[:, :, :, :, :].rearrange("p c j h d -> p (c j) (h d)")
            VPb = VP[:, :, :, :, :].rearrange("p c j h d -> p (c j) (h d)")
            COSLb = COSL[:, :, :]
            SQv = SQ[:, :, :, :].rearrange("p k (j g) d -> p k j (g d)", j=CB)
            R2s = R2[:, :, :].rearrange("p j (g v d) -> p j g v d", v=2, d=DH // 2)
            SINs = SINL[:, :, :].rearrange("p t (g v d) -> p t g v d", v=2, d=DH // 2)
            RRg = RR[:, :, :].rearrange("p j (g d) -> p (j g) d", d=DH)
            QKg = [QK[:, k, :, :, :].rearrange("p j k (h d) -> p (j k h) d", d=DH) for k in range(2)]
            PQ, TQ, SC, PT, PO, OT = PS[:, 0:2, :], PS[:, 2, :], PS[:, 3:5, :], PS[:, 5, :], PS[:, 6, :], PS[:, 7, :]
            POu = PS[:, 6, 0:4 * (DH + 1)].rearrange("p (u d) -> p u d", d=DH + 1)
            wq_in = flow("next_wqkv_in")
            layer_in = flow("layer_weights_in")
            proj_in = flow("qkv_in_psum")
            rot_in = flow("rotation_products_ready")
            sq_in = flow("squares_ready")
            pq_free = flow("qkv_banks_read")
            n2_in = flow("square_norms_ready")
            n2g_in = flow("square_norms_guarded")
            rr_in = flow("rotated_and_rnorm_ready")
            qk_in = flow("rotated_scaled_ready")
            qkt_ps = flow("qk_transposed_in_psum")
            qkt_in = flow("qk_feature_major_ready")
            sc_in = flow("head_scores_in_psum")
            nmx_in = flow("head_max_ready")
            p_in = flow("probabilities_ready")
            p_tail = flow("probabilities_complete")
            pt_ps = flow("probabilities_transposed_in_psum")
            pts_in = flow("probabilities_transposed")
            pps_in = flow("previous_window_transposed")
            o_ps = flow("attention_out_in_psum")
            ro_in = flow("softmax_sums_inverted")
            on_in = flow("attention_out_normalised")
            ot_ps = flow("attention_out_transposed")
            x_in = flow("attention_residual_added")
            x_in_dve = flow("attention_residual_written")
            shift_in = flow("shifted_half_ready")
            xn_in = flow("normalised_half_ready")
            ot_free = flow("transposed_out_copied")
            wo_in = flow("projected_half_in_psum")
            table_in = flow("first_scales_ready")
            qks_in = flow("qk_scales_in")
            SMALL_LOADS = 4 * 16
            gelu_free = flow("gate_tile_used")

            for b in range(B):
                norm(tokens=x_tiles(b), dst=XT[:, b, :])
            with nc.Block() as block:
                @block.vector
                def _(dve):
                    for shifted in (XS, YT):
                        nc.vector.memset(shifted[D // 2:P, 0:1], 0.0)

            def shift_tokens(b):
                with nc.Block() as block:
                    @block.vector
                    def _(dve):
                        nc.vector.tensor_copy(XS[0:D // 2, :], XTf[0:D // 2, bass.ds(b * S, S)])

                    @block.scalar
                    def _(act):
                        nc.scalar.activation(XS[D // 2:P, 1:S], XTf[D // 2:P, bass.ds(b * S, S - 1)],
                                             ACT.Copy)

            N = PAIRS * CH

            def run(eng, step, flows):
                def settle():
                    for f in flows:
                        f.settle(eng)
                for n in range(-3, 2):
                    step(n, 0)
                settle()
                with eng.Fori(0, PAIRS - 2) as i:
                    for n in range(2, 2 + CH):
                        step(n, i)
                    settle()
                for n in range(N + 2 - 2 * CH, N + 2):
                    step(n, 0)
                return settle

            def attention(l, b):
                def pq(n):
                    return SC if n == 1 else PQ

                par = (l % 2) * (PAIRS * 384)
                upcoming = (l * B + b + 1) // B % LAYERS

                with nc.Block() as block:
                    @block.sync
                    def _(sp):
                        load_scales(sp, upcoming)

                    @block.tensor
                    def _(pe):
                        def step(n, i):
                            if 0 <= n - 1 < N:
                                pe.wait_ge(p_in.sem, p_in.take(4))
                                for u in range(4):
                                    tr = nc.tensor.transpose(PT[:, u * P:(u + 1) * P],
                                                             PR[:, (n - 1) % 2, u, WIN:KW], ident[:, :])
                                    if u == 0:
                                        tr.then_inc(p_tail.sem, 1)
                                tr.then_inc(pt_ps.sem, 1)
                            if 0 <= n < N:
                                c = n % CH
                                pe.wait_ge(qkt_in.sem, qkt_in.take())
                                if n == 0:
                                    pe.wait_ge(pq_free.sem, pq_free.take())
                                for h in range(2):
                                    rows = slice(DH * h, DH * h + DH)
                                    first = 0 if c == 0 else 1
                                    nc.tensor.matmul(
                                        SC[:, h, 0:CB * KW], identb[:, :],
                                        bandmask[:, first:first + CB, :].rearrange("p j k -> p (j k)"),
                                        start=True, stop=False)
                                    for j in range(CB):
                                        t0 = (CB * c + j) * P
                                        mm = nc.tensor.matmul(SC[:, h, j * KW:(j + 1) * KW],
                                                              QKT[rows, 0, WIN + t0:WIN + t0 + P],
                                                              QKT[rows, 1, t0:t0 + KW],
                                                              start=False, stop=j == CB - 1)
                                    mm.then_inc(sc_in.sem, 1)
                            if 0 <= n - 2 < N:
                                pe.wait_ge(on_in.sem, on_in.take())
                                if n - 1 < N:
                                    pe.wait_ge(pts_in.sem, pts_in.take())
                                else:
                                    pe.wait_ge(ot_free.sem, ot_free.take())
                                for j in range(CB):
                                    tr = nc.tensor.transpose(OT[:, j * P:(j + 1) * P], ON[:, j, :],
                                                             ident[:, :])
                                tr.then_inc(ot_ps.sem, 1)
                            if 0 <= n - 1 < N:
                                c = (n - 1) % CH
                                if n - 2 < 0:
                                    pe.wait_ge(pts_in.sem, pts_in.take())
                                for j in range(CB):
                                    for h in range(2):
                                        u, o = 2 * h + j, 2 * j + h
                                        mm = nc.tensor.matmul(POu[:, o, :], PTS[:, u, :], V[:, c, j, h, :],
                                                              start=o == 0, stop=o == 3,
                                                              skip_group_check=True)
                                pe.wait_ge(pps_in.sem, pps_in.take())
                                for j in range(CB):
                                    for h in range(2):
                                        u, o = 2 * h + j, 2 * j + h
                                        if c > 0 or j > 0:
                                            mm = nc.tensor.matmul(POu[0:WIN, o, :], PPS[:, u, :],
                                                                  VP[:, c, j, h, :], start=False,
                                                                  stop=True, skip_group_check=True)
                                mm.then_inc(o_ps.sem, 1)
                            if 0 <= n + 1 < N:
                                pe.wait_ge(qk_in.sem, qk_in.take())
                                for k in range(2):
                                    for j in range(CB):
                                        tr = nc.tensor.transpose(TQ[:, (2 * k + j) * P:(2 * k + j + 1) * P],
                                                                 QK[:, (n + 1) % 2, j, k, :], ident[:, :])
                                tr.then_inc(qkt_ps.sem, 1)
                            if 0 <= n + 3 < N:
                                c = (n + 3) % CH
                                if n + 3 > 1:
                                    pe.wait_ge(pq_free.sem, pq_free.take())
                                w0 = par + ((n + 3) // CH + i) * 384
                                for j in range(CB):
                                    t0 = (CB * c + j) * P
                                    mm = nc.tensor.matmul(pq(n + 3)[:, j, 0:384], XS[:, t0:t0 + P],
                                                          WQf[:, bass.ds(w0, 384)], start=True, stop=True)
                                mm.then_inc(proj_in.sem, 1)
                        settle = run(pe, step, [ot_free, qkt_in, p_in, on_in, pq_free, pts_in, pps_in, qk_in])
                        pe.wait_ge(pq_free.sem, pq_free.take())
                        settle()

                    @block.scalar
                    def _(act):

                        def last_windows(c):
                            lo = 0 if c else 1
                            nc.scalar.activation(VPb[:, CB * c + lo:CB * c + CB, :],
                                                 Vb[P - WIN:P, CB * c + lo - 1:CB * c + CB - 1, :],
                                                 ACT.Copy)

                        def step(n, i):
                            if 0 <= n - 1 < N:
                                act.wait_ge(pt_ps.sem, pt_ps.take())
                                nc.scalar.activation(PTS[:, :, :].rearrange("p u k -> p (u k)"), PT,
                                                     ACT.Copy).then_inc(pts_in.sem, 1)
                            if 1 < n + 1 < N:
                                last_windows((n + 1) % CH)
                            if 0 <= n < N:
                                for h in range(2):
                                    act.wait_ge(nmx_in.sem, nmx_in.take())
                                    for j in range(CB):
                                        u = 2 * h + j
                                        nc.scalar.activation(PR[:, n % 2, u, :],
                                                             SC[:, h, j * KW:(j + 1) * KW], ACT.Exp,
                                                             bias=NMX[:, u:u + 1]).then_inc(p_in.sem, 1)
                            if 0 <= n + 1 < N:
                                c = (n + 1) % CH
                                act.wait_ge(qkt_ps.sem, qkt_ps.take())
                                nc.scalar.activation(
                                    QKT[:, :, WIN + c * CB * P:WIN + (c + 1) * CB * P],
                                    TQ.rearrange("p (k s) -> p k s", k=2), ACT.Copy).then_inc(qkt_in.sem, 1)
                                if n + 1 <= 1:
                                    last_windows(c)
                            if 0 <= n + 3 < N:
                                c = (n + 3) % CH
                                act.wait_ge(proj_in.sem, proj_in.take())
                                nc.scalar.activation(SQv[:, (n + 3) % 2, :, :], pq(n + 3)[:, :, 0:256],
                                                     ACT.Square)
                                nc.scalar.activation(V[:, c, :, :, 0:DH], pq(n + 3)[:, :, 256:384]
                                                     .rearrange("p j (h d) -> p j h d", h=2), ACT.Copy)\
                                    .then_inc(sq_in.sem, 1)
                            if 0 <= n - 2 < N:
                                c = (n - 2) % CH
                                act.wait_ge(ot_ps.sem, ot_ps.take())
                                cp = nc.scalar.activation(
                                    BIGf[:, bass.ds(((n - 2) // CH + i) * S + c * CB * P, CB * P)],
                                    OT[:, 0:CB * P], ACT.Copy)
                                if n == N:
                                    cp.then_inc(ot_free.sem, 1)
                        run(act, step, [nmx_in, ot_ps, pt_ps, proj_in, qkt_ps])()

                    @block.vector
                    def _(dve):
                        def step(n, i):
                            if 0 <= n - 1 < N:
                                dve.wait_ge(p_tail.sem, p_tail.take())
                                nc.vector.transpose(PPS[:, :, :], PR[0:WIN, (n - 1) % 2, :, 0:WIN])\
                                    .then_inc(pps_in.sem, 1)
                            if 0 <= n + 1 < N:
                                dve.wait_ge(rr_in.sem, rr_in.take())
                                nc.vector.tensor_tensor(QKg[(n + 1) % 2], RRg, RN[:, :].unsqueeze(2)
                                                        .to_broadcast([P, 8, DH]), ALU.mult)\
                                    .then_inc(qk_in.sem, 1)
                            if 0 <= n + 2 < N:
                                c = (n + 2) % CH
                                t = slice(CB * c, CB * c + CB)
                                qk5 = pq(n + 2)[:, :, 0:256].rearrange("p j (g v d) -> p j g v d", v=2, d=DH // 2)
                                dve.wait_ge(sq_in.sem, sq_in.take())
                                nc.vector.tensor_reduce(N2[:, :], SQ[:, n % 2, :, :], AX.X, ALU.add)\
                                    .then_inc(n2_in.sem, 1)
                                nc.vector.tensor_tensor(R1[:, :, :], pq(n + 2)[:, :, 0:256], COSLb[:, t, :],
                                                        ALU.mult)
                                for v in range(2):
                                    rot = nc.vector.tensor_tensor(R2s[:, :, :, v, :], qk5[:, :, :, 1 - v, :],
                                                                  SINs[:, t, :, v, :], ALU.mult)
                                rot.then_inc(rot_in.sem, 1)
                            if 0 <= n < N:
                                for h in range(2):
                                    dve.wait_ge(sc_in.sem, sc_in.take())
                                    nc.vector.tensor_reduce(
                                        NMX[:, 2 * h:2 * h + 2],
                                        SC[:, h, 0:CB * KW].rearrange("p (j k) -> p j k", k=KW),
                                        AX.X, ALU.max, negate=True).then_inc(nmx_in.sem, 1)
                            if 0 <= n - 1 < N:
                                dve.wait_ge(o_ps.sem, o_ps.take())
                                nc.vector.reciprocal(RO[:, :], POu[:, :, DH]).then_inc(ro_in.sem, 1)
                                dve.wait_ge(ro_in.sem, ro_in.take())
                                nc.vector.tensor_tensor(
                                    ON[:, :, :].rearrange("p j (h d) -> p (j h) d", h=2), POu[:, :, 0:DH],
                                    RO[:, :].unsqueeze(2).to_broadcast([P, 4, DH]), ALU.mult)\
                                    .then_inc(on_in.sem, 1)
                        run(dve, step, [sc_in, p_tail, rr_in, sq_in, o_ps, ro_in])()

                    @block.gpsimd
                    def _(pool):
                        def step(n, i):
                            if 0 <= n + 2 < N:
                                pool.wait_ge(n2_in.sem, n2_in.take())
                                nc.gpsimd.tensor_scalar(N2G[:, :], N2[:, :], 1e-24, None, ALU.max)\
                                    .then_inc(n2g_in.sem, 1)
                                pool.wait_ge(n2g_in.sem, n2g_in.take())
                                nc.gpsimd.tensor_tensor(RN[:, :], N2G[:, :], minus_half[:, :], ALU.pow)
                                pool.wait_ge(rot_in.sem, rot_in.take())
                                pool.sem_inc(pq_free.sem, 1)
                                nc.gpsimd.tensor_tensor(RR[:, :, :], R1[:, :, :], R2[:, :, :], ALU.add)\
                                    .then_inc(rr_in.sem, 1)
                        run(pool, step, [n2_in, n2g_in, rot_in])()

            GL = [BIG[:, k * HALF:(k + 1) * HALF] for k in range(2)]
            HB = BIG[:, 2 * HALF:2 * HALF + 3 * S].rearrange("p (j s) -> p j s", j=3)
            GU = [PS[:, 6:8, :], PS[:, 0:2, :]]

            def feed_forward(b):
                with nc.Block() as block:
                    def tokens_of(h):
                        return [(t, PS[:, 2 + h, (t % 4) * P:(t % 4 + 1) * P])
                                for t in range(4 * h, 4 * h + 4)]

                    @block.tensor
                    def _(pe):
                        def project(h, heads):
                            for hp in heads:
                                mm = nc.tensor.matmul(PS[:, h, :], WO[:, hp, :],
                                                      OTS[:, hp, h * HALF:(h + 1) * HALF],
                                                      start=hp == 0, stop=hp == PAIRS - 1)
                            if hp == PAIRS - 1:
                                mm.then_inc(wo_in.sem, 1)

                        def to_token_major(h):
                            pe.wait_ge(shift_in.sem, shift_in.take(2))
                            for t, tile in tokens_of(h):
                                tr = nc.tensor.transpose(tile, YT[:, t * P:(t + 1) * P], ident[:, :])
                            tr.then_inc(to_tokens.sem, 1)

                        def to_feature_major(h):
                            for t in range(4):
                                pe.wait_ge(ntok_in.sem, ntok_in.take())
                                tr = nc.tensor.transpose(PS[:, 4 + h, t * P:(t + 1) * P],
                                                         NTOK[:, 4 * h + t, :], ident[:, :])
                            tr.then_inc(nfeat_in.sem, 1)

                        def gate_and_up(i):
                            h, j = i // 3, i % 3
                            cols, w = slice(h * HALF, (h + 1) * HALF), FJ[j]
                            if j == 0:
                                pe.wait_ge(xn_in.sem, xn_in.take())
                            if i >= 2:
                                used = i - 1 if i < 4 else i - 4
                                pe.wait_ge(gelu_free.sem, gelu_free.peek(used))
                            nc.tensor.matmul(GU[i % 2][0:w, 0, :], W1[:, FI + j * P:FI + j * P + w],
                                             XN[:, cols], start=True, stop=True).then_inc(proj_in.sem, 1)
                            nc.tensor.matmul(GU[i % 2][0:w, 1, :], W1[:, j * P:j * P + w],
                                             XN[:, cols], start=True, stop=True).then_inc(sc_in.sem, 1)

                        def down(h):
                            pe.wait_ge(gelu_free.sem, gelu_free.take(3))
                            for j, w in enumerate(FJ):
                                mm = nc.tensor.matmul(PS[:, 2 + h, :], W2[0:w, j, :],
                                                      HB[0:w, j, h * HALF:(h + 1) * HALF],
                                                      start=j == 0, stop=j == 2)
                            mm.then_inc(wo_in.sem, 1)

                        pe.wait_ge(layer_in.sem, SMALL_LOADS)
                        project(0, range(PAIRS))
                        project(1, range(3))
                        to_token_major(0)
                        project(1, range(3, PAIRS))
                        to_feature_major(0)
                        gate_and_up(0)
                        to_token_major(1)
                        gate_and_up(1)
                        gate_and_up(2)
                        to_feature_major(1)
                        gate_and_up(3)
                        down(0)
                        gate_and_up(4)
                        gate_and_up(5)
                        down(1)
                        for f in (shift_in, ntok_in, xn_in, gelu_free):
                            f.settle(pe)

                    @block.scalar
                    def _(act):
                        def shift(h):
                            act.wait_ge(x_in.sem, x_in.take())
                            first = 1 if h == 0 else 0
                            nc.scalar.activation(
                                YT[D // 2:P, h * HALF + first:(h + 1) * HALF],
                                XTf[D // 2:P, bass.ds(b * S + h * HALF - 1 + first, HALF - first)],
                                ACT.Copy).then_inc(shift_in.sem, 1)

                        def affine(h):
                            act.wait_ge(nfeat_in.sem, nfeat_in.take())
                            nc.scalar.activation(XN[:, h * HALF:(h + 1) * HALF], PS[:, 4 + h, :],
                                                 ACT.Identity, scale=PL[:, 0:1], bias=PL[:, 1:2])\
                                .then_inc(xn_in.sem, 1)

                        def gelu(i):
                            w, j = FJ[i % 3], i % 3
                            act.wait_ge(proj_in.sem, proj_in.take())
                            nc.scalar.activation(GL[i % 2][0:w, :], GU[i % 2][0:w, 0, :], ACT.Gelu,
                                                 bias=PL[0:w, 5 + j:6 + j]).then_inc(nmx_in.sem, 1)

                        nc.scalar.activation(XS[D // 2:P, 1:S], XTf[D // 2:P, bass.ds((b + 1) % B * S, S - 1)],
                                             ACT.Copy)
                        act.wait_ge(layer_in.sem, SMALL_LOADS)
                        shift(0)
                        affine(0)
                        shift(1)
                        for i in range(3):
                            gelu(i)
                        affine(1)
                        for i in range(3, 6):
                            gelu(i)
                        for f in (x_in, nfeat_in, proj_in):
                            f.settle(act)

                    @block.vector
                    def _(dve):
                        def residual(h):
                            dve.wait_ge(wo_in.sem, wo_in.take())
                            cols = bass.ds(b * S + h * HALF, HALF)
                            nc.vector.tensor_tensor(XTf[:, cols], XTf[:, cols], PS[:, h, :], ALU.add)\
                                .then_inc(x_in_dve.sem, 1)
                            dve.wait_ge(x_in_dve.sem, x_in_dve.take())
                            dve.sem_inc(x_in.sem, 1)
                            nc.vector.tensor_copy(YT[0:D // 2, h * HALF:(h + 1) * HALF],
                                                  XTf[0:D // 2, cols]).then_inc(shift_in.sem, 1)

                        def statistics(h):
                            dve.wait_ge(to_tokens.sem, to_tokens.take())
                            for t, tile in tokens_of(h):
                                nc.vector.bn_stats(bn[:, t, :], tile).then_inc(stats_in.sem, 1)
                            for t, tile in tokens_of(h):
                                dve.wait_ge(stats_in.sem, stats_in.take())
                                nc.vector.bn_aggr(mv[:, t, :], bn[:, t, :]).then_inc(aggr_in.sem, 1)
                            dve.wait_ge(aggr_in.sem, aggr_in.take(4))
                            nc.vector.tensor_scalar(ve[:, 4 * h:4 * h + 4], mv[:, 4 * h:4 * h + 4, 1],
                                                    1e-5, None, ALU.add).then_inc(var_in.sem, 1)

                        def normalise(h):
                            dve.wait_ge(rstd_in.sem, rstd_in.take())
                            for t, tile in tokens_of(h):
                                nc.vector.tensor_scalar(NTOK[:, t, :], tile, mv[:, t, 0:1],
                                                        rstd[:, t:t + 1], ALU.subtract, ALU.mult)\
                                    .then_inc(ntok_in.sem, 1)

                        def gated(i):
                            h, j, w = i // 3, i % 3, FJ[i % 3]
                            dve.wait_ge(nmx_in.sem, nmx_in.take())
                            dve.wait_ge(sc_in.sem, sc_in.take())
                            nc.vector.scalar_tensor_tensor(
                                HB[0:w, j, h * HALF:(h + 1) * HALF], GU[i % 2][0:w, 1, :],
                                PL[0:w, 2 + j:3 + j], GL[i % 2][0:w, :], ALU.add, ALU.mult)\
                                .then_inc(gelu_free.sem, 1)

                        def add_out(h):
                            dve.wait_ge(wo_in.sem, wo_in.take())
                            cols = bass.ds(b * S + h * HALF, HALF)
                            nc.vector.scalar_tensor_tensor(XTf[:, cols], PS[:, 2 + h, :], PL[:, 8:9],
                                                           XTf[:, cols], ALU.add, ALU.add)

                        nc.vector.tensor_copy(XS[0:D // 2, :], XTf[0:D // 2, bass.ds((b + 1) % B * S, S)])
                        dve.wait_ge(layer_in.sem, SMALL_LOADS)
                        residual(0)
                        statistics(0)
                        normalise(0)
                        residual(1)
                        gated(0)
                        statistics(1)
                        gated(1)
                        normalise(1)
                        for i in range(2, 4):
                            gated(i)
                        add_out(0)
                        gated(4)
                        gated(5)
                        add_out(1)
                        for f in (wo_in, x_in_dve, to_tokens, stats_in, aggr_in, rstd_in, nmx_in, sc_in):
                            f.settle(dve)

                    @block.gpsimd
                    def _(pool):
                        for h in range(NH):
                            pool.wait_ge(var_in.sem, var_in.take())
                            nc.gpsimd.tensor_tensor(rstd[:, 4 * h:4 * h + 4], ve[:, 4 * h:4 * h + 4],
                                                    minus_half[:, 0:4], ALU.pow).then_inc(rstd_in.sem, 1)
                        make_tables(nc.gpsimd)
                        var_in.settle(pool)

            def make_tables(vec):
                for k, (dst, src) in enumerate(((COSL, COS0), (SINL, SIN0))):
                    vec.tensor_tensor(dst[:, :, :], src[:, :, :],
                                      QKS[:, k, :].unsqueeze(1).to_broadcast([P, NT, 256]), ALU.mult)

            def load_scales(sp, l):
                src = a["qks"][bass.ds(l, 1), :, :].partition_broadcast(P)
                sp.dma_start(QKS[:, :, :], src.rearrange("p o k n -> p (o k) n")).then_inc(qks_in.sem, 16)
                sp.wait_ge(qks_in.sem, qks_in.take(16))
                qks_in.settle(sp)

            shift_tokens(0)
            with nc.Block() as block:
                @block.sync
                def _(sp):
                    load_scales(sp, 0)
                    sp.wait_ge(tables_loaded, 3 * 16)
                    sp.sem_inc(table_in.sem, 1)
                    sp.sem_inc(wq_in.sem, 16)
                    sp.sem_inc(layer_in.sem, SMALL_LOADS)

                @block.vector
                def _(dve):
                    dve.wait_ge(table_in.sem, table_in.take())
                    make_tables(nc.vector)
                    table_in.settle(dve)
            with nc.Fori(0, LAYERS) as l:
                with nc.Block() as block:
                    @block.sync
                    def _(sp):
                        sp.wait_ge(wq_in.sem, wq_in.take(16))
                        wq_in.settle(sp)
                        sp.wait_ge(layer_in.sem, layer_in.take(SMALL_LOADS))
                        layer_in.settle(sp)
                        for dst, name in ((PL[:, :], "pl"), (WO[:, :, :], "wo"), (W1[:, :], "w1"),
                                          (W2[:, :, :], "w2")):
                            src = a[name]
                            if len(src.shape) == 4:
                                src = src[bass.ds(l, 1), :, :, :].rearrange("o p j n -> (o p) j n")
                            else:
                                src = src[bass.ds(l, 1), :, :].rearrange("o p n -> (o p) n")
                            sp.dma_start(dst, src).then_inc(layer_in.sem, 16)
                        sp.dma_start(WQf[:, bass.ds(((l + 1) % 2) * (PAIRS * 384), PAIRS * 384)],
                                     a["wqkv"][bass.ds((l + 1) % LAYERS, 1), :, :]
                                     .rearrange("o p n -> (o p) n")).then_inc(wq_in.sem, 16)
                with nc.Fori(0, B) as b:
                    attention(l, b)
                    feed_forward(b)
            with nc.Block() as block:
                @block.sync
                def _(sp):
                    sp.wait_ge(wq_in.sem, wq_in.take(16))
                    wq_in.settle(sp)
                    sp.wait_ge(layer_in.sem, layer_in.take(SMALL_LOADS))
                    layer_in.settle(sp)
            with nc.Fori(0, B) as b:
                with nc.Block() as block:
                    @block.scalar
                    def _(act):
                        nc.scalar.activation(YT[:, :], XTf[:, bass.ds(b * S, S)], ACT.Copy)
                norm(features=YT, residual=x_batch(b))
        if "C" in stages:
            WC = BIG[:, 0:384]
            WOC = BIG[:, 384:512]
            HM = BIG[:, 512:516]
            BDM = BIG[:, 640:768]
            CAU = BIG[:, 768:896]
            BD = [BIG[:, 896:1024], BIG[:, 7296:7424]]
            BDT = BIG[:, 1024:1152]
            KE = COSL[:, 0:4, :].rearrange("p a b -> p (a b)")
            ZR = COSL[:, 4:8, :].rearrange("p a b -> p (a b)")
            KET = SINL[:, 0:4, :].rearrange("p a (c n) -> p (a c) n", n=P)
            QP = SINL[:, 4:8, :].rearrange("p a b -> p (a b)")
            QV = BIG[:, 1152:1152 + NT * 256].rearrange("p (t n) -> p t n", n=256)
            QM = BIG[:, 3200:3200 + 4 * S].rearrange("p (t g j s) -> p t g j s", g=4, j=4, s=P)
            AM = [r[:, :, :].rearrange("p a b -> p (a b)").rearrange("p (g n) -> p g n", g=4)
                  for r in (COS0, XT)]
            OCT = SIN0[:, 0:4, :].rearrange("p a b -> p (a b)")
            ONES = SIN0[:, 4:8, :].rearrange("p a b -> p (a b)")
            CMASK = SQ[:, 0, :, :].rearrange("p g d -> p (g d)").rearrange("p (j n) -> p j n", n=P)
            VM = [r[:, :, :].rearrange("p a b -> p (a b)").rearrange("p (j n) -> p j n", n=P)
                  for r in (R1, R2)]
            qm = RR[:, 0, 0:P]
            qsum = RR[:, 0, P:2 * P]
            qr = RR[:, 1, 0:P]
            kmx = NMX[:, 0:1]
            layer_c = flow("stage_c_weights_in")
            SQ8 = QV[:, :, 0:P].rearrange("p t (h c) -> p t h c", c=LC)
            qv_ps = flow("qv_tile_in_psum")
            qv_in = flow("qv_tile_copied")
            qv_free = flow("qv_bank_copied")
            k_ps = flow("k_in_psum")
            kmx_in = flow("k_max_ready")
            ke_in = flow("k_exp_ready")
            ke_pe = flow("k_exp_ready_for_transposes")
            z_in = flow("k_cumulated")
            qs_in = flow("q_softmax_step")
            qe_in = flow("q_shifted")
            qx_in = flow("q_exp_ready")
            qn_in = flow("q_normalised")
            qt_ps = flow("q_transposed")
            kt_ps = flow("k_transposed")
            qm_act = flow("q_of_heads_0_to_11_ready")
            qm_dve = flow("q_of_heads_12_to_15_ready")
            qm_used = flow("q_by_head_used")
            a_ps = flow("scores_in_psum")
            a_in = flow("scores_masked")
            st_ps = flow("state_update_in_psum")
            bdt_in = flow("state_update_masked")
            bd_in = flow("state_ready")
            oc_ps = flow("linear_out_in_psum")
            vm_in = flow("values_masked")
            vm_used = flow("masked_values_used")
            oct_in = flow("linear_out_feature_major")
            yc_ps = flow("projection_in_psum")
            with nc.Block() as block:
                @block.sync
                def _(sp):
                    for dst, n in ((WC, "wc"), (WOC, "woc"), (HM, "headmask"), (BDM, "blockdiag"),
                                   (CAU, "causal"), (CMASK, "colmask")):
                        sp.dma_start(dst, a[n]).then_inc(layer_c.sem, 16)
                    sp.wait_ge(layer_c.sem, layer_c.take(96))
                    layer_c.settle(sp)

                @block.vector
                def _(dve):
                    nc.vector.memset(ONES, 1.0)
                    nc.vector.memset(QM, 0.0)
            with nc.Fori(0, B) as b:
                norm(tokens=x_tiles(b), dst=XN[:, :])
                with nc.Block() as block:
                    @block.tensor
                    def _(pe):
                        for h in range(NH):
                            mm = nc.tensor.matmul(PS[:, h, :], WC[:, 256:384], XN[:, h * HALF:(h + 1) * HALF],
                                                  start=True, stop=True)
                        mm.then_inc(k_ps.sem, 1)
                        for t in range(NT):
                            if t >= 2:
                                pe.wait_ge(qv_free.sem, qv_free.peek(t - 1))
                            nc.tensor.matmul(PS[:, 2 + t % 2, 0:256], XN[:, t * P:(t + 1) * P], WC[:, 0:256],
                                             start=True, stop=True).then_inc(qv_ps.sem, 1)
                        pe.wait_ge(qv_free.sem, qv_free.take(NT))
                        pe.wait_ge(ke_pe.sem, ke_pe.take())
                        for t in range(NT):
                            tr = nc.tensor.transpose(bank_tiles(4, t), KE[:, t * P:(t + 1) * P], ident[:, :])
                        tr.then_inc(kt_ps.sem, 1)
                        pe.wait_ge(qn_in.sem, qn_in.take())
                        for t in range(NT):
                            tr = nc.tensor.transpose(bank_tiles(6, t), QV[:, t, 0:P], ident[:, :])
                        tr.then_inc(qt_ps.sem, 1)
                        for f in (qv_free, ke_pe, qn_in):
                            f.settle(pe)

                    @block.scalar
                    def _(act):
                        for t in range(NT):
                            act.wait_ge(qv_ps.sem, qv_ps.take())
                            nc.scalar.activation(QV[:, t, :], PS[:, 2 + t % 2, 0:256], ACT.Copy)\
                                .then_inc(qv_free.sem, 1)
                        act.drain().then_inc(qv_in.sem, 1)
                        act.wait_ge(kmx_in.sem, kmx_in.take())
                        nc.scalar.activation(KE.rearrange("p (h s) -> p h s", h=NH), PS[:, 0:2, :], ACT.Exp,
                                             bias=kmx).then_inc(ke_in.sem, 1)
                        act.drain().then_inc(ke_pe.sem, 1)
                        act.wait_ge(qe_in.sem, qe_in.take())
                        nc.scalar.activation(SQ8, SQ8, ACT.Exp).then_inc(qx_in.sem, 1)
                        act.wait_ge(kt_ps.sem, kt_ps.take())
                        nc.scalar.activation(KET.rearrange("p (h t) n -> p h (t n)", h=2), PS[:, 4:6, :],
                                             ACT.Copy)
                        for f in (qv_ps, kmx_in, qe_in, kt_ps):
                            f.settle(act)

                    @block.vector
                    def _(dve):
                        dve.wait_ge(k_ps.sem, k_ps.take())
                        nc.vector.tensor_reduce(kmx, PS[:, 0:2, :], AX.XY, ALU.max, negate=True)\
                            .then_inc(kmx_in.sem, 1)
                        dve.wait_ge(qv_in.sem, qv_in.take())
                        qh = qm.rearrange("p (t h) -> p t h", h=LH)
                        nc.vector.tensor_reduce(qh, SQ8, AX.X, ALU.max).then_inc(qs_in.sem, 1)
                        dve.wait_ge(qs_in.sem, qs_in.take())
                        for half in range(2):
                            t = slice(4 * half, 4 * half + 4)
                            sub = nc.vector.tensor_tensor(
                                SQ8[:, t, :, :],
                                SQ8[:, t, :, :],
                                qh[:, t, :].unsqueeze(3).to_broadcast([P, 4, LH, LC]), ALU.subtract)
                        sub.then_inc(qe_in.sem, 1)
                        dve.wait_ge(ke_in.sem, ke_in.take())
                        nc.vector.tensor_tensor_scan(ZR, ONES, KE, 0.0, ALU.mult, ALU.add).then_inc(z_in.sem, 1)
                        dve.wait_ge(qx_in.sem, qx_in.take())
                        nc.vector.tensor_reduce(qsum.rearrange("p (t h) -> p t h", h=LH), SQ8, AX.X, ALU.add)\
                            .then_inc(qs_in.sem, 1)
                        dve.wait_ge(qs_in.sem, qs_in.take())
                        nc.vector.reciprocal(qr, qsum).then_inc(qs_in.sem, 1)
                        dve.wait_ge(qs_in.sem, qs_in.take())
                        qrh = qr.rearrange("p (t h) -> p t h", h=LH)
                        for half in range(2):
                            t = slice(4 * half, 4 * half + 4)
                            mul = nc.vector.tensor_tensor(SQ8[:, t, :, :], SQ8[:, t, :, :],
                                                          qrh[:, t, :].unsqueeze(3)
                                                          .to_broadcast([P, 4, LH, LC]), ALU.mult)
                        mul.then_inc(qn_in.sem, 1)
                        dve.wait_ge(z_in.sem, z_in.take())
                        nc.vector.tensor_scalar(XS[:, :], ZR, 1e-9, None, ALU.add).then_inc(z_in.sem, 1)
                        dve.wait_ge(z_in.sem, z_in.take())
                        nc.vector.reciprocal(ZR, XS[:, :]).then_inc(z_in.sem, 1)
                        dve.wait_ge(qt_ps.sem, qt_ps.take())
                        dve.wait_ge(z_in.sem, z_in.take())
                        nc.vector.scalar_tensor_tensor(QP.rearrange("p (h s) -> p h s", h=NH), PS[:, 6:8, :],
                                                       float(LC) ** -0.5, ZR.rearrange("p (h s) -> p h s", h=NH),
                                                       ALU.mult, ALU.mult)
                        nc.vector.memset(BD[0], 0.0)
                        for f in (k_ps, qv_in, qs_in, ke_in, z_in, qx_in, qt_ps):
                            f.settle(dve)
                with nc.Block() as block:
                    @block.tensor
                    def _(pe):
                        for t in range(NT + 1):
                            if t < NT:
                                pe.wait_ge(qm_act.sem, qm_act.take())
                                pe.wait_ge(qm_dve.sem, qm_dve.take())
                            for pair in range(2):
                                if 0 <= t - 1 < NT:
                                    pe.wait_ge(a_in.sem, a_in.take())
                                if t < NT:
                                    for g in (2 * pair, 2 * pair + 1):
                                        mm = nc.tensor.matmul(
                                            PS[:, g, :].rearrange("p (j s) -> p j s", j=4),
                                            KE[:, t * P:(t + 1) * P], QM[:, t % 2, g, :, :],
                                            start=True, stop=True)
                                    mm.then_inc(a_ps.sem, 1)
                            if 0 <= t - 1 < NT:
                                if t > 1:
                                    pe.wait_ge(oct_in.sem, oct_in.take())
                                nc.tensor.matmul(PS[:, 5, 0:P], BD[(t - 1) % 2], QP[:, (t - 1) * P:t * P],
                                                 start=True, stop=False)
                                pe.wait_ge(vm_in.sem, vm_in.take())
                                for j in range(4):
                                    for g in range(4):
                                        rows = slice(32 * g, 32 * g + 32)
                                        mm = nc.tensor.matmul(PS[rows, 5, 0:P], VM[(t - 1) % 2][:, j, rows],
                                                              AM[(t - 1) % 2][:, g, j * P:(j + 1) * P],
                                                              start=False, stop=j == 3,
                                                              tile_position=(0, 32 * g))
                                mm.then_inc(oc_ps.sem, 1)
                            if t < NT - 1:
                                if t:
                                    pe.wait_ge(bd_in.sem, bd_in.take())
                                nc.tensor.matmul(PS[:, 4, 0:P], KET[:, t, :], QV[:, t, P:2 * P],
                                                 start=True, stop=True).then_inc(st_ps.sem, 1)
                            elif t == NT - 1:
                                pe.wait_ge(bd_in.sem, bd_in.take())
                        pe.wait_ge(oct_in.sem, oct_in.take())
                        for h in range(NH):
                            nc.tensor.matmul(PS[:, h, :], WOC, OCT[:, h * HALF:(h + 1) * HALF],
                                             start=True, stop=True).then_inc(yc_ps.sem, 1)
                        for f in (qm_act, qm_dve, a_in, bd_in, oct_in, vm_in):
                            f.settle(pe)

                    @block.vector
                    def _(dve):
                        def last_q_by_head(t):
                            rows = slice(96, 128)
                            nc.vector.tensor_tensor(
                                QM[rows, t % 2, 3, :, :],
                                QP[rows, t * P:(t + 1) * P].unsqueeze(1).to_broadcast([32, 4, P]),
                                HM[rows, :].unsqueeze(2).to_broadcast([32, 4, P]), ALU.mult)\
                                .then_inc(qm_dve.sem, 1)
                        last_q_by_head(0)
                        last_q_by_head(1)
                        for t in range(NT):
                            for pair in range(2):
                                g = slice(2 * pair, 2 * pair + 2)
                                dve.wait_ge(a_ps.sem, a_ps.take())
                                if pair == 1 and t + 2 < NT:
                                    dve.sem_inc(qm_used.sem, 1)
                                nc.vector.tensor_tensor(
                                    AM[t % 2][:, g, :].rearrange("p g (j s) -> p (g j) s", s=P),
                                    PS[:, g, :].rearrange("p g (j s) -> p (g j) s", s=P),
                                    CAU.unsqueeze(1).to_broadcast([P, 8, P]), ALU.mult)\
                                    .then_inc(a_in.sem, 1)
                            if t + 2 < NT:
                                last_q_by_head(t + 2)
                            if t < NT - 1:
                                dve.wait_ge(st_ps.sem, st_ps.take())
                                nc.vector.tensor_tensor(BDT, PS[:, 4, 0:P], BDM, ALU.mult)\
                                    .then_inc(bdt_in.sem, 1)
                                dve.wait_ge(bdt_in.sem, bdt_in.take())
                                nc.vector.tensor_tensor(BD[(t + 1) % 2], BD[t % 2], BDT, ALU.add)\
                                    .then_inc(bd_in.sem, 1)
                        for f in (a_ps, st_ps, bdt_in):
                            f.settle(dve)

                    @block.scalar
                    def _(act):
                        def q_by_head(t):
                            for g in range(3):
                                rows = slice(32 * g, 32 * g + 32)
                                for j in range(4):
                                    q = nc.scalar.activation(QM[rows, t % 2, g, j, :],
                                                             QP[rows, t * P:(t + 1) * P], ACT.Copy,
                                                             scale=HM[rows, j:j + 1])
                            q.then_inc(qm_act.sem, 1)
                        q_by_head(0)
                        q_by_head(1)
                        for t in range(NT + 1):
                            if t + 2 < NT:
                                act.wait_ge(qm_used.sem, qm_used.take())
                                q_by_head(t + 2)
                            if t > 0:
                                act.wait_ge(oc_ps.sem, oc_ps.take())
                                if t + 1 < NT:
                                    act.sem_inc(vm_used.sem, 1)
                                nc.scalar.activation(OCT[:, (t - 1) * P:t * P], PS[:, 5, 0:P], ACT.Copy)\
                                    .then_inc(oct_in.sem, 1)
                        for h in range(NH):
                            act.wait_ge(yc_ps.sem, yc_ps.take())
                            nc.scalar.activation(YT[:, h * HALF:(h + 1) * HALF], PS[:, h, :], ACT.Copy)
                        for f in (qm_used, oc_ps, yc_ps):
                            f.settle(act)

                    @block.gpsimd
                    def _(pool):
                        for t in range(NT):
                            if t > 1:
                                pool.wait_ge(vm_used.sem, vm_used.take())
                            nc.gpsimd.tensor_tensor(VM[t % 2],
                                                    QV[:, t:t + 1, P:2 * P].to_broadcast([P, 4, P]), CMASK,
                                                    ALU.mult).then_inc(vm_in.sem, 1)
                        vm_used.settle(pool)
                norm(features=YT, residual=x_batch(b))
        if "D" in stages:
            WGU = BIG[:, 0:NE * 2 * EI]
            WD = BIG[:, 4096:4096 + NE * 2 * D]
            GW = BIG[:, 6144:6144 + NE]
            AF = BIG[:, 6160:6160 + NT * B * NE].rearrange("p (t n) -> p t n", n=B * NE)
            GT = BIG[:, 6300:6300 + NT * B * NE].rearrange("p (t n) -> p t n", n=B * NE)
            LG = BIG[:, 6432:6432 + NT * NE].rearrange("p (t e) -> p t e", e=NE)
            LE = BIG[:, 6496:6496 + NT * NE].rearrange("p (t e) -> p t e", e=NE)
            AT = COS0[0:B * NE, 0:4, :].rearrange("p a b -> p (a b)")
            WK = [COS0[0:B * NE, 4:8, :].rearrange("p a b -> p (a b)"),
                  SIN0[0:B * NE, 0:4, :].rearrange("p a b -> p (a b)")]
            RK = COS0[0:B * NE, 4:8, :].rearrange("p a b -> p (a b)")
            SEL = SIN0[0:B * NE, 4:8, :].rearrange("p a b -> p (a b)")
            ONESD = XS[0:B * NE, :]
            XTOK = XT[:, :, :].rearrange("p b s -> p (b s)").rearrange("p (t n) -> p t n", n=D)
            TOK = QKT[:, :, :].rearrange("p k s -> p (k s)")[:, 0:NT * (D + NE)]\
                .rearrange("p (t n) -> p t n", n=D + NE)
            ONEHOT = COSL[:, 0:4, :].rearrange("p a (c n) -> p (a c) n", n=P)
            ONEHOT_T = COSL[:, 4:8, :].rearrange("p a b -> p (a b)")
            PLACES = SINL[:, 0, 0:TOPK]
            PLACE = SINL[:, 1, 0:1]
            CHOSEN = [SINL[:, 2 + k, 0:D + NE] for k in range(2)]
            CHOSEN_T = SINL[:, 4, 0:TOPK]
            SGD, GSD, HD, HTD = SQ[:, 0, 0:4, :].rearrange("p a b -> p (a b)"), R1[:, 0, :], \
                R2[:, 0, :], RR[:, 0, :]
            OE = R1[:, 1, 0:D]
            top8 = [mv[0:B * NE, 4 * k:4 * k + 4, :].rearrange("p a b -> p (a b)") for k in range(2)]
            layer_d = flow("stage_d_weights_in")
            experts_d = flow("expert_weights_in")
            lg_ps = flow("logits_in_psum")
            lg_in = flow("logit_step")
            le_in = flow("logits_shifted")
            lx_in = flow("logits_exp_ready")
            at_ps = flow("affinities_transposed")
            top_in = flow("top8_step")
            rk_in = flow("places_ready")
            rkt_ps = flow("places_token_major")
            hot_in = flow("one_hot_ready")
            hot_used = flow("one_hot_used")
            place_ps = flow("places_broadcast")
            hott_in = flow("one_hot_transposed_ready")
            hott_used = flow("expert_output_scattered")
            ch_ps = flow("chosen_tokens_in_psum")
            ch_in = flow("chosen_tokens_ready")
            cht_ps = flow("chosen_tokens_transposed")
            cht_in = flow("chosen_tokens_feature_major")
            oe_in = flow("expert_output_ready")
            up_ps = flow("gate_up_in_psum")
            sg_in = flow("sigmoid_ready")
            gs_in = flow("silu_ready")
            hd_in = flow("hidden_tile_ready")
            ht_ps = flow("hidden_transposed")
            ht_in = flow("hidden_feature_major")
            dn_ps = flow("down_in_psum")
            with nc.Block() as block:
                @block.sync
                def _(sp):
                    sp.dma_start(GW, a["gw"]).then_inc(layer_d.sem, 16)
                    sp.dma_start(PLACES, a["places"]).then_inc(layer_d.sem, 16)
                    sp.dma_start(PLACE, a["places"][0:1, :].rearrange("o p -> p o")).then_inc(layer_d.sem, 16)
                    sp.dma_start(WGU.rearrange("p (e n) -> p e n", e=NE), a["wgu"])\
                        .then_inc(experts_d.sem, 16)
                    sp.dma_start(WD.rearrange("p (e k n) -> p e k n", e=NE, k=2), a["wd"])\
                        .then_inc(experts_d.sem, 16)
                    sp.wait_ge(layer_d.sem, layer_d.take(48))
                    layer_d.settle(sp)
            with nc.Fori(0, B) as b:
                norm(tokens=x_tiles(b), dst=XN[:, :])
                with nc.Block() as block:
                    @block.tensor
                    def _(pe):
                        for t in range(NT):
                            mm = nc.tensor.matmul(PS[:, 0, NE * t:NE * t + NE], XN[:, t * P:(t + 1) * P], GW,
                                                  start=True, stop=True)
                        mm.then_inc(lg_ps.sem, 1)

                    @block.scalar
                    def _(act):
                        nc.scalar.activation(XTOK[:, bass.ds(b * NT, NT), :], NTOK[:, :, :], ACT.Copy)
                        act.wait_ge(le_in.sem, le_in.take())
                        nc.scalar.activation(LE, LG, ACT.Exp).then_inc(lx_in.sem, 1)
                        le_in.settle(act)

                    @block.vector
                    def _(dve):
                        pl = PS[:, 0, 0:NT * NE].rearrange("p (t e) -> p t e", e=NE)

                        def per_token(col):
                            return col.unsqueeze(2).to_broadcast([P, NT, NE])
                        dve.wait_ge(lg_ps.sem, lg_ps.take())
                        nc.vector.tensor_reduce(ms[:, :], pl, AX.X, ALU.max).then_inc(lg_in.sem, 1)
                        dve.wait_ge(lg_in.sem, lg_in.take())
                        nc.vector.tensor_tensor(LG, pl, per_token(ms[:, :]), ALU.subtract)\
                            .then_inc(le_in.sem, 1)
                        dve.wait_ge(lx_in.sem, lx_in.take())
                        nc.vector.tensor_reduce(ve[:, :], LE, AX.X, ALU.add).then_inc(lg_in.sem, 1)
                        dve.wait_ge(lg_in.sem, lg_in.take())
                        nc.vector.reciprocal(rstd[:, :], ve[:, :]).then_inc(lg_in.sem, 1)
                        dve.wait_ge(lg_in.sem, lg_in.take())
                        nc.vector.tensor_tensor(AF[:, :, bass.ds(b * NE, NE)], LE, per_token(rstd[:, :]),
                                                ALU.mult)
                        for f in (lg_ps, lg_in, lx_in):
                            f.settle(dve)
            with nc.Block() as block:
                @block.sync
                def _(sp):
                    sp.wait_ge(experts_d.sem, experts_d.take(32))
                    experts_d.settle(sp)

                @block.tensor
                def _(pe):
                    for t in range(NT):
                        tr = nc.tensor.transpose(PS[0:B * NE, t // 4, (t % 4) * P:(t % 4 + 1) * P],
                                                 AF[:, t, :], ident[:, :])
                    tr.then_inc(at_ps.sem, 1)
                    pe.wait_ge(rk_in.sem, rk_in.take())
                    for t in range(NT):
                        tr = nc.tensor.transpose(PS[:, 2, B * NE * t:B * NE * (t + 1)],
                                                 RK[:, t * P:(t + 1) * P], ident[0:B * NE, 0:B * NE])
                    tr.then_inc(rkt_ps.sem, 1)
                    rk_in.settle(pe)

                @block.vector
                def _(dve):
                    dve.wait_ge(at_ps.sem, at_ps.take())
                    nc.vector.tensor_copy(AT.rearrange("p (h s) -> p h s", h=2), PS[0:B * NE, 0:2, :])\
                        .then_inc(top_in.sem, 1)
                    nc.vector.memset(ONESD, 1.0).then_inc(top_in.sem, 1)
                    dve.wait_ge(top_in.sem, top_in.take(2))
                    src = AT
                    for r in range(TOPK // 8):
                        nc.vector.max(top8[r % 2], src).then_inc(top_in.sem, 1)
                        dve.wait_ge(top_in.sem, top_in.take())
                        nc.vector.match_replace(WK[r % 2], top8[r % 2], src, -1.0)\
                            .then_inc(top_in.sem, 1)
                        dve.wait_ge(top_in.sem, top_in.take())
                        src = WK[r % 2]
                    nc.vector.tensor_scalar(SEL, src, 0.0, None, ALU.is_lt).then_inc(top_in.sem, 1)
                    dve.wait_ge(top_in.sem, top_in.take())
                    nc.vector.tensor_tensor_scan(AT, ONESD, SEL, 0.0, ALU.mult, ALU.add)\
                        .then_inc(top_in.sem, 1)
                    dve.wait_ge(top_in.sem, top_in.take())
                    nc.vector.tensor_tensor(RK, AT, SEL, ALU.mult).then_inc(rk_in.sem, 1)
                    nc.vector.tensor_tensor(RKB[:, :], AT, SEL, ALU.mult)
                    dve.wait_ge(rkt_ps.sem, rkt_ps.take())
                    nc.vector.tensor_copy(GT.rearrange("p t n -> p (t n)"), PS[:, 2, 0:NT * B * NE])
                    for f in (at_ps, top_in, rkt_ps):
                        f.settle(dve)
            with nc.Fori(0, B) as b:
                def run(eng, step, flows):
                    def settle():
                        for f in flows:
                            f.settle(eng)
                    for n in range(-2, 0):
                        step(n, 0)
                    settle()
                    with eng.Fori(0, NE // 2 - 1) as i:
                        for n in range(2):
                            step(n, i)
                        settle()
                    for n in range(NE - 2, NE):
                        step(n, 0)
                    settle()

                def expert(n, i):
                    return n + 2 * i

                with nc.Block() as block:
                    @block.scalar
                    def _(act):
                        nc.scalar.activation(TOK[:, :, 0:D], XTOK[:, bass.ds(b * NT, NT), :], ACT.Copy)

                    @block.vector
                    def _(dve):
                        nc.vector.tensor_copy(TOK[:, :, D:D + NE], AF[:, :, bass.ds(b * NE, NE)])
                        nc.vector.memset(YT[:, 0:HALF], 0.0)
                with nc.Block() as block:
                    @block.tensor
                    def _(pe):
                        def step(n, i):
                            now, coming = 0 <= n, 0 <= n + 1 < NE
                            if coming:
                                pe.wait_ge(hot_in.sem, hot_in.take())
                                for t in range(NT):
                                    mm = nc.tensor.matmul(
                                        PS[:, 2, 0:D + NE], ONEHOT[:, t, :], TOK[:, t, :],
                                        start=t == 0, stop=t == NT - 1)
                                mm.then_inc(ch_ps.sem, 1)
                            if now:
                                pe.wait_ge(hd_in.sem, hd_in.take())
                                for k in range(2):
                                    tr = nc.tensor.transpose(PS[:, 5, k * P:(k + 1) * P],
                                                             HD[:, k * P:(k + 1) * P], ident[:, :])
                                tr.then_inc(ht_ps.sem, 1)
                            if now:
                                pe.wait_ge(hott_in.sem, hott_in.take())
                            if coming:
                                which = identb[0:B * NE, bass.ds(b * NE + expert(n + 1, i), 1)]
                                for h in range(NH):
                                    mm = nc.tensor.matmul(PS[:, h, :], which.to_broadcast([B * NE, P]),
                                                          RKB[:, h * HALF:(h + 1) * HALF],
                                                          start=True, stop=True)
                                mm.then_inc(place_ps.sem, 1)
                            if coming:
                                pe.wait_ge(ch_in.sem, ch_in.take())
                                nc.tensor.transpose(PS[:, 3, 0:P], CHOSEN[(n + 1) % 2][:, 0:D], ident[:, :])\
                                    .then_inc(cht_ps.sem, 1)
                            if now:
                                pe.wait_ge(ht_in.sem, ht_in.take())
                                for k in range(2):
                                    mm = nc.tensor.matmul(PS[:, 5, 0:D], HTD[:, k * P:(k + 1) * P],
                                                          WD[:, bass.ds((expert(n, i) * 2 + k) * D, D)],
                                                          start=k == 0, stop=k == 1)
                                mm.then_inc(dn_ps.sem, 1)
                            if coming:
                                pe.wait_ge(cht_in.sem, cht_in.take())
                                nc.tensor.matmul(PS[:, 4, :], CHOSEN_T,
                                                 WGU[:, bass.ds(expert(n + 1, i) * 2 * EI, 2 * EI)],
                                                 start=True, stop=True).then_inc(up_ps.sem, 1)
                            if now:
                                pe.wait_ge(oe_in.sem, oe_in.take())
                                for t in range(NT):
                                    mm = nc.tensor.matmul(bank_tiles(6, t), ONEHOT_T[:, t * P:(t + 1) * P],
                                                          OE, start=False, stop=False,
                                                          skip_group_check=True)
                                mm.then_inc(hott_used.sem, 1)

                        for h in range(NH):
                            nc.tensor.matmul(PS[:, 6 + h, :], ident[:, :], YT[:, 0:HALF], start=True,
                                             stop=False)
                        run(pe, step, [hot_in, hd_in, ch_in, ht_in, cht_in, hott_in, oe_in])
                        for h in range(NH):
                            nc.tensor.matmul(PS[:, 6 + h, :], ident[:, :], YT[:, 0:HALF], start=False,
                                             stop=True)

                    @block.scalar
                    def _(act):
                        def step(n, i):
                            now, coming = 0 <= n, 0 <= n + 1 < NE
                            if now:
                                act.wait_ge(up_ps.sem, up_ps.take())
                                nc.scalar.activation(SGD, PS[:, 4, 0:EI], ACT.Sigmoid).then_inc(sg_in.sem, 1)
                            if coming:
                                act.wait_ge(ch_ps.sem, ch_ps.take())
                                act.sem_inc(hot_used.sem, 1)
                                nc.scalar.activation(CHOSEN[(n + 1) % 2], PS[:, 2, 0:D + NE], ACT.Copy)\
                                    .then_inc(ch_in.sem, 1)
                            if now:
                                act.wait_ge(ht_ps.sem, ht_ps.take())
                                nc.scalar.activation(HTD, PS[:, 5, 0:EI], ACT.Copy).then_inc(ht_in.sem, 1)
                            if coming:
                                act.wait_ge(cht_ps.sem, cht_ps.take())
                                nc.scalar.activation(CHOSEN_T, PS[:, 3, 0:P], ACT.Copy)\
                                    .then_inc(cht_in.sem, 1)
                            if now:
                                act.wait_ge(dn_ps.sem, dn_ps.take())
                                nc.scalar.activation(OE, PS[:, 5, 0:D], ACT.Copy).then_inc(oe_in.sem, 1)
                        run(act, step, [up_ps, ch_ps, ht_ps, cht_ps, dn_ps])

                    @block.vector
                    def _(dve):
                        def step(n, i):
                            if 0 <= n:
                                dve.wait_ge(sg_in.sem, sg_in.take())
                                nc.vector.tensor_tensor(GSD, PS[:, 4, 0:EI], SGD, ALU.mult)\
                                    .then_inc(gs_in.sem, 1)
                                dve.wait_ge(gs_in.sem, gs_in.take())
                                nc.vector.scalar_tensor_tensor(HD, PS[:, 4, EI:2 * EI],
                                                               CHOSEN[n % 2][:, bass.ds(D + expert(n, i), 1)],
                                                               GSD,
                                                               ALU.mult, ALU.mult).then_inc(hd_in.sem, 1)
                                dve.wait_ge(hott_used.sem, hott_used.take())
                                dve.wait_ge(place_ps.sem, place_ps.take())
                                nc.vector.tensor_scalar(ONEHOT_T.rearrange("p (h s) -> p h s", h=NH),
                                                        PS[:, 0:2, :], PLACE, None, ALU.is_equal)\
                                    .then_inc(hott_in.sem, 1)
                            if 0 <= n + 2 < NE:
                                if n + 2 > 0:
                                    dve.wait_ge(hot_used.sem, hot_used.take())
                                col = GT[:, :, bass.ds(b * NE + expert(n + 2, i), 1)]
                                nc.vector.tensor_tensor(ONEHOT,
                                                        PLACES.unsqueeze(1).to_broadcast([P, NT, TOPK]),
                                                        col.to_broadcast([P, NT, TOPK]), ALU.is_equal)\
                                    .then_inc(hot_in.sem, 1)
                        dve.sem_inc(hott_used.sem, 1)
                        run(dve, step, [sg_in, gs_in, hott_used, place_ps, hot_used])
                        dve.wait_ge(hott_used.sem, hott_used.take())
                        dve.wait_ge(hot_used.sem, hot_used.take())
                        for f in (hott_used, hot_used):
                            f.settle(dve)
                norm(tokens=lambda t: bank_tiles(6, t), residual=x_batch(b))
        with nc.Block() as block:
            @block.sync
            def _(sp):
                sp.dma_start(out.rearrange("(t p) d -> p t d", p=P), X[:, :, :]).then_inc(s_out, 16)
                sp.wait_ge(s_out, 16)


def _rotary_tables():
    f = np.float32
    half = np.arange(0, DH, 2, dtype=f)
    inv_freq = (f(1.0) / f(10000.0) ** (half / f(DH))).astype(f)
    t = np.arange(S, dtype=f)
    freqs = t[:, None] * inv_freq[None, :]
    base = ((half + f(0.4 * DH)) / f(1.4 * DH)).astype(f)
    power = ((t - S // 2) / (WIN // 2)).astype(f)
    scale = (base[None, :].astype(np.float64) ** power[:, None]).astype(f)
    cos, sin = np.cos(freqs.astype(np.float64)), np.sin(freqs.astype(np.float64))
    tables = []
    for fn, sign in ((cos, 1.0), (sin, -1.0)):
        q = np.concatenate([sign * fn * scale * 8.0, fn * scale * 8.0], 1)
        k = np.concatenate([sign * fn / scale, fn / scale], 1)
        full = np.concatenate([q, q, k, k], 1).astype(f)
        tables.append(np.ascontiguousarray(full.reshape(NT, P, 256).transpose(1, 0, 2)))
    return tables


def _band_mask():
    i = np.arange(P)[:, None]
    j = np.arange(KW)[None, :] - WIN
    rest = (j <= i) & (j >= i - WIN)
    masks = [rest & (j >= 0), rest, rest]
    return np.stack([np.where(m, 0.0, NEG) for m in masks], 1).astype(np.float32)


def kernel(**inputs):
    import concourse.bacc as _bacc
    from concourse.bass_utils import run_bass_kernel_spmd as _run

    g = {k: np.asarray(v) for k, v in inputs.items()}
    cos, sin = _rotary_tables()

    def cols(*vs):
        return np.stack(vs, 1)

    def features(w, n):
        return np.ascontiguousarray(w.reshape(n, P, -1).transpose(1, 0, 2))

    wqkv = g["L0_ffn_Wqkv"].reshape(DEPTH, D, 3, PAIRS, P).transpose(0, 1, 3, 2, 4).reshape(DEPTH, D, -1)
    qs, ks = g["L0_ffn_q_scale"], g["L0_ffn_k_scale"]
    qks = np.concatenate([qs, qs, ks, ks], 1)
    swapped = qks.reshape(DEPTH, 4, 2, DH // 2)[:, :, ::-1].reshape(DEPTH, 256)
    b1 = np.zeros((DEPTH, P, 6), np.float32)
    w2 = np.zeros((DEPTH, P, 3, D), np.float32)
    for j, w in enumerate(FJ):
        b1[:, :w, j] = g["L0_ffn_b1"][:, j * P:j * P + w]
        b1[:, :w, 3 + j] = g["L0_ffn_b1"][:, FI + j * P:FI + j * P + w]
        w2[:, :w, j] = g["L0_ffn_W2"][:, j * P:j * P + w]
    pl = np.concatenate([g["L0_ffn_ln_g"][:, :, None], g["L0_ffn_ln_b"][:, :, None], b1,
                         g["L0_ffn_b2"][:, :, None]], 2)
    c_idx = np.arange(P)
    arrays = {
        "x": g["L0_attn_x"].reshape(B * S, D), "cos": cos, "sin": sin, "bandmask": _band_mask(),
        "w3": np.stack([g["L0_attn_Wg"], g["L0_attn_Wv"], g["L0_attn_Wd"]], 1),
        "wga": g["L0_attn_W_gate"], "wua": g["L0_attn_W_up"], "woa": features(g["L0_attn_W_out"], 3),
        "pa": cols(g["L0_attn_w_rms_mix"], g["L0_attn_w_rms_ffn"], g["L0_attn_bg"], g["L0_attn_bv"],
                   g["L0_attn_bd"]),
        "wqkv": wqkv, "wo": g["L0_ffn_Wo"].reshape(DEPTH, PAIRS, P, D).transpose(0, 2, 1, 3),
        "w1": g["L0_ffn_W1"], "w2": w2, "pl": pl,
        "qks": np.stack([qks, swapped], 1),
        "wc": np.concatenate([g["L1_attn_W_qkv"].T[:, 0:P], g["L1_attn_W_qkv"].T[:, 2 * P:],
                              g["L1_attn_W_qkv"].T[:, P:2 * P]], 1),
        "woc": g["L1_attn_W_out"].T,
        "headmask": (c_idx[:, None] // LC % 4 == np.arange(4)[None, :]).astype(np.float32),
        "blockdiag": (c_idx[:, None] // LC == c_idx[None, :] // LC).astype(np.float32),
        "colmask": np.tile(c_idx[None, :] // LC % 4 == np.arange(4)[:, None], (P, 1, 1)).astype(np.float32),
        "causal": (c_idx[None, :] >= c_idx[:, None]).astype(np.float32),
        "places": np.tile(c_idx + 1, (P, 1)).astype(np.float32),
        "gw": g["L1_ffn_gate_w"],
        "wgu": np.concatenate([g["L1_ffn_Wg"], g["L1_ffn_Wu"]], 2).transpose(1, 0, 2),
        "wd": g["L1_ffn_Wd"].reshape(NE, 2, P, D).transpose(2, 0, 1, 3),
    }
    arrays = {k: np.ascontiguousarray(v) for k, v in arrays.items()}
    nc = _bacc.Bacc("TRN2", target_bir_lowering=False, num_devices=1)
    aps = {k: nc.dram_tensor(f"in_{k}", v.shape, mybir.dt.from_np(v.dtype), kind="ExternalInput").ap()
           for k, v in arrays.items()}
    o = nc.dram_tensor("out_x", (B * S, D), F32, kind="ExternalOutput").ap()
    mixed_layers_kernel(nc, aps, o, STAGES)
    r = _run(nc, [{f"in_{k}": v for k, v in arrays.items()}], core_ids=[0])
    return r.results[0]["out_x"].reshape(B, S, D)
```
